# Optimizing a Trainium2 kernel written in Bass

```python
import numpy as np
import jax
import jax.numpy as jnp

def _softmax(x, axis=-1):
    return jax.nn.softmax(x, axis=axis)

def _gelu(x):
    return jax.nn.gelu(x, approximate=True)

def _silu(x):
    return jax.nn.silu(x)

def _sigmoid(x):
    return jax.nn.sigmoid(x)

def _layernorm(x, axis=-1, eps=1e-05):
    m = jnp.mean(x, axis=axis, keepdims=True)
    v = jnp.var(x, axis=axis, keepdims=True)
    return (x - m) / jnp.sqrt(v + eps)

def _scatter_add(tgt, idx, src, axis=0):
    return tgt.at[idx].add(src)

def _segment_sum(src, seg, n):
    return jax.ops.segment_sum(src, seg, n)
kernel_name = 'mk_decoder_postln_d2_seqx_r8_bed314'

def setup_inputs(seed: int=0):
    np.random.seed(seed)
    _w = jnp.asarray

    def _rec_inputs():
        import jax
        import jax.numpy as jnp
        _rk = jax.random.key(seed)
        x = 7.22e-05 + 1 * jax.random.normal(jax.random.fold_in(_rk, 1), (128, 64, 128), jnp.float32)
        _lenS = 64 - jax.random.randint(jax.random.fold_in(_rk, 7), (128,), 0, max(1, 64 // 4) + 1, jnp.int32)
        _lenS2 = 64 - jax.random.randint(jax.random.fold_in(_rk, 8), (128,), 0, max(1, 64 // 4) + 1, jnp.int32)
        _ctx_1024P = jax.random.normal(jax.random.fold_in(_rk, 11), (128, 16, 128), jnp.float32)
        _ctx_1024c = jax.random.dirichlet(jax.random.fold_in(_rk, 511), 0.3 * jnp.ones((16,), jnp.float32), (128, 64))
        _ctx_1024t = jnp.einsum('bsk,bkd->bsd', _ctx_1024c, _ctx_1024P)
        _ctx_1024t = _ctx_1024t * jax.lax.rsqrt(jnp.mean(jnp.square(_ctx_1024t)) + 1e-12) * 0.953939
        ctx_1024 = 4.13588e-05 + 0.999923 * (_ctx_1024t + 0.3 * jax.random.normal(jax.random.fold_in(_rk, 611), (128, 64, 128), jnp.float32))
        return (x, ctx_1024)
    x, ctx_1024 = _rec_inputs()

    def _L0_attn_setup():
        import jax, jax.numpy as jnp
        import numpy as np
        B, S, D, H, NB = (2, 256, 128, 16, 32)
        DH = D // H
        MLP = 512
        CLUSTER_SCORE = 0.1
        LN_EPS = 1e-06

        def _layernorm(x, g, b):
            mu = jnp.mean(x, axis=-1, keepdims=True)
            var = jnp.mean(jnp.square(x - mu), axis=-1, keepdims=True)
            return (x - mu) * jax.lax.rsqrt(var + LN_EPS) * g + b

        def _lha_attention(x, Wq, Wk, Wv, Whq, Whk, Wo):
            q = jnp.einsum('bsd,dhf->bshf', x, Wq)
            k = jnp.einsum('bsd,dhf->bshf', x, Wk)
            v = jnp.einsum('bsd,dhf->bshf', x, Wv)
            qb = jax.nn.softmax(jnp.einsum('bshf,hfn->bshn', q, Whq), axis=-1)
            kb = jax.nn.softmax(jnp.einsum('bshf,hfn->bshn', k, Whk), axis=-1)
            logits = jnp.einsum('bqhf,bkhf->bhqk', q, k) / jnp.sqrt(jnp.float32(DH))
            aff = jnp.einsum('bqhn,bkhn->bhqk', qb, kb)
            logits = logits + CLUSTER_SCORE * aff
            attn = jax.nn.softmax(logits, axis=-1)
            out = jnp.einsum('bhqk,bkhf->bqhf', attn, v)
            out = jnp.einsum('bqhf,hfd->bqd', out, Wo)
            mq = jnp.mean(qb, axis=(0, 1))
            mk = jnp.mean(kb, axis=(0, 1))
            extra_loss = 0.5 * NB * (jnp.mean(jnp.sum(mq * mq, -1)) + jnp.mean(jnp.sum(mk * mk, -1)))
            return (out, extra_loss)

        def _reference_tuple_inner(inputs, ln1_g, ln1_b, Wq, Wk, Wv, Whq, Whk, Wo, ln2_g, ln2_b, W1, b1, W2, b2):
            x = _layernorm(inputs, ln1_g, ln1_b)
            attn_out, extra_loss = _lha_attention(x, Wq, Wk, Wv, Whq, Whk, Wo)
            x = attn_out + inputs
            y = _layernorm(x, ln2_g, ln2_b)
            y = jax.nn.relu(jnp.einsum('bsd,dm->bsm', y, W1) + b1)
            y = jnp.einsum('bsm,md->bsd', y, W2) + b2
            return (x + y, extra_loss)
        key = jax.random.key(seed)
        ks = jax.random.split(key, 10)
        std = 0.02
        return {'inputs': jax.random.normal(ks[0], (B, S, D), jnp.float32), 'ln1_g': jnp.ones((D,), jnp.float32), 'ln1_b': jnp.zeros((D,), jnp.float32), 'Wq': jax.random.normal(ks[1], (D, H, DH), jnp.float32) * std, 'Wk': jax.random.normal(ks[2], (D, H, DH), jnp.float32) * std, 'Wv': jax.random.normal(ks[3], (D, H, DH), jnp.float32) * std, 'Whq': jax.random.normal(ks[4], (H, DH, NB), jnp.float32) * std, 'Whk': jax.random.normal(ks[5], (H, DH, NB), jnp.float32) * std, 'Wo': jax.random.normal(ks[6], (H, DH, D), jnp.float32) * std, 'ln2_g': jnp.ones((D,), jnp.float32), 'ln2_b': jnp.zeros((D,), jnp.float32), 'W1': jax.random.normal(ks[7], (D, MLP), jnp.float32) * std, 'b1': jnp.zeros((MLP,), jnp.float32), 'W2': jax.random.normal(ks[8], (MLP, D), jnp.float32) * std, 'b2': jnp.zeros((D,), jnp.float32)}
    _L0_attn_all = _L0_attn_setup()
    _L0_attn_in = {k: v for k, v in _L0_attn_all.items() if k in ('ln1_g', 'ln1_b', 'Wq', 'Wk', 'Wv', 'Whq', 'Whk', 'Wo', 'ln2_g', 'ln2_b', 'W1', 'b1', 'W2', 'b2')}
    del _L0_attn_all

    def _L0_xattn_setup():
        import jax, jax.numpy as jnp
        import numpy as np
        H = 16
        D = 128
        DK = D // H
        key = jax.random.key(seed)
        ks = jax.random.split(key, 12)
        B, S = (4, 256)
        inp = {'query': jax.random.normal(ks[0], (B, S, D), jnp.float32), 'key': jax.random.normal(ks[1], (B, S, D), jnp.float32), 'value': jax.random.normal(ks[2], (B, S, D), jnp.float32)}
        scale = 1.0 / np.sqrt(D)
        names = ['Wq', 'Wk', 'Wv', 'Wo']
        for i, n in enumerate(names):
            inp[n] = jax.random.normal(ks[3 + i], (D, D), jnp.float32) * scale
            inp['b' + n[1]] = jnp.zeros((D,), jnp.float32)
        return inp
    _L0_xattn_all = _L0_xattn_setup()
    _L0_xattn_in = {k: v for k, v in _L0_xattn_all.items() if k in ('Wq', 'bq', 'Wk', 'bk', 'Wv', 'bv', 'Wo', 'bo')}
    del _L0_xattn_all

    def _L0_ffn_setup():
        import jax, jax.numpy as jnp
        import numpy as np
        B, S, D, F, E = (4, 256, 128, 512, 8)
        LN_EPS = 1e-05
        key = jax.random.key(seed)
        ks = jax.random.split(key, 6)
        sc = 0.02
        return {'x': jax.random.normal(ks[0], (B, S, D), dtype=jnp.float32), 'Wr': jax.random.normal(ks[1], (D, E), dtype=jnp.float32) * sc, 'br': jnp.zeros((E,), jnp.float32), 'ln_g': jnp.ones((D,), jnp.float32), 'ln_b': jnp.zeros((D,), jnp.float32), 'W1': jax.random.normal(ks[2], (E, D, F), dtype=jnp.float32) * sc, 'b1': jnp.zeros((E, F), jnp.float32), 'W2': jax.random.normal(ks[3], (E, F, D), dtype=jnp.float32) * sc, 'b2': jnp.zeros((E, D), jnp.float32)}
    _L0_ffn_all = _L0_ffn_setup()
    _L0_ffn_in = {k: v for k, v in _L0_ffn_all.items() if k in ('Wr', 'br', 'ln_g', 'ln_b', 'W1', 'b1', 'W2', 'b2')}
    del _L0_ffn_all

    def _L1_attn_setup():
        import jax, jax.numpy as jnp
        import numpy as np
        N_HEADS = 16
        MAX_LEN = 128
        key = jax.random.key(seed)
        ks = jax.random.split(key, 6)
        B, T, C = (4, 128, 128)
        scale = 0.02
        return {'x': jax.random.normal(ks[0], (B, T, C), dtype=jnp.float32), 'qkv_w': jax.random.normal(ks[1], (3 * C, C), dtype=jnp.float32) * scale, 'qkv_b': jax.random.normal(ks[2], (3 * C,), dtype=jnp.float32) * scale, 'proj_w': jax.random.normal(ks[3], (C, C), dtype=jnp.float32) * scale, 'proj_b': jax.random.normal(ks[4], (C,), dtype=jnp.float32) * scale, 'rel_pos_emb': jax.random.normal(ks[5], (2 * MAX_LEN - 1, C), dtype=jnp.float32) * scale}
    _L1_attn_all = _L1_attn_setup()
    _L1_attn_in = {k: v for k, v in _L1_attn_all.items() if k in ('qkv_w', 'qkv_b', 'proj_w', 'proj_b', 'rel_pos_emb')}
    del _L1_attn_all

    def _L1_xattn_setup():
        import jax, jax.numpy as jnp
        import numpy as np
        D_MODEL = 128
        D_K = 64
        D_V = 64
        N_HEADS = 16
        LN_EPS = 1e-05
        key = jax.random.key(seed)
        ks = jax.random.split(key, 9)
        B, S = (2, 256)
        scale = 0.02
        return {'input_Q': jax.random.normal(ks[0], (B, S, D_MODEL), dtype=jnp.float32), 'input_K': jax.random.normal(ks[1], (B, S, D_MODEL), dtype=jnp.float32), 'input_V': jax.random.normal(ks[2], (B, S, D_MODEL), dtype=jnp.float32), 'W_Q': jax.random.normal(ks[3], (D_MODEL, N_HEADS * D_K), dtype=jnp.float32) * scale, 'W_K': jax.random.normal(ks[4], (D_MODEL, N_HEADS * D_K), dtype=jnp.float32) * scale, 'W_V': jax.random.normal(ks[5], (D_MODEL, N_HEADS * D_V), dtype=jnp.float32) * scale, 'W_O': jax.random.normal(ks[6], (N_HEADS * D_V, D_MODEL), dtype=jnp.float32) * scale, 'ln_gamma': jnp.ones((D_MODEL,), dtype=jnp.float32), 'ln_beta': jnp.zeros((D_MODEL,), dtype=jnp.float32)}
    _L1_xattn_all = _L1_xattn_setup()
    _L1_xattn_in = {k: v for k, v in _L1_xattn_all.items() if k in ('W_Q', 'W_K', 'W_V', 'W_O', 'ln_gamma', 'ln_beta')}
    del _L1_xattn_all

    def _L1_ffn_setup():
        import jax, jax.numpy as jnp
        import numpy as np
        D_MODEL, D_FF, N_EXPERTS, TOP_K = (128, 512, 4, 2)
        B, S = (4, 256)
        key = jax.random.key(seed)
        ks = jax.random.split(key, 7)
        s_r = 1.0 / np.sqrt(D_MODEL)
        s_f = 1.0 / np.sqrt(D_FF)
        return {'x': jax.random.normal(ks[0], (B, S, D_MODEL), dtype=jnp.float32), 'Wr': jax.random.uniform(ks[1], (D_MODEL, N_EXPERTS), jnp.float32, -s_r, s_r), 'br': jnp.zeros((N_EXPERTS,), jnp.float32), 'W1': jax.random.uniform(ks[2], (N_EXPERTS, D_MODEL, D_FF), jnp.float32, -s_r, s_r), 'b1': jax.random.uniform(ks[3], (N_EXPERTS, D_FF), jnp.float32, -s_r, s_r), 'W2': jax.random.uniform(ks[4], (N_EXPERTS, D_FF, D_MODEL), jnp.float32, -s_f, s_f), 'b2': jax.random.uniform(ks[5], (N_EXPERTS, D_MODEL), jnp.float32, -s_f, s_f)}
    _L1_ffn_all = _L1_ffn_setup()
    _L1_ffn_in = {k: v for k, v in _L1_ffn_all.items() if k in ('Wr', 'br', 'W1', 'b1', 'W2', 'b2')}
    del _L1_ffn_all
    return {'x': x, 'ctx_1024': ctx_1024, 'L0_attn_ln1_g': _L0_attn_in['ln1_g'], 'L0_attn_ln1_b': _L0_attn_in['ln1_b'], 'L0_attn_Wq': _L0_attn_in['Wq'], 'L0_attn_Wk': _L0_attn_in['Wk'], 'L0_attn_Wv': _L0_attn_in['Wv'], 'L0_attn_Whq': _L0_attn_in['Whq'], 'L0_attn_Whk': _L0_attn_in['Whk'], 'L0_attn_Wo': _L0_attn_in['Wo'], 'L0_attn_ln2_g': _L0_attn_in['ln2_g'], 'L0_attn_ln2_b': _L0_attn_in['ln2_b'], 'L0_attn_W1': _L0_attn_in['W1'], 'L0_attn_b1': _L0_attn_in['b1'], 'L0_attn_W2': _L0_attn_in['W2'], 'L0_attn_b2': _L0_attn_in['b2'], 'L0_xattn_Wq': _L0_xattn_in['Wq'], 'L0_xattn_bq': _L0_xattn_in['bq'], 'L0_xattn_Wk': _L0_xattn_in['Wk'], 'L0_xattn_bk': _L0_xattn_in['bk'], 'L0_xattn_Wv': _L0_xattn_in['Wv'], 'L0_xattn_bv': _L0_xattn_in['bv'], 'L0_xattn_Wo': _L0_xattn_in['Wo'], 'L0_xattn_bo': _L0_xattn_in['bo'], 'L0_ffn_Wr': _L0_ffn_in['Wr'], 'L0_ffn_br': _L0_ffn_in['br'], 'L0_ffn_ln_g': _L0_ffn_in['ln_g'], 'L0_ffn_ln_b': _L0_ffn_in['ln_b'], 'L0_ffn_W1': _L0_ffn_in['W1'], 'L0_ffn_b1': _L0_ffn_in['b1'], 'L0_ffn_W2': _L0_ffn_in['W2'], 'L0_ffn_b2': _L0_ffn_in['b2'], 'L1_attn_qkv_w': _L1_attn_in['qkv_w'], 'L1_attn_qkv_b': _L1_attn_in['qkv_b'], 'L1_attn_proj_w': _L1_attn_in['proj_w'], 'L1_attn_proj_b': _L1_attn_in['proj_b'], 'L1_attn_rel_pos_emb': _L1_attn_in['rel_pos_emb'], 'L1_xattn_W_Q': _L1_xattn_in['W_Q'], 'L1_xattn_W_K': _L1_xattn_in['W_K'], 'L1_xattn_W_V': _L1_xattn_in['W_V'], 'L1_xattn_W_O': _L1_xattn_in['W_O'], 'L1_xattn_ln_gamma': _L1_xattn_in['ln_gamma'], 'L1_xattn_ln_beta': _L1_xattn_in['ln_beta'], 'L1_ffn_Wr': _L1_ffn_in['Wr'], 'L1_ffn_br': _L1_ffn_in['br'], 'L1_ffn_W1': _L1_ffn_in['W1'], 'L1_ffn_b1': _L1_ffn_in['b1'], 'L1_ffn_W2': _L1_ffn_in['W2'], 'L1_ffn_b2': _L1_ffn_in['b2']}

def reference(x, ctx_1024, L0_attn_ln1_g, L0_attn_ln1_b, L0_attn_Wq, L0_attn_Wk, L0_attn_Wv, L0_attn_Whq, L0_attn_Whk, L0_attn_Wo, L0_attn_ln2_g, L0_attn_ln2_b, L0_attn_W1, L0_attn_b1, L0_attn_W2, L0_attn_b2, L0_xattn_Wq, L0_xattn_bq, L0_xattn_Wk, L0_xattn_bk, L0_xattn_Wv, L0_xattn_bv, L0_xattn_Wo, L0_xattn_bo, L0_ffn_Wr, L0_ffn_br, L0_ffn_ln_g, L0_ffn_ln_b, L0_ffn_W1, L0_ffn_b1, L0_ffn_W2, L0_ffn_b2, L1_attn_qkv_w, L1_attn_qkv_b, L1_attn_proj_w, L1_attn_proj_b, L1_attn_rel_pos_emb, L1_xattn_W_Q, L1_xattn_W_K, L1_xattn_W_V, L1_xattn_W_O, L1_xattn_ln_gamma, L1_xattn_ln_beta, L1_ffn_Wr, L1_ffn_br, L1_ffn_W1, L1_ffn_b1, L1_ffn_W2, L1_ffn_b2):
    import jax
    import jax.numpy as jnp

    def _L0_attn_ref(inputs, ln1_g, ln1_b, Wq, Wk, Wv, Whq, Whk, Wo, ln2_g, ln2_b, W1, b1, W2, b2):
        import jax, jax.numpy as jnp
        import numpy as np
        B, S, D, H, NB = (2, 256, 128, 16, 32)
        DH = D // H
        MLP = 512
        CLUSTER_SCORE = 0.1
        LN_EPS = 1e-06

        def _layernorm(x, g, b):
            mu = jnp.mean(x, axis=-1, keepdims=True)
            var = jnp.mean(jnp.square(x - mu), axis=-1, keepdims=True)
            return (x - mu) * jax.lax.rsqrt(var + LN_EPS) * g + b

        def _lha_attention(x, Wq, Wk, Wv, Whq, Whk, Wo):
            q = jnp.einsum('bsd,dhf->bshf', x, Wq)
            k = jnp.einsum('bsd,dhf->bshf', x, Wk)
            v = jnp.einsum('bsd,dhf->bshf', x, Wv)
            qb = jax.nn.softmax(jnp.einsum('bshf,hfn->bshn', q, Whq), axis=-1)
            kb = jax.nn.softmax(jnp.einsum('bshf,hfn->bshn', k, Whk), axis=-1)
            logits = jnp.einsum('bqhf,bkhf->bhqk', q, k) / jnp.sqrt(jnp.float32(DH))
            aff = jnp.einsum('bqhn,bkhn->bhqk', qb, kb)
            logits = logits + CLUSTER_SCORE * aff
            attn = jax.nn.softmax(logits, axis=-1)
            out = jnp.einsum('bhqk,bkhf->bqhf', attn, v)
            out = jnp.einsum('bqhf,hfd->bqd', out, Wo)
            mq = jnp.mean(qb, axis=(0, 1))
            mk = jnp.mean(kb, axis=(0, 1))
            extra_loss = 0.5 * NB * (jnp.mean(jnp.sum(mq * mq, -1)) + jnp.mean(jnp.sum(mk * mk, -1)))
            return (out, extra_loss)

        def _reference_tuple_inner(inputs, ln1_g, ln1_b, Wq, Wk, Wv, Whq, Whk, Wo, ln2_g, ln2_b, W1, b1, W2, b2):
            x = _layernorm(inputs, ln1_g, ln1_b)
            attn_out, extra_loss = _lha_attention(x, Wq, Wk, Wv, Whq, Whk, Wo)
            x = attn_out + inputs
            y = _layernorm(x, ln2_g, ln2_b)
            y = jax.nn.relu(jnp.einsum('bsd,dm->bsm', y, W1) + b1)
            y = jnp.einsum('bsm,md->bsd', y, W2) + b2
            return (x + y, extra_loss)
        return _reference_tuple_inner(inputs, ln1_g, ln1_b, Wq, Wk, Wv, Whq, Whk, Wo, ln2_g, ln2_b, W1, b1, W2, b2)[0]

    def _L0_xattn_ref(query, key, value, Wq, bq, Wk, bk, Wv, bv, Wo, bo):
        import jax, jax.numpy as jnp
        import numpy as np
        H = 16
        D = 128
        DK = D // H
        B, S, _ = query.shape

        def proj(x, W, b):
            return (x @ W.T + b).reshape(B, -1, H, DK).transpose(0, 2, 1, 3)
        q = proj(query, Wq, bq)
        k = proj(key, Wk, bk)
        v = proj(value, Wv, bv)
        score = jnp.einsum('bhqd,bhkd->bhqk', q, k / jnp.sqrt(jnp.float32(DK)))
        p_attn = jax.nn.softmax(score, axis=-1)
        ctx = jnp.einsum('bhqk,bhkd->bhqd', p_attn, v)
        ctx = ctx.transpose(0, 2, 1, 3).reshape(B, S, H * DK)
        return ctx @ Wo.T + bo

    def _L0_ffn_ref(x, Wr, br, ln_g, ln_b, W1, b1, W2, b2):
        import jax, jax.numpy as jnp
        import numpy as np
        B, S, D, F, E = (4, 256, 128, 512, 8)
        LN_EPS = 1e-05
        tokens_shape = x.shape[:-1]
        xt = x.reshape(-1, x.shape[-1])
        router_logits = xt @ Wr + br
        router_probs = jax.nn.softmax(router_logits, axis=-1)
        gates = jnp.max(router_probs, axis=-1, keepdims=True)
        idx = jnp.argmax(router_probs, axis=-1)
        onehot = jax.nn.one_hot(idx, E, dtype=xt.dtype)
        mu = jnp.mean(xt, axis=-1, keepdims=True)
        var = jnp.mean(jnp.square(xt - mu), axis=-1, keepdims=True)
        xn = (xt - mu) * jax.lax.rsqrt(var + LN_EPS) * ln_g + ln_b
        h = jnp.einsum('te,td,edf->tf', onehot, xn, W1) + b1[idx]
        h = jax.nn.relu(h)
        y = jnp.einsum('te,tf,efd->td', onehot, h, W2) + b2[idx]
        y = y * gates
        return y.reshape(tokens_shape + (y.shape[-1],))

    def _L1_attn_ref(x, qkv_w, qkv_b, proj_w, proj_b, rel_pos_emb):
        import jax, jax.numpy as jnp
        import numpy as np
        N_HEADS = 16
        MAX_LEN = 128
        B, T, C = x.shape
        H = N_HEADS
        D = C // H
        qkv = (x @ qkv_w.T + qkv_b).reshape(B, T, 3, H, D)
        qkv = jnp.transpose(qkv, (2, 0, 3, 1, 4))
        q, k, v = (qkv[0], qkv[1], qkv[2])
        att = jnp.einsum('bhtd,bhsd->bhts', q, k) / np.sqrt(D).astype(np.float32)
        table = rel_pos_emb.reshape(2 * MAX_LEN - 1, H, D).sum(axis=-1)
        pos = jnp.arange(T)
        rel_idx = pos[:, None] - pos[None, :] + (MAX_LEN - 1)
        bias = jnp.transpose(table[rel_idx], (2, 0, 1))
        att = att + bias[None]
        causal = pos[None, :] > pos[:, None]
        att = jnp.where(causal[None, None], -jnp.inf, att)
        att = jax.nn.softmax(att, axis=-1)
        out = jnp.einsum('bhts,bhsd->bhtd', att, v)
        out = jnp.transpose(out, (0, 2, 1, 3)).reshape(B, T, C)
        return out @ proj_w.T + proj_b

    def _L1_xattn_ref(input_Q, input_K, input_V, W_Q, W_K, W_V, W_O, ln_gamma, ln_beta):
        import jax, jax.numpy as jnp
        import numpy as np
        D_MODEL = 128
        D_K = 64
        D_V = 64
        N_HEADS = 16
        LN_EPS = 1e-05
        B, Lq, _ = input_Q.shape
        Lk = input_K.shape[1]
        Q = (input_Q @ W_Q).reshape(B, Lq, N_HEADS, D_K).transpose(0, 2, 1, 3)
        K = (input_K @ W_K).reshape(B, Lk, N_HEADS, D_K).transpose(0, 2, 1, 3)
        V = (input_V @ W_V).reshape(B, Lk, N_HEADS, D_V).transpose(0, 2, 1, 3)
        scores = jnp.einsum('bhqd,bhkd->bhqk', Q, K) / jnp.sqrt(jnp.float32(D_K))
        attn = jax.nn.softmax(scores, axis=1)
        context = jnp.einsum('bhqk,bhkv->bhqv', attn, V)
        context = context.transpose(0, 2, 1, 3).reshape(B, Lq, N_HEADS * D_V)
        output = context @ W_O
        x = output + input_Q
        mu = jnp.mean(x, axis=-1, keepdims=True)
        var = jnp.mean(jnp.square(x - mu), axis=-1, keepdims=True)
        return (x - mu) / jnp.sqrt(var + LN_EPS) * ln_gamma + ln_beta

    def _L1_ffn_ref(x, Wr, br, W1, b1, W2, b2):
        import jax, jax.numpy as jnp
        import numpy as np
        D_MODEL, D_FF, N_EXPERTS, TOP_K = (128, 512, 4, 2)
        B, S = (4, 256)
        router_logits = jnp.einsum('bsd,de->bse', x, Wr) + br
        router_probs = jax.nn.softmax(router_logits, axis=-1)
        top_k_probs, top_k_idx = jax.lax.top_k(router_probs, TOP_K)
        top_k_probs = top_k_probs / jnp.sum(top_k_probs, axis=-1, keepdims=True)
        h = jnp.einsum('bsd,edf->bsef', x, W1) + b1
        h = jax.nn.gelu(h, approximate=False)
        expert_out = jnp.einsum('bsef,efd->bsed', h, W2) + b2
        sel = jnp.take_along_axis(expert_out, top_k_idx[..., None], axis=2)
        out = jnp.sum(sel * top_k_probs[..., None], axis=2)
        return out
    x = _layernorm(x + _L0_attn_ref(x, L0_attn_ln1_g, L0_attn_ln1_b, L0_attn_Wq, L0_attn_Wk, L0_attn_Wv, L0_attn_Whq, L0_attn_Whk, L0_attn_Wo, L0_attn_ln2_g, L0_attn_ln2_b, L0_attn_W1, L0_attn_b1, L0_attn_W2, L0_attn_b2), axis=-1)
    x = _layernorm(x + _L0_xattn_ref(x, ctx_1024, ctx_1024, L0_xattn_Wq, L0_xattn_bq, L0_xattn_Wk, L0_xattn_bk, L0_xattn_Wv, L0_xattn_bv, L0_xattn_Wo, L0_xattn_bo), axis=-1)
    x = _layernorm(x + _L0_ffn_ref(x, L0_ffn_Wr, L0_ffn_br, L0_ffn_ln_g, L0_ffn_ln_b, L0_ffn_W1, L0_ffn_b1, L0_ffn_W2, L0_ffn_b2), axis=-1)
    x = _layernorm(x + _L1_attn_ref(x, L1_attn_qkv_w, L1_attn_qkv_b, L1_attn_proj_w, L1_attn_proj_b, L1_attn_rel_pos_emb), axis=-1)
    x = _layernorm(x + _L1_xattn_ref(x, ctx_1024, ctx_1024, L1_xattn_W_Q, L1_xattn_W_K, L1_xattn_W_V, L1_xattn_W_O, L1_xattn_ln_gamma, L1_xattn_ln_beta), axis=-1)
    x = _layernorm(x + _L1_ffn_ref(x, L1_ffn_Wr, L1_ffn_br, L1_ffn_W1, L1_ffn_b1, L1_ffn_W2, L1_ffn_b2), axis=-1)
    return x

_drawn_inputs = setup_inputs


def setup_inputs(seed=0):
    import zlib

    import numpy as np

    out = dict(_drawn_inputs(seed))
    spreads = {'L0_attn_ln1_g': (1.0, 0.6),
     'L0_attn_ln1_b': (0.0, 0.8),
     'L0_attn_ln2_g': (1.0, 0.6),
     'L0_attn_ln2_b': (0.0, 2.0),
     'L0_attn_b1': (0.0, 0.454),
     'L0_attn_b2': (0.0, 0.1),
     'L0_xattn_bq': (0.0, 0.299),
     'L0_xattn_bk': (0.0, 2.0),
     'L0_xattn_bv': (0.0, 0.1),
     'L0_xattn_bo': (0.0, 0.1),
     'L0_ffn_br': (0.0, 0.338),
     'L0_ffn_ln_g': (1.0, 0.6),
     'L0_ffn_ln_b': (0.0, 0.8),
     'L0_ffn_b1': (0.0, 0.8),
     'L0_ffn_b2': (0.0, 0.386),
     'L1_xattn_ln_gamma': (1.0, 0.2),
     'L1_xattn_ln_beta': (0.0, 0.1),
     'L1_ffn_br': (0.0, 0.1)}
    factors = {'L0_attn_Wq': 8.0,
     'L0_attn_Wk': 8.0,
     'L0_attn_Wv': 8.0,
     'L0_attn_Whq': 64.0,
     'L0_attn_Whk': 64.0,
     'L0_attn_Wo': 8.0,
     'L0_ffn_W1': 3.794,
     'L0_ffn_W2': 3.218,
     'L1_attn_qkv_b': 6.944,
     'L1_attn_rel_pos_emb': 62.645,
     'L1_xattn_W_Q': 7.439,
     'L1_xattn_W_K': 7.621,
     'L1_ffn_b1': 4.524,
     'L1_ffn_b2': 3.06}
    for name, (base, spread) in spreads.items():
        noise = np.random.default_rng([zlib.crc32(name.encode()), seed]).standard_normal(out[name].shape)
        drawn = base * np.exp(spread * noise) if base else spread * noise
        out[name] = jnp.asarray(drawn.astype(out[name].dtype))
    for name, factor in factors.items():
        out[name] = (out[name] * factor).astype(out[name].dtype)
    return out
```

```python
from contextlib import ExitStack

import concourse.bass as bass
from concourse import mybir

F32 = mybir.dt.float32
BF16 = mybir.dt.bfloat16
I32 = mybir.dt.int32
ALU = mybir.AluOpType
ACT = mybir.ActivationFunctionType
AX = mybir.AxisListType

P = 128
B, S, D = 128, 64, 128
GT = 512
NG = B * S // GT
NT = GT // P
NU = NT // 2
NB = GT // S
H, DH, QUAD = 16, 8, 4
NBK = 32
F = 512
FC = F // P
E0, E1 = 8, 4
DK = 64
NCH = H * DK // P
SQ8 = float(DH) ** 0.5
NEG = -1e30
N_SETUP = 14

COLS = ["ln1_g", "ln1_b", "ln2_g", "ln2_b", "mb0", "mb1", "mb2", "mb3", "xbq", "xbk", "xbv",
        "lnf_g", "lnf_b", "cbq", "cbk", "cbv"] + [f"fb{i}" for i in range(E1 * FC)]
COL = {n: i for i, n in enumerate(COLS)}
ROWS = {"mlp_b2": (0, P), "xbo": (P, P), "cbo": (2 * P, P), "lnx_g": (3 * P, P), "lnx_b": (4 * P, P),
        "r0": (5 * P, E0), "r1": (5 * P + E0, E1)}
NROW = 5 * P + E0 + E1

LN_EPS = [1e-6, 1e-6, 1e-5, 1e-5, 1e-5, 1e-5, 1e-5, 1e-5, 1e-5, 1e-5]
L_A1, L_A2, L_O1, L_O2, L_F, L_O3, L_O4, L_X, L_O5, L_O6 = range(10)

SIGNALS = {
    "ln_stats": 40, "ln_mv": 20, "ln_newton": 20 * 3, "ln_out": 20,
    "ln_log": 20, "ln_guess": 20,
    "xT_ps": 8, "xT": 8,
    "q_ps": 3, "k_ps": 3, "v_ps": 3, "qT": 3, "kT": 3, "kexp": 3, "vbd": 3,
    "scores": 6, "biased": 2, "smax": 6, "sdiff": 6, "probs": 12,
    "pT_ps": 12, "pT_a": 12, "pT_v": 12, "pv_ps": 12, "rden": 24, "attn": 12,
    "aT_ps": 6, "aT": 6, "o_ps": 6, "res": 6,
    "hb_ps": 4, "hb_max": 4, "hb_diff": 4, "hb_exp": 4, "hb_sum": 4, "hb_rec": 4, "hb_norm": 4,
    "hbT_ps": 4, "qbT": 4, "kbT": 4,
    "m_ps": 4, "m_h": 4, "m2_ps": 2, "xs_part": 2, "xs": 2,
    "r_ps": 1, "rv": 9, "r_exp": 1, "onehot": 1, "ohT_ps": 1, "ohT": 1, "mask_ps": 8, "xe": 8,
    "e_ps": 4, "e_h": 4, "e2_ps": 4, "e_prod": 4, "e_sum": 4, "e_out": 4,
    "wq_ps": 8, "wk_ps": 8, "wv_ps": 4, "wq": 8, "wk": 8, "wv": 4,
    "ws_ps": 4, "w_max": 4, "w_diff": 4, "w_exp": 4, "w_sum": 4, "w_rec": 4, "w_attn": 4,
    "wc_ps": 4, "wc": 4, "wo_ps": 2, "w_res": 2, "w_gain": 2,"w_x": 2,
    "g_ps": 16, "g_h": 16, "r6_ps": 1, "r6v": 14, "r6_exp": 1, "gw": 1, "gwT_ps": 1, "gwT": 1,
    "g2_ps": 4, "g_prod": 4, "g_sum": 4, "g_out": 4,
    "outer": 16,
}
DMA_SIGNALS = ("x_in", "ctx_in", "out_done", "weights", "bias_dup")
OTHER = ("setup", "setup_pe", "setup_v", "setup_act", "x_free", "ctx_free", "out_ready", "out_free", "apart")


class Values:

    def __init__(self, eng, sems, it):
        self.eng, self.sems, self.it = eng, sems, it
        self.base = {}

    def wait(self, name, k):
        per = SIGNALS[name]
        assert 1 <= k <= per, (name, k)
        if per not in self.base:
            self.base[per] = self.eng.snap(self.it * per)
        self.eng.wait_ge(self.sems[name], self.base[per] + k)

    def wait_apart(self, *waits):
        for name, k in waits:
            self.wait(name, k)
        self.eng.sem_inc(self.sems["apart"], 1)


def decoder_kernel(nc, A, out, groups=NG, last_stage=6):
    ctx = ExitStack()
    with ctx:
        def sb(name, shape, dt=F32):
            return ctx.enter_context(nc.sbuf_tensor(name, shape, dt))

        sem = {n: ctx.enter_context(nc.semaphore(n)) for n in (*SIGNALS, *DMA_SIGNALS, *OTHER)}
        given = {n: 0 for n in SIGNALS}

        wq = [sb(f"wq{c}", [P, P]) for c in range(3)]
        wk = [sb(f"wk{c}", [P, P]) for c in range(3)]
        wv = [sb(f"wv{c}", [P, P]) for c in range(3)]
        wo = [sb(f"wo{c}", [P, P]) for c in range(3)]
        whash_raw = sb("whash_raw", [P, 2, NBK])
        whash = sb("whash", [P, 2, H * NBK])
        m_w1, m_w2 = sb("m_w1", [P, F]), sb("m_w2", [P, FC, P])
        e_w1, e_w2 = sb("e_w1", [P, E0, F]), sb("e_w2", [P, FC, E0, P])
        e_b1, e_b2, e_r = sb("e_b1", [E0, F]), sb("e_b2", [E0, P]), sb("e_r", [P, E0])
        ww = [sb(f"ww{n}", [P, H * DK]) for n in "qkv"]
        wwo = sb("wwo", [P, NCH, P])
        g_w1, g_w2 = sb("g_w1", [P, E1, F]), sb("g_w2", [P, FC, E1, P])
        g_b2, g_r = sb("g_b2", [E1, P]), sb("g_r", [P, E1])
        cols = sb("cols", [P, len(COLS)])
        rows = sb("rows", [P, NROW])
        emb = sb("emb", [P, P])

        ident = sb("ident", [P, P])
        hmask = sb("hmask", [P, H])
        qmask = sb("qmask", [P, QUAD])
        pick = sb("pick", [E0, E0, P], BF16)
        falling0, falling1 = sb("falling0", [P, E0]), sb("falling1", [P, E1])
        epsc = sb("epsc", [P, 2])
        bias = sb("bias", [P, H, S])
        embT, tabT = sb("embT", [P, P]), sb("tabT", [H, P])

        xin = sb("xin", [P, NT, D])
        xa, xb, xc = sb("xa", [P, NT, D]), sb("xb", [P, NT, D]), sb("xc", [P, NT, D])
        xsum = sb("xsum", [P, NT, D])
        xn = sb("xn", [P, NT, D])
        yout = sb("yout", [P, NT, D])
        xT, xT2, ctxT = sb("xT", [P, GT]), sb("xT2", [P, GT]), sb("ctxT", [P, GT])
        qT, kT = sb("qT", [P, GT]), sb("kT", [P, GT])
        vbd = sb("vbd", [P, NB, H // 2, 2 * (DH + 1)])
        attn, aT = sb("attn", [P, NT, D]), sb("aT", [P, GT])
        probs = sb("probs", [P, 2, QUAD, 2, QUAD * S])
        pT = sb("pT", [P, 2, H // 2, P])
        smax = sb("smax", [P, 2, 2 * H])
        rden = sb("rden", [P, 2, H // 2, 2])
        stats, mv = sb("stats", [P, NT, 6]), sb("mv", [P, NT, 2])
        lnlog, rstd = sb("lnlog", [P, NT]), sb("rstd", [P, NT, 4])
        hbm, hbs, hbr = sb("hbm", [P, 2, 2 * H]), sb("hbs", [P, 2, 2 * H]), sb("hbr", [P, 2, 2 * H])
        wmax, wsum, wrec = sb("wmax", [P, 2, S]), sb("wsum", [P, 2, S]), sb("wrec", [P, 2, S])
        lg, lgm = sb("lg", [P, NT, E0]), sb("lgm", [P, NT, 8])
        le, oh, oh2 = sb("le", [P, NT, E0]), sb("oh", [P, NT, E0]), sb("oh2", [P, NT, E0])
        ohT, ohTb = sb("ohT", [E0, GT]), sb("ohTb", [E0, GT], BF16)
        ebias = sb("ebias", [P, NT, D])

        arena = sb("arena", [P, 8192])
        hash_T = [arena[:, 4096 + 2048 * n:4096 + 2048 * (n + 1)].rearrange("p (i t) -> p i t", i=QUAD)
                  for n in range(2)]
        xe = arena[:, 0:4096].rearrange("p (e t) -> p e t", e=E0)
        wqT = arena[:, 0:4096].rearrange("p (c t) -> p c t", c=NCH)
        wkT = arena[:, 4096:8192].rearrange("p (c t) -> p c t", c=NCH)
        gh = arena[:, :].rearrange("p (c t) -> p c t", c=E1 * FC)
        arena2 = sb("arena2", [P, 4096])
        kexp = arena2[:, 0:2048].rearrange("p (i t) -> p i t", i=QUAD)
        hT = arena2[:, 2048:4096].rearrange("p (c t) -> p c t", c=FC)
        wvt = arena2[:, :].rearrange("p (t f) -> p t f", t=NT)
        hb = arena[:, 0:2048].rearrange("p (s f) -> p s f", s=2)
        prod = probs[:, 0, :, :, :].rearrange("p j t f -> p (j t f)").rearrange("p (s f) -> p s f", s=2)

        ps = ctx.enter_context(nc.psum_tensor("ps", [P, 8, 512], F32))
        flat = ps[:, :, :].rearrange("p a b -> p (a b)")

        def bank(b, n=1):
            return flat[:, 512 * b:512 * (b + n)]

        quad = ps[:, 0:4, :]

        def col(name):
            return cols[:, COL[name]:COL[name] + 1]

        def row(name):
            return rows[:, ROWS[name][0]:ROWS[name][0] + ROWS[name][1]]

        def done(instruction, name):
            given[name] += 1
            instruction.then_inc(sem[name], 1)

        block = ctx.enter_context(nc.Block())
        run = lambda n: last_stage >= n

        x_v = A["x"].rearrange("(g t p) d -> g p t d", t=NT, p=P)
        c_v = A["ctxT"].rearrange("p (g t) -> g p t", t=GT)
        o_v = out.rearrange("b s d -> (b s) d").rearrange("(g t p) d -> g p t d", t=NT, p=P)
        loads = [
            (cols[:], A["cols"]), (rows[:], A["rows"].to_broadcast((P, NROW))), (emb[0:127, :], A["emb"]),
            (wq[0][:], A["wq0"]), (wk[0][:], A["wk0"]), (wv[0][:], A["wv0"]), (wo[0][:], A["wo0"]),
            (whash_raw[:, 0, :], A["whq"]), (whash_raw[:, 1, :], A["whk"]),
            (m_w1[:], A["m_w1"]), (m_w2[:], A["m_w2"].rearrange("(c p) d -> p c d", p=P)),
            (wq[1][:], A["wq1"]), (wk[1][:], A["wk1"]), (wv[1][:], A["wv1"]), (wo[1][:], A["wo1"]),
            (e_r[:], A["e_r"]), (e_w1[:], A["e_w1"].rearrange("e d f -> d e f")),
            (e_b1[:], A["e_b1"]), (e_b2[:], A["e_b2"]),
        ] + [(e_w2[:, c, :, :], A["e_w2"][:, c * P:(c + 1) * P, :].rearrange("e p d -> p e d"))
             for c in range(FC)] + [
            (wq[2][:], A["wq2"]), (wk[2][:], A["wk2"]), (wv[2][:], A["wv2"]), (wo[2][:], A["wo2"]),
            (ww[0][:], A["wwq"]), (ww[1][:], A["wwk"]), (ww[2][:], A["wwv"]),
            (wwo[:], A["wwo"].rearrange("(c p) d -> p c d", p=P)),
            (g_r[:], A["g_r"]), (g_w1[:], A["g_w1"].rearrange("e d f -> d e f")), (g_b2[:], A["g_b2"]),
        ] + [(g_w2[:, c, :, :], A["g_w2"][:, c * P:(c + 1) * P, :].rearrange("e p d -> p e d"))
             for c in range(FC)]
        NW = len(loads)

        @block.sync
        def _(sp):
            sp.dma_start(xin[:], x_v[0]).then_inc(sem["x_in"], 16)
            for dst, src in loads:
                sp.dma_start(dst, src).then_inc(sem["weights"], 16)
            sp.dma_start(ctxT[:], c_v[0]).then_inc(sem["ctx_in"], 16)
            sp.wait_ge(sem["setup_v"], 6)
            sp.dma_start(bias[S:P, :, :], bias[0:S, :, :]).then_inc(sem["bias_dup"], 16)
            if groups > 1:
                with sp.Fori(0, groups - 1) as it:
                    sp.wait_ge(sem["x_free"], it + 1)
                    sp.dma_start(xin[:], x_v[it + 1]).then_inc(sem["x_in"], 16)
                    sp.wait_ge(sem["ctx_free"], it + 1)
                    sp.dma_start(ctxT[:], c_v[it + 1]).then_inc(sem["ctx_in"], 16)
                    sp.wait_ge(sem["out_ready"], it + 1)
                    sp.dma_start(o_v[it], yout[:]).then_inc(sem["out_done"], 16)
                    sp.wait_ge(sem["out_done"], (it + 1) * 16)
                    sp.sem_inc(sem["out_free"], 1)
            sp.wait_ge(sem["out_ready"], groups)
            sp.dma_start(o_v[groups - 1], yout[:]).then_inc(sem["out_done"], 16)
            sp.wait_ge(sem["out_done"], groups * 16)

        @block.gpsimd
        def _(pool):
            n = [0]

            def link(instruction):
                n[0] += 1
                instruction.then_inc(sem["setup"], 1)
                pool.wait_ge(sem["setup"], n[0])

            link(pool.memset(ident[:], 0.0))
            link(pool.affine_select(ident[:], ident[:], [[-1, P]], ALU.not_equal, 1.0, base=0, channel_multiplier=1))
            link(pool.memset(hmask[:], 1.0))
            link(pool.affine_select(hmask[:], hmask[:], [[-DH, H]], ALU.is_ge, 0.0, base=0, channel_multiplier=1))
            link(pool.affine_select(hmask[:], hmask[:], [[DH, H]], ALU.is_ge, 0.0, base=DH - 1, channel_multiplier=-1))
            link(pool.memset(pick[:], 0.0))
            link(pool.affine_select(pick[:], pick[:], [[-1, E0], [0, P]], ALU.not_equal, 1.0, base=0, channel_multiplier=1))
            link(pool.iota(falling0[:], [[-1, E0]], base=E0, channel_multiplier=0, allow_small_or_imprecise_dtypes=True))
            link(pool.iota(falling1[:], [[-1, E1]], base=E1, channel_multiplier=0, allow_small_or_imprecise_dtypes=True))
            link(pool.memset(vbd[:], 0.0))
            link(pool.memset(vbd[0:S, :, :, DH:DH + 1], 1.0))
            link(pool.memset(vbd[S:P, :, :, 2 * DH + 1:2 * DH + 2], 1.0))
            link(pool.memset(epsc[:, 0:1], 1e-6))
            link(pool.memset(epsc[:, 1:2], 1e-5))
            pool.wait_ge(sem["setup_v"], 5)
            pool.affine_select(bias[0:S], bias[0:S], [[0, H], [-1, S]], ALU.is_ge, NEG, base=0,
                               channel_multiplier=1).then_inc(sem["setup_v"], 1)
            pool.sem_inc(sem["out_free"], 1)

            def expand_k(v, c):
                v.wait("kT", c + 1)
                done(pool.tensor_tensor(kexp, kT[:].unsqueeze(1).broadcast_to((P, QUAD, GT)),
                                        qmask[:].unsqueeze(2).broadcast_to((P, QUAD, GT)), ALU.mult), "kexp")

            assert n[0] == N_SETUP
            pool.wait_ge(sem["weights"], 16 * NW)
            with pool.Fori(0, groups) as it:
                v = Values(pool, sem, it)
                if run(1):
                    pool.wait_ge(sem["setup_v"], 1)
                    expand_k(v, 0)
                    for t in range(NT):
                        v.wait("hb_rec", t + 1)
                        e = hb[:, t % 2, :].rearrange("p (h n) -> p h n", n=NBK)
                        done(pool.tensor_tensor(e, e, hbr[:, t % 2, :].unsqueeze(2).broadcast_to((P, 2 * H, NBK)),
                                                ALU.mult), "hb_norm")
                    for u in range(NU):
                        v.wait("res", u + 1)
                        s = slice(2 * u, 2 * u + 2)
                        done(pool.tensor_tensor(xsum[:, s, :], xin[:, s, :], xa[:, s, :], ALU.add), "xs_part")
                        v.wait("xs_part", u + 1)
                        done(pool.tensor_tensor(xsum[:, s, :], xsum[:, s, :],
                                                row("mlp_b2").unsqueeze(1).broadcast_to((P, 2, D)), ALU.add), "xs")
                if run(2):
                    expand_k(v, 1)
                if run(4):
                    expand_k(v, 2)

        @block.scalar
        def _(act):
            act.wait_ge(sem["setup_pe"], 1)
            nc.scalar.activation(embT[:, 0:127], bank(0)[:, 0:127], ACT.Copy).then_inc(sem["setup_act"], 1)
            act.wait_ge(sem["setup_pe"], 2)
            nc.scalar.activation(tabT[:, 0:127], bank(1)[0:H, 0:127], ACT.Copy).then_inc(sem["setup_act"], 1)

            def ln(v, n):
                eps = epsc[:, 0:1] if LN_EPS[n] == 1e-6 else epsc[:, 1:2]
                for u in range(NU):
                    s = slice(2 * u, 2 * u + 2)
                    v.wait("ln_mv", 2 * n + u + 1)
                    done(nc.scalar.activation(lnlog[:, s], mv[:, s, 1], ACT.Ln, bias=eps), "ln_log")
                    v.wait("ln_log", 2 * n + u + 1)
                    done(nc.scalar.activation(rstd[:, s, 0], lnlog[:, s], ACT.Exp, scale=-0.5), "ln_guess")

            def copy_xT(v, k, dst, b, gain=None, shift=None):
                v.wait("xT_ps", k)
                if gain is None:
                    i = nc.scalar.activation(dst, bank(b), ACT.Copy)
                else:
                    i = nc.scalar.activation(dst, bank(b), ACT.Identity, scale=col(gain), bias=col(shift))
                done(i, "xT")

            def attention(v, c, bv=None):
                for u in range(NU):
                    v.wait("sdiff", 2 * c + u + 1)
                    for t in range(2):
                        p = probs[:, u, :, t, :]
                        done(nc.scalar.activation(p, p, ACT.Exp), "probs")
                    for t in range(2 * u, 2 * u + 2):
                        v.wait("pT_ps", 4 * c + t + 1)
                        done(nc.scalar.activation(pT[:, t % 2, 0:4, :].rearrange("p c q -> p (c q)"), bank(4), ACT.Copy),
                             "pT_a")
                    v.wait("aT_ps", 2 * c + u + 1)
                    src, dst = bank(7)[:, 0:256], aT[:, 256 * u:256 * (u + 1)]
                    if bv is None:
                        i = nc.scalar.activation(dst, src, ACT.Copy)
                    else:
                        i = nc.scalar.activation(dst, src, ACT.Identity, bias=col(bv))
                    done(i, "aT")

            act.wait_ge(sem["weights"], 16 * NW)
            act.wait_ge(sem["setup"], N_SETUP)
            tables = "natural_log_exp_and_others"
            act.preload_act_table_set(tables)
            with act.Fori(0, groups) as it:
                v = Values(act, sem, it)
                if run(1):
                    ln(v, L_A1)
                    copy_xT(v, 1, xT[:], 4, "ln1_g", "ln1_b")
                    v.wait("q_ps", 1)
                    done(nc.scalar.activation(qT[:], bank(0), ACT.Copy, scale=1.0 / SQ8), "qT")
                    v.wait("k_ps", 1)
                    done(nc.scalar.activation(kT[:], bank(1), ACT.Copy), "kT")
                    for t in range(NT):
                        v.wait("hb_diff", t + 1)
                        e = hb[:, t % 2, :]
                        nc.scalar.activation(e[:, 0:512], e[:, 0:512], ACT.Exp, scale=SQ8)
                        done(nc.scalar.activation(e[:, 512:1024], e[:, 512:1024], ACT.Exp), "hb_exp")
                        v.wait("hbT_ps", t + 1)
                        tok = slice(P * t, P * (t + 1))
                        done(nc.scalar.activation(hash_T[0][:, :, tok], bank(6).rearrange("p (i q) -> p i q", i=QUAD),
                                                  ACT.Copy, scale=0.1), "qbT")
                    attention(v, 0)
                    ln(v, L_A2)
                    copy_xT(v, 2, xT2[:], 4, "ln2_g", "ln2_b")
                    for c in range(FC):
                        v.wait("m_ps", c + 1)
                        done(nc.scalar.activation(hT[:, c, :], bank(c), ACT.Relu, bias=col(f"mb{c}")), "m_h")
                    ln(v, L_O1)
                if run(2):
                    copy_xT(v, 3, xT[:], 4)
                    attention(v, 1, "xbv")
                    ln(v, L_O2)
                if run(3):
                    copy_xT(v, 4, xT[:], 4)
                    v.wait("rv", 2)
                    done(nc.scalar.activation(le[:], lg[:], ACT.Exp), "r_exp")
                    ln(v, L_F)
                    copy_xT(v, 5, xT2[:], 5, "lnf_g", "lnf_b")
                    for c in range(FC):
                        v.wait("e_ps", c + 1)
                        done(nc.scalar.activation(hT[:, c, :], bank(c), ACT.Relu), "e_h")
                    ln(v, L_O3)
                if run(4):
                    copy_xT(v, 6, xT[:], 4)
                    attention(v, 2, "cbv")
                    ln(v, L_O4)
                if run(5):
                    copy_xT(v, 7, xT[:], 4)
                    for c in range(NCH):
                        v.wait("wq_ps", c + 1)
                        done(nc.scalar.activation(wqT[:, c, :], bank(2 * (c % 2)), ACT.Copy, scale=DK ** -0.5), "wq")
                    for t in range(NT):
                        v.wait("wv_ps", t + 1)
                        done(nc.scalar.activation(wvt[:, t, :], bank(4 + 2 * (t % 2), 2), ACT.Copy), "wv")
                    for t in range(NT):
                        v.wait("w_diff", t + 1)
                        e = probs[:, t // 2, 2 * (t % 2):2 * (t % 2) + 2, :, :].rearrange("p a b c -> p (a b c)")
                        done(nc.scalar.activation(e, e, ACT.Exp), "w_exp")
                        v.wait("wc_ps", t + 1)
                        if t == 2:
                            v.wait("wo_ps", 1)
                        for bb in range(2):
                            i = nc.scalar.activation(pT[:, t % 2, :, S * bb:S * (bb + 1)],
                                                     bank(4 + bb).rearrange("p (c q) -> p c q", c=NCH), ACT.Copy)
                        done(i, "wc")
                    ln(v, L_X)
                    ln(v, L_O5)
                if run(6):
                    copy_xT(v, 8, xT[:], 4)
                    v.wait("r6v", 2)
                    done(nc.scalar.activation(le[:, :, 0:E1], lg[:, :, 0:E1], ACT.Exp), "r6_exp")
                    for n in range(E1 * FC):
                        v.wait("g_ps", n + 1)
                        done(nc.scalar.activation(gh[:, n, :], bank(n % 4), ACT.Gelu, bias=col(f"fb{n}")), "g_h")
                    act.preload_act_table_set(tables)
                    ln(v, L_O6)

        @block.vector
        def _(dve):
            dve.wait_ge(sem["setup"], N_SETUP)
            dve.tensor_reduce(qmask[:], hmask[:].rearrange("p (j i) -> p i j", i=QUAD), AX.X, ALU.add)\
               .then_inc(sem["setup_v"], 1)
            dve.wait_ge(sem["weights"], 16 * NW)
            for n in range(2):
                for i in range(QUAD):
                    m = dve.tensor_tensor(
                        whash[:, n, i * P:(i + 1) * P].rearrange("p (j n) -> p j n", n=NBK),
                        whash_raw[:, n, :].unsqueeze(1).broadcast_to((P, QUAD, NBK)),
                        hmask[:].rearrange("p (j i) -> p i j", i=QUAD)[:, i, :].unsqueeze(2).broadcast_to((P, QUAD, NBK)),
                        ALU.mult)
                m.then_inc(sem["setup_v"], 1)
            dve.memset(rstd[:], 0.0).then_inc(sem["setup_v"], 1)
            dve.wait_ge(sem["setup_pe"], 3)
            dve.tensor_copy(bias[0:S], bank(2, 2)[0:S, 0:S * H].rearrange("p (s h) -> p h s", h=H))\
               .then_inc(sem["setup_v"], 1)

            def ln(v, n, src, dst):
                eps = LN_EPS[n]
                for u in range(NU):
                    for t in range(2 * u, 2 * u + 2):
                        done(dve.bn_stats(stats[:, t, :], src[:, t, :]), "ln_stats")
                    for t in range(2 * u, 2 * u + 2):
                        v.wait_apart(("ln_stats", 4 * n + t + 1))
                        m = dve.bn_aggr(mv[:, t, :], stats[:, t, :])
                    done(m, "ln_mv")
                for u in range(NU):
                    s = slice(2 * u, 2 * u + 2)
                    v.wait("ln_guess", 2 * n + u + 1)
                    y, a, b, r = (rstd[:, s, k] for k in range(4))
                    k = 3 * (2 * n + u)
                    done(dve.scalar_tensor_tensor(a, mv[:, s, 1], eps, y, ALU.add, ALU.mult), "ln_newton")
                    v.wait("ln_newton", k + 1)
                    done(dve.scalar_tensor_tensor(b, a, -0.5, y, ALU.mult, ALU.mult), "ln_newton")
                    v.wait("ln_newton", k + 2)
                    done(dve.scalar_tensor_tensor(r, b, 1.5, y, ALU.add, ALU.mult), "ln_newton")
                    v.wait("ln_newton", k + 3)
                    for t in range(2 * u, 2 * u + 2):
                        m = dve.tensor_scalar(dst[:, t, :], src[:, t, :], mv[:, t, 0:1], rstd[:, t, 3:4],
                                              ALU.subtract, ALU.mult)
                    done(m, "ln_out")
                v.wait("ln_out", 2 * n + 2)

            def values_by_head(v, c):
                v.wait("v_ps", c + 1)
                for r in range(2):
                    half = slice(S * r, S * (r + 1))
                    m = dve.tensor_copy(vbd[half, :, :, (DH + 1) * r:(DH + 1) * r + DH],
                                        bank(2)[half, :].rearrange("p (b c d) -> p b c d", b=NB, d=DH))
                done(m, "vbd")

            def attention(v, c, res_in, res_out, obias=None):
                for u in range(NU):
                    v.wait("scores", 2 * c + u + 1)
                    sc = flat[:, 0:2048].rearrange("p (g k) -> p g k", k=S)
                    pr = probs[:, u, :, :, :].rearrange("p j t (i k) -> p (j t i) k", k=S)
                    if c == 2:
                        for t in range(2):
                            m = dve.tensor_tensor(
                                probs[:, u, :, t, :], quad[:, :, 256 * t:256 * (t + 1)],
                                bias[:].rearrange("p (j i) k -> p j (i k)", i=QUAD), ALU.add)
                        done(m, "biased")
                        v.wait("biased", u + 1)
                        sc = pr
                    done(dve.tensor_reduce(smax[:, u, :], sc, AX.X, ALU.max), "smax")
                    v.wait("smax", 2 * c + u + 1)
                    done(dve.tensor_tensor(pr, sc, smax[:, u, :].unsqueeze(2).broadcast_to((P, 2 * H, S)),
                                           ALU.subtract), "sdiff")
                for u in range(NU):
                    for t in range(2 * u, 2 * u + 2):
                        v.wait("pT_ps", 4 * c + t + 1)
                        done(dve.tensor_copy(pT[:, t % 2, 4:8, :].rearrange("p c q -> p (c q)"), bank(5)), "pT_v")
                        v.wait("pv_ps", 4 * c + t + 1)
                        pv = bank(6)[:, 0:288].rearrange("p (c b h e) -> p c b h e", c=8, b=2, h=2)
                        for bb in range(2):
                            q = slice(S * bb, S * (bb + 1))
                            done(dve.reciprocal(rden[q, t % 2, :, :], pv[q, :, bb, :, DH]), "rden")
                        for bb in range(2):
                            q = slice(S * bb, S * (bb + 1))
                            v.wait("rden", 8 * c + 2 * t + bb + 1)
                            m = dve.tensor_tensor(attn[q, t, :].rearrange("p (c h d) -> p c h d", c=8, h=2),
                                                  pv[q, :, bb, :, 0:DH],
                                                  rden[q, t % 2, :, :].unsqueeze(3).broadcast_to((S, 8, 2, DH)), ALU.mult)
                        done(m, "attn")
                    s = slice(2 * u, 2 * u + 2)
                    v.wait("o_ps", 2 * c + u + 1)
                    o = bank(7)[:, 256:512].rearrange("p (t d) -> p t d", t=2)
                    if obias is None:
                        done(dve.tensor_tensor(res_out[:, s, :], o, res_in[:, s, :], ALU.add), "res")
                    else:
                        done(dve.tensor_tensor(res_out[:, s, :], o, xsum[:, s, :], ALU.add), "res")

            n_outer = [0]

            def chain(v, instruction):
                done(instruction, "outer")
                n_outer[0] += 1
                v.wait("outer", n_outer[0])

            dve.wait_ge(sem["bias_dup"], 16)
            with dve.Fori(0, groups) as it:
                v = Values(dve, sem, it)
                n_outer[0] = 0
                if run(1):
                    dve.wait_ge(sem["x_in"], it * 16 + 16)
                    ln(v, L_A1, xin, xn)
                    values_by_head(v, 0)
                    for t in range(NT):
                        v.wait("hb_ps", t + 1)
                        b = 4 if t % 2 == 0 else 2
                        src = bank(b, 2).rearrange("p (h n) -> p h n", n=NBK)
                        e = hb[:, t % 2, :].rearrange("p (h n) -> p h n", n=NBK)
                        done(dve.tensor_reduce(hbm[:, t % 2, :], src, AX.X, ALU.max), "hb_max")
                        v.wait("hb_max", t + 1)
                        done(dve.tensor_tensor(e, src, hbm[:, t % 2, :].unsqueeze(2).broadcast_to((P, 2 * H, NBK)),
                                               ALU.subtract), "hb_diff")
                        v.wait("hb_exp", t + 1)
                        done(dve.tensor_reduce(hbs[:, t % 2, :], e, AX.X, ALU.add), "hb_sum")
                        v.wait("hb_sum", t + 1)
                        done(dve.reciprocal(hbr[:, t % 2, :], hbs[:, t % 2, :]), "hb_rec")
                        v.wait("hbT_ps", t + 1)
                        done(dve.tensor_copy(hash_T[1][:, :, P * t:P * (t + 1)],
                                             bank(7).rearrange("p (i q) -> p i q", i=QUAD)), "kbT")
                    attention(v, 0, xin, xa)
                    ln(v, L_A2, xa, xn)
                    for u in range(NU):
                        s = slice(2 * u, 2 * u + 2)
                        v.wait("m2_ps", u + 1)
                        v.wait("xs", u + 1)
                        m = dve.tensor_tensor(xb[:, s, :], bank(4 + u)[:, 0:256].rearrange("p (t d) -> p t d", t=2),
                                              xsum[:, s, :], ALU.add)
                        if u == NU - 1:
                            m.then_inc(sem["x_free"], 1)
                            dve.wait_ge(sem["x_free"], it + 1)
                    ln(v, L_O1, xb, xa)
                if run(2):
                    for u in range(1):
                        chain(v, dve.tensor_tensor(xsum[:], xa[:], row("xbo").unsqueeze(1).broadcast_to((P, NT, D)), ALU.add))
                    v.wait("q_ps", 2)
                    done(dve.tensor_scalar(qT[:], bank(0), col("xbq"), 1.0 / SQ8, ALU.add, ALU.mult), "qT")
                    v.wait("k_ps", 2)
                    done(dve.tensor_scalar(kT[:], bank(1), col("xbk"), None, ALU.add), "kT")
                    values_by_head(v, 1)
                    attention(v, 1, None, xb, obias=True)
                    v.wait("res", 4)
                    ln(v, L_O2, xb, xa)
                if run(3):
                    v.wait("r_ps", 1)
                    r = [0]

                    def rstep(instruction):
                        done(instruction, "rv")
                        r[0] += 1
                        v.wait("rv", r[0])

                    l8 = bank(6)[:, 0:NT * E0].rearrange("p (t e) -> p t e", e=E0)
                    bc = lambda a, e: a.unsqueeze(2).broadcast_to((P, NT, e))
                    rstep(dve.tensor_tensor(oh[:], l8, row("r0").unsqueeze(1).broadcast_to((P, NT, E0)), ALU.add))
                    dve.tensor_reduce(lgm[:, :, 0], oh[:], AX.X, ALU.max).then_inc(sem["outer"], 1)
                    given["outer"] += 1
                    n_outer[0] += 1
                    v.wait("outer", n_outer[0])
                    rstep(dve.tensor_tensor(lg[:], oh[:], bc(lgm[:, :, 0], E0), ALU.subtract))
                    rstep(dve.tensor_scalar(oh[:], lg[:], 0.0, None, ALU.is_equal))
                    rstep(dve.tensor_tensor(oh[:], oh[:], falling0[:].unsqueeze(1).broadcast_to((P, NT, E0)), ALU.mult))
                    rstep(dve.tensor_reduce(lgm[:, :, 1], oh[:], AX.X, ALU.max))
                    v.wait("r_exp", 1)
                    rstep(dve.tensor_reduce(lgm[:, :, 2], le[:], AX.X, ALU.add))
                    rstep(dve.reciprocal(lgm[:, :, 3], lgm[:, :, 2]))
                    done(dve.tensor_tensor(oh2[:], oh[:], bc(lgm[:, :, 1], E0), ALU.is_equal), "onehot")
                    v.wait("onehot", 1)
                    rstep(dve.tensor_tensor(oh[:], oh2[:], bc(lgm[:, :, 3], E0), ALU.mult))
                    ln(v, L_F, xa, xn)
                    v.wait("ohT_ps", 1)
                    rstep(dve.tensor_copy(ohT[:], bank(7)[0:E0, :]))
                    done(dve.tensor_copy(ohTb[:], bank(7)[0:E0, :]), "ohT")
                    for e in range(E0):
                        v.wait("mask_ps", e + 1)
                        if e == 0:
                            v.wait("xT", 5)
                        done(dve.tensor_tensor(xe[:, e, :], bank(6 + e % 2), xT2[:], ALU.mult), "xe")
                    for t in range(NT):
                        v.wait("e2_ps", t + 1)
                        b = 4 if t % 2 == 0 else 0
                        w = oh[:, t, :].unsqueeze(2).broadcast_to((P, E0, D))
                        done(dve.tensor_tensor(prod[:, t % 2, :].rearrange("p (e d) -> p e d", e=E0),
                                               bank(b, 2).rearrange("p (e d) -> p e d", e=E0), w, ALU.mult), "e_prod")
                        v.wait("e_prod", t + 1)
                        done(dve.tensor_reduce(xsum[:, t, :], prod[:, t % 2, :].rearrange("p (e d) -> p d e", e=E0),
                                               AX.X, ALU.add), "e_sum")
                        bb = 2 if t % 2 == 0 else 6
                        chain(v, dve.scalar_tensor_tensor(ebias[:, t, :], bank(bb)[:, 0:D], lgm[:, t, 3:4],
                                                          xa[:, t, :], ALU.mult, ALU.add))
                        v.wait("e_sum", t + 1)
                        done(dve.tensor_tensor(xb[:, t, :], xsum[:, t, :], ebias[:, t, :], ALU.add), "e_out")
                    v.wait("e_out", NT)
                    ln(v, L_O3, xb, xa)
                if run(4):
                    chain(v, dve.tensor_tensor(xsum[:], xa[:], row("cbo").unsqueeze(1).broadcast_to((P, NT, D)), ALU.add))
                    v.wait("q_ps", 3)
                    done(dve.tensor_scalar(qT[:], bank(0), col("cbq"), 1.0 / SQ8, ALU.add, ALU.mult), "qT")
                    v.wait("k_ps", 3)
                    done(dve.tensor_scalar(kT[:], bank(1), col("cbk"), None, ALU.add), "kT")
                    values_by_head(v, 2)
                    attention(v, 2, None, xb, obias=True)
                    v.wait("res", 6)
                    ln(v, L_O4, xb, xa)
                if run(5):
                    for c in range(NCH):
                        v.wait("wk_ps", c + 1)
                        done(dve.tensor_copy(wkT[:, c, :], bank(1 + 2 * (c % 2))), "wk")
                    for t in range(NT):
                        v.wait("ws_ps", t + 1)
                        src = bank(2 * (t % 2), 2).rearrange("p (h q) -> p h q", q=S)
                        e = probs[:, t // 2, 2 * (t % 2):2 * (t % 2) + 2, :, :].rearrange("p a b (i q) -> p (a b i) q", q=S)
                        over = lambda a: a.unsqueeze(1).broadcast_to((P, H, S))
                        done(dve.tensor_reduce(wmax[:, t % 2, :], src.rearrange("p h q -> p q h"), AX.X, ALU.max), "w_max")
                        v.wait("w_max", t + 1)
                        done(dve.tensor_tensor(e, src, over(wmax[:, t % 2, :]), ALU.subtract), "w_diff")
                        v.wait("w_exp", t + 1)
                        done(dve.tensor_reduce(wsum[:, t % 2, :], e.rearrange("p h q -> p q h"), AX.X, ALU.add), "w_sum")
                        v.wait("w_sum", t + 1)
                        done(dve.reciprocal(wrec[:, t % 2, :], wsum[:, t % 2, :]), "w_rec")
                        v.wait("w_rec", t + 1)
                        done(dve.tensor_tensor(e, e, over(wrec[:, t % 2, :]), ALU.mult), "w_attn")
                    for u in range(NU):
                        s = slice(2 * u, 2 * u + 2)
                        v.wait("wo_ps", u + 1)
                        done(dve.tensor_tensor(xb[:, s, :], bank(6 + u)[:, 0:256].rearrange("p (t d) -> p t d", t=2),
                                               xa[:, s, :], ALU.add), "w_res")
                        v.wait("w_res", u + 1)
                    ln(v, L_X, xb, xn)
                    for u in range(NU):
                        s = slice(2 * u, 2 * u + 2)
                        v.wait("ln_out", 2 * L_X + u + 1)
                        done(dve.tensor_tensor(xn[:, s, :], xn[:, s, :],
                                               row("lnx_g").unsqueeze(1).broadcast_to((P, 2, D)), ALU.mult), "w_gain")
                        chain(v, dve.tensor_tensor(xsum[:, s, :], xa[:, s, :],
                                                   row("lnx_b").unsqueeze(1).broadcast_to((P, 2, D)), ALU.add))
                        v.wait("w_gain", u + 1)
                        done(dve.tensor_tensor(xb[:, s, :], xn[:, s, :], xsum[:, s, :], ALU.add), "w_x")
                        v.wait("w_x", u + 1)
                    ln(v, L_O5, xb, xa)
                if run(6):
                    v.wait("r6_ps", 1)
                    r6 = [0]

                    def r6step(instruction):
                        done(instruction, "r6v")
                        r6[0] += 1
                        v.wait("r6v", r6[0])

                    l4 = bank(6)[:, 0:NT * E1].rearrange("p (t e) -> p t e", e=E1)
                    g, o1, o2, ex = lg[:, :, 0:E1], oh[:, :, 0:E1], oh2[:, :, 0:E1], le[:, :, 0:E1]
                    fall = falling1[:].unsqueeze(1).broadcast_to((P, NT, E1))
                    chain(v, dve.tensor_tensor(o1, l4, row("r1").unsqueeze(1).broadcast_to((P, NT, E1)), ALU.add))
                    r6step(dve.tensor_reduce(lgm[:, :, 0], o1, AX.X, ALU.max))
                    r6step(dve.tensor_tensor(g, o1, bc(lgm[:, :, 0], E1), ALU.subtract))
                    r6step(dve.tensor_scalar(o1, g, 0.0, None, ALU.is_equal))
                    r6step(dve.tensor_tensor(o1, o1, fall, ALU.mult))
                    r6step(dve.tensor_reduce(lgm[:, :, 1], o1, AX.X, ALU.max))
                    r6step(dve.tensor_tensor(o2, o1, bc(lgm[:, :, 1], E1), ALU.is_equal))
                    r6step(dve.scalar_tensor_tensor(o1, o2, NEG, g, ALU.mult, ALU.add))
                    r6step(dve.tensor_reduce(lgm[:, :, 2], o1, AX.X, ALU.max))
                    r6step(dve.tensor_tensor(o1, o1, bc(lgm[:, :, 2], E1), ALU.is_equal))
                    r6step(dve.tensor_tensor(o1, o1, fall, ALU.mult))
                    r6step(dve.tensor_reduce(lgm[:, :, 3], o1, AX.X, ALU.max))
                    r6step(dve.tensor_tensor(o1, o1, bc(lgm[:, :, 3], E1), ALU.is_equal))
                    r6step(dve.tensor_tensor(o2, o2, o1, ALU.add))
                    v.wait("r6_exp", 1)
                    chain(v, dve.tensor_tensor(o2, o2, ex, ALU.mult))
                    chain(v, dve.tensor_reduce(lgm[:, :, 4], o2, AX.X, ALU.add))
                    r6step(dve.reciprocal(lgm[:, :, 5], lgm[:, :, 4]))
                    done(dve.tensor_tensor(o1, o2, bc(lgm[:, :, 5], E1), ALU.mult), "gw")
                    v.wait("gwT_ps", 1)
                    done(dve.tensor_copy(ohT[0:E1, :], bank(7)[0:E1, :]), "gwT")
                    for t in range(NT):
                        v.wait("g2_ps", t + 1)
                        b = 4 if t % 2 == 0 else 6
                        w = o1[:, t, :].unsqueeze(2).broadcast_to((P, E1, D))
                        done(dve.tensor_tensor(prod[:, t % 2, 0:512].rearrange("p (e d) -> p e d", e=E1),
                                               bank(b).rearrange("p (e d) -> p e d", e=E1), w, ALU.mult), "g_prod")
                        v.wait("g_prod", t + 1)
                        done(dve.tensor_reduce(xsum[:, t, :], prod[:, t % 2, 0:512].rearrange("p (e d) -> p d e", e=E1),
                                               AX.X, ALU.add), "g_sum")
                        chain(v, dve.tensor_tensor(ebias[:, t, :], bank(b + 1)[:, 0:D], xa[:, t, :], ALU.add))
                        v.wait("g_sum", t + 1)
                        done(dve.tensor_tensor(xb[:, t, :], xsum[:, t, :], ebias[:, t, :], ALU.add), "g_out")
                    v.wait("g_out", NT)
                    dve.wait_ge(sem["out_free"], it + 1)
                    ln(v, L_O6, xb, yout)
                    v.wait("ln_out", 20)
                    dve.sem_inc(sem["out_ready"], 1)
                else:
                    v.wait("ln_out", 2 * {1: L_O1, 2: L_O2, 3: L_O3, 4: L_O4, 5: L_O5}[last_stage] + 2)
                    dve.wait_ge(sem["out_free"], it + 1)
                    dve.tensor_copy(yout[:], xa[:]).then_inc(sem["out_ready"], 1)

        @block.tensor
        def _(pe):
            mm = nc.tensor.matmul
            pe.wait_ge(sem["weights"], 16 * NW)
            pe.wait_ge(sem["setup"], N_SETUP)
            nc.tensor.transpose(bank(0)[:, 0:127], emb[0:127, :], ident[0:127, 0:127]).then_inc(sem["setup_pe"], 1)
            pe.wait_ge(sem["setup_act"], 1)
            mm(bank(1)[0:H, 0:127], hmask[:], embT[:, 0:127], start=True, stop=True).then_inc(sem["setup_pe"], 1)
            pe.wait_ge(sem["setup_act"], 2)
            for s in range(S):
                m = nc.tensor.transpose(bank(2, 2)[0:S, H * s:H * (s + 1)], tabT[:, S - 1 - s:2 * S - 1 - s], ident[0:H, 0:H])
            m.then_inc(sem["setup_pe"], 1)

            def transpose_x(v, n, k, src, b):
                for t in range(NT):
                    if t % 2 == 0:
                        v.wait("ln_out", 2 * n + t // 2 + 1)
                    m = nc.tensor.transpose(bank(b)[:, P * t:P * (t + 1)], src[:, t, :], ident[:])
                done(m, "xT_ps")

            def project(v, c, kx, src_q, src_kv):
                mm(bank(0), wq[c][:], src_q, start=True, stop=True).then_inc(sem["q_ps"], 1)
                mm(bank(1), wk[c][:], src_kv, start=True, stop=True).then_inc(sem["k_ps"], 1)
                given["q_ps"] += 1
                given["k_ps"] += 1
                for b in range(NB):
                    for r in range(2):
                        m = mm(bank(2)[S * r:S * (r + 1), S * b:S * (b + 1)], src_kv[:, S * b:S * (b + 1)],
                               wv[c][:].rearrange("p (c r d) -> p r c d", r=2, d=DH)[:, r, :, :], start=True, stop=True)
                done(m, "v_ps")

            def attention(v, c):
                v.wait("qT", c + 1)
                v.wait("kexp", c + 1)
                v.wait("vbd", c + 1)
                for u in range(NU):
                    if u:
                        v.wait("sdiff" if c < 2 else "biased", 2 * c + u if c < 2 else u)
                    for t in range(2):
                        for bb in range(2):
                            b = 4 * u + 2 * t + bb
                            tok, q = slice(S * b, S * (b + 1)), slice(S * bb, S * (bb + 1))
                            if c == 0 and bb == 0:
                                v.wait("qbT", 2 * u + t + 1)
                                v.wait("kbT", 2 * u + t + 1)
                            for j in range(4):
                                r = slice(32 * j, 32 * (j + 1))
                                m = mm(quad[q, j, 256 * t:256 * (t + 1)], qT[r, tok], kexp[r, :, tok],
                                       start=True, stop=(c > 0))
                            if c == 0:
                                for i in range(QUAD):
                                    for j in range(4):
                                        r = slice(32 * j, 32 * (j + 1))
                                        at = 256 * t + S * i
                                        m = mm(quad[q, j, at:at + S], hash_T[0][r, i, tok], hash_T[1][r, i, tok],
                                               start=False, stop=(i == 3))
                    done(m, "scores")
                for u in range(NU):
                    for t in range(2 * u, 2 * u + 2):
                        v.wait("probs", 4 * c + t + 1)
                        if t:
                            v.wait("pT_a", 4 * c + t)
                            v.wait("pT_v", 4 * c + t)
                        for k in range(8):
                            j, i0 = k // 2, 2 * (k % 2)
                            m = nc.tensor.transpose(bank(4 + k // 4)[:, P * (k % 4):P * (k % 4 + 1)],
                                                    probs[:, u, j, t % 2, S * i0:S * (i0 + 2)], ident[:])
                        done(m, "pT_ps")
                        v.wait("pT_a", 4 * c + t + 1)
                        v.wait("pT_v", 4 * c + t + 1)
                        if t:
                            v.wait("attn", 4 * c + t)
                        for k in range(8):
                            m = mm(bank(6)[:, 36 * k:36 * (k + 1)], pT[:, t % 2, k, :], vbd[:, 2 * t:2 * t + 2, k, :],
                                   start=True, stop=True)
                        done(m, "pv_ps")
                    v.wait("attn", 4 * c + 2 * u + 2)
                    if u:
                        v.wait("res", 2 * c + u)
                    for t in range(2):
                        m = nc.tensor.transpose(bank(7)[:, P * t:P * (t + 1)], attn[:, 2 * u + t, :], ident[:])
                    done(m, "aT_ps")
                    v.wait("aT", 2 * c + u + 1)
                    for t in range(2):
                        k = 2 * u + t
                        m = mm(bank(7)[:, 256 + P * t:256 + P * (t + 1)], aT[:, P * k:P * (k + 1)], wo[c][:],
                               start=True, stop=True)
                    done(m, "o_ps")

            with pe.Fori(0, groups) as it:
                v = Values(pe, sem, it)
                if run(1):
                    pe.wait_ge(sem["setup_v"], 6)
                    transpose_x(v, L_A1, 1, xn, 4)
                    v.wait("xT", 1)
                    project(v, 0, 1, xT[:], xT[:])
                    v.wait("qT", 1)
                    v.wait("kT", 1)
                    for t in range(NT):
                        b = 4 if t % 2 == 0 else 2
                        if t == 1:
                            v.wait("vbd", 1)
                        if t >= 2:
                            v.wait("hb_diff", t - 1)
                        tok = slice(P * t, P * (t + 1))
                        mm(bank(b), qT[:, tok], whash[:, 0, :], start=True, stop=True)
                        done(mm(bank(b + 1), kT[:, tok], whash[:, 1, :], start=True, stop=True), "hb_ps")
                        if t >= 1:
                            v.wait("hb_norm", t)
                            if t >= 2:
                                v.wait("qbT", t - 1)
                                v.wait("kbT", t - 1)
                            for k in range(8):
                                m = nc.tensor.transpose(bank(6 + k // 4)[:, P * (k % 4):P * (k % 4 + 1)],
                                                        hb[:, (t - 1) % 2, P * k:P * (k + 1)], ident[:])
                            done(m, "hbT_ps")
                    v.wait("hb_norm", NT)
                    v.wait("qbT", NT - 1)
                    v.wait("kbT", NT - 1)
                    for k in range(8):
                        m = nc.tensor.transpose(bank(6 + k // 4)[:, P * (k % 4):P * (k % 4 + 1)],
                                                hb[:, (NT - 1) % 2, P * k:P * (k + 1)], ident[:])
                    done(m, "hbT_ps")
                    v.wait("hb_diff", NT)
                    attention(v, 0)
                    transpose_x(v, L_A2, 2, xn, 4)
                    v.wait("xT", 2)
                    for c in range(FC):
                        done(mm(bank(c), m_w1[:, P * c:P * (c + 1)], xT2[:], start=True, stop=True), "m_ps")
                    for u in range(NU):
                        for t in range(2):
                            k = 2 * u + t
                            for c in range(FC):
                                v.wait("m_h", c + 1)
                                m = mm(bank(4 + u)[:, P * t:P * (t + 1)], hT[:, c, P * k:P * (k + 1)], m_w2[:, c, :],
                                       start=(c == 0), stop=(c == FC - 1))
                        done(m, "m2_ps")
                if run(2):
                    transpose_x(v, L_O1, 3, xa, 4)
                    pe.wait_ge(sem["ctx_in"], it * 16 + 16)
                    v.wait("xT", 3)
                    project(v, 1, 3, xT[:], ctxT[:])
                    attention(v, 1)
                if run(3):
                    transpose_x(v, L_O2, 4, xa, 4)
                    v.wait("xT", 4)
                    for t in range(NT):
                        m = mm(bank(6)[:, E0 * t:E0 * (t + 1)], xT[:, P * t:P * (t + 1)], e_r[:], start=True, stop=True)
                    done(m, "r_ps")
                    transpose_x(v, L_F, 5, xn, 5)
                    v.wait("onehot", 1)
                    for t in range(NT):
                        m = nc.tensor.transpose(bank(7)[0:E0, P * t:P * (t + 1)], oh2[:, t, :], ident[:])
                    done(m, "ohT_ps")
                    v.wait("ohT", 1)
                    for e in range(E0):
                        if e >= 2:
                            v.wait("xe", e - 1)
                        done(mm(bank(6 + e % 2), pick[:, e, :], ohTb[:], start=True, stop=True), "mask_ps")
                    for c in range(FC):
                        f = slice(P * c, P * (c + 1))
                        mm(bank(c), e_b1[:, f], ohT[:], start=True, stop=False)
                        for e in range(E0):
                            v.wait("xe", e + 1)
                            m = mm(bank(c), e_w1[:, e, f], xe[:, e, :], start=False, stop=(e == E0 - 1))
                        done(m, "e_ps")
                    v.wait("e_h", FC)
                    for t in range(NT):
                        b, bb = (4, 2) if t % 2 == 0 else (0, 6)
                        if t >= 2:
                            v.wait("e_out", t - 1)
                        tok = slice(P * t, P * (t + 1))
                        for c in range(FC):
                            for n in range(2):
                                mm(bank(b + n), hT[:, c, tok],
                                   e_w2[:, c, 4 * n:4 * n + 4, :].rearrange("p e d -> p (e d)"),
                                   start=(c == 0), stop=(c == FC - 1))
                        done(mm(bank(bb)[:, 0:D], ohT[:, tok], e_b2[:], start=True, stop=True), "e2_ps")
                if run(4):
                    transpose_x(v, L_O3, 6, xa, 4)
                    v.wait("xT", 6)
                    project(v, 2, 6, xT[:], xT[:])
                    attention(v, 2)
                if run(5):
                    transpose_x(v, L_O4, 7, xa, 4)
                    v.wait("xT", 7)
                    for c in range(NCH):
                        f = slice(P * c, P * (c + 1))
                        if c >= 2:
                            v.wait("wq", c - 1)
                            v.wait("wk", c - 1)
                        done(mm(bank(2 * (c % 2)), ww[0][:, f], xT[:], start=True, stop=True), "wq_ps")
                        done(mm(bank(1 + 2 * (c % 2)), ww[1][:, f], ctxT[:], start=True, stop=True), "wk_ps")
                    for t in range(NT):
                        if t >= 2:
                            v.wait("wv", t - 1)
                        tok = slice(P * t, P * (t + 1))
                        for n in range(2):
                            m = mm(bank(4 + 2 * (t % 2) + n), ctxT[:, tok], ww[2][:, 512 * n:512 * (n + 1)],
                                   start=True, stop=True)
                        done(m, "wv_ps")
                    v.wait_apart(("wv", NT), ("wq", NCH), ("wk", NCH))

                    def wide_scores(t):
                        for bb in range(2):
                            tok = slice(P * t + S * bb, P * t + S * (bb + 1))
                            for c in range(NCH):
                                for r in range(2):
                                    d = slice(S * r, S * (r + 1))
                                    m = mm(bank(2 * (t % 2) + r)[S * bb:S * (bb + 1), S * c:S * (c + 1)],
                                           wkT[d, c, tok], wqT[d, c, tok], start=True, stop=True)
                        done(m, "ws_ps")

                    wide_scores(0)
                    for t in range(NT):
                        if t + 1 < NT:
                            if t >= 1:
                                v.wait_apart(("w_diff", t))
                            wide_scores(t + 1)
                        v.wait_apart(("w_attn", t + 1), *([("wc", t)] if t else []))
                        for c in range(NCH):
                            for r in range(2):
                                for bb in range(2):
                                    k = slice(S * bb, S * (bb + 1))
                                    e = probs[k, t // 2, 2 * (t % 2) + r, c // 4, S * (c % 4):S * (c % 4 + 1)]
                                    m = mm(bank(4 + bb)[S * r:S * (r + 1), S * c:S * (c + 1)],
                                           wvt[k, t, P * c + S * r:P * c + S * (r + 1)], e, start=True, stop=True)
                        done(m, "wc_ps")
                        if t % 2:
                            v.wait("wc", t + 1)
                            for n in range(2):
                                for c in range(NCH):
                                    m = mm(bank(6 + t // 2)[:, P * n:P * (n + 1)], pT[:, n, c, :], wwo[:, c, :],
                                           start=(c == 0), stop=(c == NCH - 1))
                            done(m, "wo_ps")
                    v.wait("w_res", 2)
                    pe.sem_inc(sem["ctx_free"], 1)
                if run(6):
                    transpose_x(v, L_O5, 8, xa, 4)
                    v.wait("xT", 8)
                    for t in range(NT):
                        m = mm(bank(6)[:, E1 * t:E1 * (t + 1)], xT[:, P * t:P * (t + 1)], g_r[:], start=True, stop=True)
                    done(m, "r6_ps")
                    for n in range(E1 * FC):
                        e, c = n // FC, n % FC
                        if n >= 4:
                            v.wait("g_h", n - 3)
                        done(mm(bank(n % 4), g_w1[:, e, P * c:P * (c + 1)], xT[:], start=True, stop=True), "g_ps")
                        if n == E1 * FC - 5:
                            v.wait("gw", 1)
                            for t in range(NT):
                                m = nc.tensor.transpose(bank(7)[0:E1, P * t:P * (t + 1)], oh[:, t, 0:E1], ident[:])
                            done(m, "gwT_ps")
                    v.wait("gwT", 1)
                    v.wait("g_h", E1 * FC)
                    for t in range(NT):
                        b = 4 if t % 2 == 0 else 6
                        if t >= 2:
                            v.wait("g_out", t - 1)
                        tok = slice(P * t, P * (t + 1))
                        for c in range(FC):
                            for e in range(E1):
                                mm(bank(b)[:, D * e:D * (e + 1)], gh[:, e * FC + c, tok], g_w2[:, c, e, :],
                                   start=(c == 0 and e == 0), stop=(c == FC - 1), skip_group_check=True)
                        done(mm(bank(b + 1)[:, 0:D], ohT[0:E1, tok], g_b2[:], start=True, stop=True), "g2_ps")

        if last_stage == 6:
            wrong = {n: given[n] for n, per in SIGNALS.items() if given[n] != per}
            assert not wrong, f"signals given another number of times a group: {wrong}"


def host_layout(x):
    import numpy as np

    a = {k: np.ascontiguousarray(v) for k, v in x.items()}
    r = {}
    r["x"] = a["x"].reshape(B * S, D)
    r["ctxT"] = a["ctx_1024"].reshape(B * S, D).T
    r["wq0"], r["wk0"], r["wv0"] = (a[f"L0_attn_W{n}"].reshape(D, D) for n in "qkv")
    r["wo0"] = a["L0_attn_Wo"].reshape(D, D)
    r["whq"], r["whk"] = (a[f"L0_attn_Wh{n}"].reshape(D, NBK) for n in "qk")
    r["m_w1"], r["m_w2"] = a["L0_attn_W1"], a["L0_attn_W2"]
    for n in "qkvo":
        r[f"w{n}1"] = a[f"L0_xattn_W{n}"].T
    r["e_r"], r["e_w1"], r["e_w2"] = a["L0_ffn_Wr"], a["L0_ffn_W1"], a["L0_ffn_W2"]
    r["e_b1"], r["e_b2"] = a["L0_ffn_b1"], a["L0_ffn_b2"]
    for i, n in enumerate("qkv"):
        r[f"w{n}2"] = a["L1_attn_qkv_w"][i * D:(i + 1) * D].T
    r["wo2"] = a["L1_attn_proj_w"].T
    r["emb"] = a["L1_attn_rel_pos_emb"][S:S + 127]
    for n in "qkvo":
        r[f"ww{n}"] = a[f"L1_xattn_W_{n.upper()}"]
    r["g_r"], r["g_w1"], r["g_w2"], r["g_b2"] = (a[f"L1_ffn_{n}"] for n in ("Wr", "W1", "W2", "b2"))
    qkv_b = a["L1_attn_qkv_b"].reshape(3, D)
    r["cols"] = np.stack([a["L0_attn_ln1_g"], a["L0_attn_ln1_b"], a["L0_attn_ln2_g"], a["L0_attn_ln2_b"],
                          *a["L0_attn_b1"].reshape(FC, P), a["L0_xattn_bq"], a["L0_xattn_bk"], a["L0_xattn_bv"],
                          a["L0_ffn_ln_g"], a["L0_ffn_ln_b"], *qkv_b, *a["L1_ffn_b1"].reshape(E1 * FC, P)], axis=1)
    r["rows"] = np.concatenate([a["L0_attn_b2"], a["L0_xattn_bo"], a["L1_attn_proj_b"], a["L1_xattn_ln_gamma"],
                                a["L1_xattn_ln_beta"], a["L0_ffn_br"], a["L1_ffn_br"]])[None, :]
    return {k: np.ascontiguousarray(v) for k, v in r.items()}


def kernel(**inputs):
    import concourse.bacc as _bacc
    from concourse import mybir as _mybir
    from concourse.bass_utils import run_bass_kernel_spmd as _run

    nc = _bacc.Bacc("TRN2", target_bir_lowering=False, num_devices=1)
    arrays, args = {}, {}
    for name, a in host_layout(inputs).items():
        arrays[f"in_{name}"] = a
        args[name] = nc.dram_tensor(f"in_{name}", a.shape, _mybir.dt.from_np(a.dtype), kind="ExternalInput").ap()
    out = nc.dram_tensor("out_0_dram", (B, S, D), _mybir.dt.float32, kind="ExternalOutput").ap()
    decoder_kernel(nc, args, out)
    r = _run(nc, [arrays], core_ids=[0])
    return r.results[0]["out_0_dram"]
```

```python
from contextlib import ExitStack

import concourse.bass as bass
from concourse import mybir

F32 = mybir.dt.float32
BF16 = mybir.dt.bfloat16
ALU = mybir.AluOpType
ACT = mybir.ActivationFunctionType
AX = mybir.AxisListType

P = 128
B, S, D = 128, 64, 128
GT = 512
NG = B * S // GT
NT = GT // P
NU = 2
UT = GT // NU
TU = NT // NU
NB = GT // S
BU = NB // NU
H, DH, QUAD = 16, 8, 4
NBK = 32
F = 512
FC = F // P
E0, E1 = 8, 4
DK = 64
NCH = H * DK // P
SQ8 = float(DH) ** 0.5
NEG = -1e30
N_SETUP = 14
N_SETUP_V = 8

COLS = ["ln1_g", "ln1_b", "ln2_g", "ln2_b", "mb0", "mb1", "mb2", "mb3", "xbq", "xbk", "xbv",
        "lnf_g", "lnf_b", "cbq", "cbk", "cbv"] + [f"fb{i}" for i in range(E1 * FC)]
COL = {n: i for i, n in enumerate(COLS)}
ROWS = {"mlp_b2": (0, P), "xbo": (P, P), "cbo": (2 * P, P), "lnx_g": (3 * P, P), "lnx_b": (4 * P, P),
        "r0": (5 * P, E0), "r1": (5 * P + E0, E1)}
NROW = 5 * P + E0 + E1

LN_EPS = [1e-6, 1e-6, 1e-5, 1e-5, 1e-5, 1e-5, 1e-5, 1e-5, 1e-5, 1e-5]
L_A1, L_A2, L_O1, L_O2, L_F, L_O3, L_O4, L_X, L_O5, L_O6 = range(10)


def attention_steps(c):
    return [("scores", c), ("softmax", c), ("probsT0", c), ("probsT1", c), ("pv", c), ("headsT", c), ("out", c)]


STAGES = [
    [("norm", L_A1), ("xT", L_A1), ("proj", 0), ("hash", 0), ("buckets", 0), ("hashT", 0), ("hashT", 1),
     *attention_steps(0), ("norm", L_A2), ("xT", L_A2), ("m_hidden", 0), ("m_out", 0), ("norm", L_O1), ("xT", L_O1)],
    [("proj", 1), *attention_steps(1), ("norm", L_O2), ("xT", L_O2)],
    [("route", 0), ("norm", L_F), ("choose", 0), ("xT", L_F), ("gateT", 0), ("masks", 0), ("e_hidden", 0),
     ("e_hidden", 1), ("e_hidden", 2), ("e_hidden", 3), ("e_out", 0), ("e_mix", 0), ("e_out", 1), ("e_mix", 1),
     ("norm", L_O3), ("xT", L_O3)],
    [("proj", 2), *attention_steps(2), ("norm", L_O4), ("xT", L_O4)],
    [("w_qk", 0), ("w_qk", 1), ("w_v", 0), ("w_scores", 0), ("w_softmax", 0), ("w_ctx", 0), ("w_ctx", 1),
     ("w_out", 0), ("norm", L_X), ("norm", L_O5), ("xT", L_O5)],
    [("route", 1), ("choose", 1), ("g_hidden", 0), ("g_hidden", 1), ("g_hidden", 2), ("g_hidden", 3), ("gateT", 1),
     ("g_out", 0), ("g_mix", 0), ("norm", L_O6)],
]
STEPS = [s for stage in STAGES for s in stage]
HEAD = 3
LAG = 3
MERGE = "0010110101001010101001010101011010101001101010110010100101100101100110110010010101101011010010101010101001010101011010100111010001101010110100101010101101"


SIGNALS = {
    "qk_ps": ("proj", 1), "v_ps": ("proj", 1), "qT": ("proj", 1), "kT": ("proj", 1), "kexp": ("proj", 1), "vbd": ("proj", 1),
    "scores": ("scores", 1), "biased": ("softmax", 2), "sdiff": ("softmax", 2), "probs": ("softmax", 2),
    "pT0_ps": ("probsT0", 1), "pT0_a": ("probsT0", 1), "pT0_v": ("probsT0", 1), "pT1_ps": ("probsT1", 1), "pT1_a": ("probsT1", 1), "pT1_v": ("probsT1", 1),
    "pv_ps": ("pv", 2), "attn": ("pv", 2), "aT_ps": ("headsT", 1), "aT": ("headsT", 1), "o_ps": ("out", 1), "res": ("out", 1),
    "hb_ps": ("hash", 2), "hb_diff": ("buckets", 2), "hb_exp": ("buckets", 2), "hb_rec": ("buckets", 2), "hb_norm": ("buckets", 2),
    "hbT_ps": ("hashT", 1), "qbT": ("hashT", 1), "kbT": ("hashT", 1),
    "m_ps": ("m_hidden", 2), "m_h": ("m_hidden", 4), "m2_ps": ("m_out", 1), "xs_part": ("out", 1), "xs": ("out", 1),
    "r_ps": ("route", 1), "r_diff": ("choose", 1), "r_exp": ("choose", 1), "gates": ("choose", 1), "gateT_ps": ("gateT", 1), "gateT": ("gateT", 1),
    "mask_ps": ("masks", 4), "xe": ("masks", 4), "e_ps": ("e_hidden", 1), "e_h": ("e_hidden", 1), "e2_ps": ("e_out", 1), "e_prod": ("e_mix", 1),
    "wq_ps": ("w_qk", 2), "wk_ps": ("w_qk", 2), "wq": ("w_qk", 2), "wk": ("w_qk", 2),
    "wv_a_ps": ("w_v", 2), "wv_v_ps": ("w_v", 2), "wv_a": ("w_v", 2), "wv_v": ("w_v", 2),
    "ws_ps": ("w_scores", 2), "w_diff": ("w_softmax", 2), "w_exp": ("w_softmax", 2), "w_attn": ("w_softmax", 2),
    "wc_ps": ("w_ctx", 1), "wc_a": ("w_ctx", 1), "wc_v": ("w_ctx", 1), "wo_ps": ("w_out", 1),
    "g_ps": ("g_hidden", 2), "g_h": ("g_hidden", 4), "g2_ps": ("g_out", 1), "g_prod": ("g_mix", 2),
}
UNIT_SIGNALS = {
    "step": 98, "ln_mv": 10, "ln_log": 10, "ln_guess": 10, "ln_out": 10, "xT_ps": 8, "xT": 8,
}
XT_OF = {L_A1: 1, L_A2: 2, L_O1: 3, L_O2: 4, L_F: 5, L_O3: 6, L_O4: 7, L_O5: 8}
DMA_SIGNALS = ("x_in", "ctx_in", "out_done", "weights0", "weights", "bias_dup")
OTHER = ("setup", "setup_pe", "setup_v", "setup_act", "x_free", "ctx_free", "out_ready", "out_free", "apart")


def order():
    n, lag = len(STEPS), LAG + HEAD
    merge = MERGE or "0" * LAG + "01" * (n - LAG) + "1" * LAG
    at = [HEAD, 0]
    for u in map(int, merge):
        yield (*STEPS[at[u] % n], u, at[u] // n)
        at[u] += 1


BODY = [0]
FIRST = [(*s, 0, 0) for s in STEPS[:HEAD]]


def giving_steps(name):
    kind, count = SIGNALS[name]
    ahead = [x for x in BODY if x[3]] + [x for x in BODY if not x[3]]
    return [(i, u) for s, i, u, _ in ahead if s == kind and (name != "biased" or i == 2)
            and (kind != "out" or name in ("o_ps", "res") or i == 0)], count


class Values:

    def __init__(self, eng, sems, it, ahead=0):
        self.eng, self.sems, self.it, self.ahead = eng, sems, it, ahead
        self.base = {}

    def group(self, per):
        if isinstance(self.it, int):
            return (self.it + self.ahead) * per
        if per not in self.base:
            self.base[per] = self.eng.snap(self.it * per + self.ahead * per)
        return self.base[per]

    def wait(self, name, u, c=0, k=None):
        steps, count = giving_steps(name)
        k = count if k is None else k
        assert 1 <= k <= count, (name, c, k)
        self.eng.wait_ge(self.sems[name], self.group(len(steps) * count) + steps.index((c, u)) * count + k)

    def wait_own(self, name, u, k):
        assert 1 <= k <= UNIT_SIGNALS[name], (name, k)
        self.eng.wait_ge(self.sems[name, u], self.group(UNIT_SIGNALS[name]) + k)

    def apart(self):
        self.eng.sem_inc(self.sems["apart"], 1)


def decoder_kernel(nc, A, out, groups=NG):
    BODY[:] = list(order())
    LAST = list(x for x in BODY if not x[3])
    ctx = ExitStack()
    with ctx:
        def sb(name, shape, dt=F32):
            return ctx.enter_context(nc.sbuf_tensor(name, shape, dt))

        sem = {n: ctx.enter_context(nc.semaphore(n)) for n in (*SIGNALS, *DMA_SIGNALS, *OTHER)}
        for n in UNIT_SIGNALS:
            for u in range(NU):
                sem[n, u] = ctx.enter_context(nc.semaphore(f"{n}_{u}"))
        given = {n: [] for n in sem}

        wq = [sb(f"wq{c}", [P, P]) for c in range(3)]
        wk = [sb(f"wk{c}", [P, P]) for c in range(3)]
        wv = [sb(f"wv{c}", [P, P]) for c in range(3)]
        wo = [sb(f"wo{c}", [P, P]) for c in range(3)]
        whash_raw = sb("whash_raw", [P, 2, NBK])
        whash = sb("whash", [P, 2, H * NBK])
        m_w1, m_w2 = sb("m_w1", [P, F]), sb("m_w2", [P, FC, P])
        e_w1, e_w2 = sb("e_w1", [P, E0, F]), sb("e_w2", [P, FC, E0, P])
        e_b1, e_b2, e_r = sb("e_b1", [E0, F]), sb("e_b2", [E0, P]), sb("e_r", [P, E0])
        ww = [sb(f"ww{n}", [P, H * DK]) for n in "qkv"]
        wwo = sb("wwo", [P, NCH, P])
        g_w1, g_w2 = sb("g_w1", [P, E1, F]), sb("g_w2", [P, FC, E1, P])
        g_b2, g_r = sb("g_b2", [E1, P]), sb("g_r", [P, E1])
        cols = sb("cols", [P, len(COLS)])
        rows = sb("rows", [P, NROW])

        ident = sb("ident", [P, P])
        hmask = sb("hmask", [P, H])
        qmask = sb("qmask", [P, QUAD])
        pick = sb("pick", [E0, E0, P], BF16)
        falling = [sb("falling0", [P, E0]), sb("falling1", [P, E1])]
        epsc = sb("epsc", [P, 2])
        bias = sb("bias", [P, H, S])

        xin = sb("xin", [P, NT, D])
        xa, xb = sb("xa", [P, NT, D]), sb("xb", [P, NT, D])
        xsum = sb("xsum", [P, NT, D])
        xn = sb("xn", [P, NT, D])
        yout = sb("yout", [P, NT, D])
        xT, ctxT = sb("xT", [P, GT]), sb("ctxT", [P, GT])
        qT, kT = sb("qT", [P, GT]), sb("kT", [P, GT])
        vbd = sb("vbd", [P, NB, H // 2, 2 * (DH + 1)])
        attn, aT = sb("attn", [P, NT, D]), sb("aT", [P, GT])
        probs = sb("probs", [P, NU, QUAD, TU, QUAD * S])
        pT = sb("pT", [P, NT, H // 2, P])
        smax = sb("smax", [P, NT, H])
        rden = sb("rden", [P, NT, H // 2, 2])
        stats, mv = sb("stats", [P, NT, 6]), sb("mv", [P, NT, 2])
        lnlog, rstd = sb("lnlog", [P, NT]), sb("rstd", [P, NT, 4])
        hbm, hbs, hbr = sb("hbm", [P, NT, 2 * H]), sb("hbs", [P, NT, 2 * H]), sb("hbr", [P, NT, 2 * H])
        wmax, wrec = sb("wmax", [P, NT, S]), sb("wrec", [P, NT, S])
        lg, lgm = sb("lg", [P, NT, E0]), sb("lgm", [P, NT, 8])
        le, oh, oh2 = sb("le", [P, NT, E0]), sb("oh", [P, NT, E0]), sb("oh2", [P, NT, E0])
        gateT, gateTb = sb("gateT", [E0, GT]), sb("gateTb", [E0, GT], BF16)

        big = [sb(f"big{u}", [P, 4096]) for u in range(NU)]
        small = [sb(f"small{u}", [P, 2048]) for u in range(NU)]
        part = lambda buf, a, b, pattern, **k: [t[:, a:b].rearrange(pattern, **k) for t in buf]
        hb = part(big, 0, 2048, "p (s f) -> p s f", s=TU)
        hash_T = [part(big, 2048 + 1024 * n, 3072 + 1024 * n, "p (i t) -> p i t", i=QUAD) for n in range(2)]
        xe = part(big, 0, 2048, "p (e t) -> p e t", e=E0)
        wqT = part(big, 0, 2048, "p (c t) -> p c t", c=NCH)
        wkT = part(big, 2048, 4096, "p (c t) -> p c t", c=NCH)
        gh = part(big, 0, 4096, "p (c t) -> p c t", c=E1 * FC)
        kexp = part(small, 0, 1024, "p (i t) -> p i t", i=QUAD)
        hT = part(small, 1024, 2048, "p (c t) -> p c t", c=FC)
        wvt = part(small, 0, 2048, "p (t f) -> p t f", t=TU)
        prod = [probs[:, u].rearrange("p j t f -> p (j t f)").rearrange("p (s f) -> p s f", s=TU) for u in range(NU)]
        emb, embT, tabT = big[0][:, 0:P], big[0][:, P:2 * P], big[0][0:H, 2 * P:3 * P]

        ps = ctx.enter_context(nc.psum_tensor("ps", [P, 8, 512], F32))
        flat = ps[:, :, :].rearrange("p a b -> p (a b)")

        def bank(b, n=1):
            return flat[:, 512 * b:512 * (b + n)]

        quad = ps[:, 0:4, :]

        def own(u, n):
            return bank(4 + 2 * u + n)

        def col(name):
            return cols[:, COL[name]:COL[name] + 1]

        def row(name):
            return rows[:, ROWS[name][0]:ROWS[name][0] + ROWS[name][1]]

        def tiles(u):
            return slice(TU * u, TU * (u + 1))

        def tokens(u):
            return slice(UT * u, UT * (u + 1))

        def tile_tokens(u, t):
            return slice(UT * u + P * t, UT * u + P * (t + 1))

        def over_tiles(r, width):
            return r.unsqueeze(1).broadcast_to((P, TU, width))

        def last(a, n):
            return a.unsqueeze(2).broadcast_to((P, TU, n))

        def done(instruction, name, u, c=0):
            given[name].append((c, u))
            instruction.then_inc(sem[name], 1)

        def done_own(instruction, name, u):
            given[name, u].append(0)
            instruction.then_inc(sem[name, u], 1)

        block = ctx.enter_context(nc.Block())

        x_v = A["x"].rearrange("(g t p) d -> g p t d", t=NT, p=P)
        c_v = A["ctxT"].rearrange("p (g t) -> g p t", t=GT)
        o_v = out.rearrange("b s d -> (b s) d").rearrange("(g t p) d -> g p t d", t=NT, p=P)
        loads0 = [
            (cols[:], A["cols"]), (emb[0:127, :], A["emb"]), (wq[0][:], A["wq0"]), (wk[0][:], A["wk0"]),
            (wv[0][:], A["wv0"]), (whash_raw[:, 0, :], A["whq"]), (whash_raw[:, 1, :], A["whk"]),
            (wo[0][:], A["wo0"]), (rows[:], A["rows"].to_broadcast((P, NROW))),
            (m_w1[:], A["m_w1"]), (m_w2[:], A["m_w2"].rearrange("(c p) d -> p c d", p=P)),
        ]
        loads = [
            (wq[1][:], A["wq1"]), (wk[1][:], A["wk1"]), (wv[1][:], A["wv1"]), (wo[1][:], A["wo1"]),
            (e_r[:], A["e_r"]), (e_w1[:], A["e_w1"].rearrange("e d f -> d e f")),
            (e_b1[:], A["e_b1"]), (e_b2[:], A["e_b2"]),
        ] + [(e_w2[:, c, :, :], A["e_w2"][:, c * P:(c + 1) * P, :].rearrange("e p d -> p e d"))
             for c in range(FC)] + [
            (wq[2][:], A["wq2"]), (wk[2][:], A["wk2"]), (wv[2][:], A["wv2"]), (wo[2][:], A["wo2"]),
            (ww[0][:], A["wwq"]), (ww[1][:], A["wwk"]), (ww[2][:], A["wwv"]),
            (wwo[:], A["wwo"].rearrange("(c p) d -> p c d", p=P)),
            (g_r[:], A["g_r"]), (g_w1[:], A["g_w1"].rearrange("e d f -> d e f")), (g_b2[:], A["g_b2"]),
        ] + [(g_w2[:, c, :, :], A["g_w2"][:, c * P:(c + 1) * P, :].rearrange("e p d -> p e d"))
             for c in range(FC)]
        W0, W1 = 16 * len(loads0), 16 * len(loads)

        @block.sync
        def _(sp):
            sp.dma_start(xin[:], x_v[0]).then_inc(sem["x_in"], 16)
            for dst, src in loads0:
                sp.dma_start(dst, src).then_inc(sem["weights0"], 16)
            sp.dma_start(ctxT[:], c_v[0]).then_inc(sem["ctx_in"], 16)
            for dst, src in loads:
                sp.dma_start(dst, src).then_inc(sem["weights"], 16)
            sp.wait_ge(sem["setup_v"], N_SETUP_V)
            sp.dma_start(bias[S:P, :, :], bias[0:S, :, :]).then_inc(sem["bias_dup"], 16)
            if groups > 1:
                with sp.Fori(0, groups - 1) as it:
                    sp.wait_ge(sem["x_free"], it + 1)
                    sp.dma_start(xin[:], x_v[it + 1]).then_inc(sem["x_in"], 16)
                    sp.wait_ge(sem["ctx_free"], it + 1)
                    sp.dma_start(ctxT[:], c_v[it + 1]).then_inc(sem["ctx_in"], 16)
                    sp.wait_ge(sem["out_ready"], it + 1)
                    sp.dma_start(o_v[it], yout[:]).then_inc(sem["out_done"], 16)
                    sp.wait_ge(sem["out_done"], (it + 1) * 16)
                    sp.sem_inc(sem["out_free"], 1)
            sp.wait_ge(sem["out_ready"], groups)
            sp.dma_start(o_v[groups - 1], yout[:]).then_inc(sem["out_done"], 16)
            sp.wait_ge(sem["out_done"], groups * 16)

        @block.gpsimd
        def _(pool):
            n = [0]

            def link(instruction):
                n[0] += 1
                instruction.then_inc(sem["setup"], 1)
                pool.wait_ge(sem["setup"], n[0])

            link(pool.memset(ident[:], 0.0))
            link(pool.affine_select(ident[:], ident[:], [[-1, P]], ALU.not_equal, 1.0, base=0, channel_multiplier=1))
            link(pool.memset(hmask[:], 1.0))
            link(pool.affine_select(hmask[:], hmask[:], [[-DH, H]], ALU.is_ge, 0.0, base=0, channel_multiplier=1))
            link(pool.affine_select(hmask[:], hmask[:], [[DH, H]], ALU.is_ge, 0.0, base=DH - 1, channel_multiplier=-1))
            link(pool.memset(pick[:], 0.0))
            link(pool.affine_select(pick[:], pick[:], [[-1, E0], [0, P]], ALU.not_equal, 1.0, base=0, channel_multiplier=1))
            for f, e in zip(falling, (E0, E1)):
                link(pool.iota(f[:], [[-1, e]], base=e, channel_multiplier=0, allow_small_or_imprecise_dtypes=True))
            link(pool.memset(vbd[:], 0.0))
            link(pool.memset(vbd[0:S, :, :, DH:DH + 1], 1.0))
            link(pool.memset(vbd[S:P, :, :, 2 * DH + 1:2 * DH + 2], 1.0))
            link(pool.memset(epsc[:, 0:1], 1e-6))
            link(pool.memset(epsc[:, 1:2], 1e-5))
            assert n[0] == N_SETUP
            pool.wait_ge(sem["setup_v"], N_SETUP_V - 1)
            pool.affine_select(bias[0:S], bias[0:S], [[0, H], [-1, S]], ALU.is_ge, NEG, base=0,
                               channel_multiplier=1).then_inc(sem["setup_v"], 1)
            pool.sem_inc(sem["out_free"], 1)

            def step(v, s, i, u):
                if s == "proj":
                    v.wait("kT", u, i)
                    done(pool.tensor_tensor(kexp[u], kT[:, tokens(u)].unsqueeze(1).broadcast_to((P, QUAD, UT)),
                                            qmask[:].unsqueeze(2).broadcast_to((P, QUAD, UT)), ALU.mult),
                         "kexp", u, i)
                if s == "buckets":
                    for t in range(TU):
                        v.wait("hb_rec", u, 0, t + 1)
                        e = hb[u][:, t, :].rearrange("p (h n) -> p h n", n=NBK)
                        done(pool.tensor_tensor(e, e, hbr[:, TU * u + t, :].unsqueeze(2).broadcast_to((P, 2 * H, NBK)),
                                                ALU.mult), "hb_norm", u)
                if s == "out" and i == 0:
                    v.wait("res", u, 0)
                    x = xsum[:, tiles(u), :]
                    done(pool.tensor_tensor(x, xin[:, tiles(u), :], xa[:, tiles(u), :], ALU.add), "xs_part", u)
                    v.wait("xs_part", u)
                    done(pool.tensor_tensor(x, x, over_tiles(row("mlp_b2"), D), ALU.add), "xs", u)

            for s, i, u, _ in FIRST:
                step(Values(pool, sem, 0), s, i, u)
            if groups > 1:
                with pool.Fori(0, groups - 1) as it:
                    now, following = Values(pool, sem, it), Values(pool, sem, it, 1)
                    for s, i, u, ahead in BODY:
                        step(following if ahead else now, s, i, u)
            for s, i, u, _ in LAST:
                step(Values(pool, sem, groups - 1), s, i, u)

        @block.scalar
        def _(act):
            activate = nc.scalar.activation
            act.wait_ge(sem["setup_pe"], 1)
            activate(embT[:, 0:127], bank(0)[:, 0:127], ACT.Copy).then_inc(sem["setup_act"], 1)
            act.wait_ge(sem["setup_pe"], 2)
            activate(tabT[:, 0:127], bank(1)[0:H, 0:127], ACT.Copy).then_inc(sem["setup_act"], 1)

            def step(v, s, i, u):
                tok = tokens(u)
                if s == "norm":
                    t = tiles(u)
                    v.wait_own("ln_mv", u, i + 1)
                    eps = epsc[:, 0:1] if LN_EPS[i] == 1e-6 else epsc[:, 1:2]
                    done_own(activate(lnlog[:, t], mv[:, t, 1], ACT.Ln, bias=eps), "ln_log", u)
                    v.wait_own("ln_log", u, i + 1)
                    done_own(activate(rstd[:, t, 0], lnlog[:, t], ACT.Exp, scale=-0.5), "ln_guess", u)
                if s == "xT":
                    v.wait_own("xT_ps", u, XT_OF[i])
                    gain = {L_A1: "ln1", L_A2: "ln2", L_F: "lnf"}.get(i)
                    src = own(u, 0)[:, 0:UT]
                    if gain:
                        x = activate(xT[:, tok], src, ACT.Identity, scale=col(gain + "_g"), bias=col(gain + "_b"))
                    else:
                        x = activate(xT[:, tok], src, ACT.Copy)
                    done_own(x, "xT", u)
                if s == "proj":
                    v.wait("qk_ps", u, i)
                    bq, bk = {0: (None, None), 1: ("xbq", "xbk"), 2: ("cbq", "cbk")}[i]
                    if i == 0:
                        done(activate(kT[:, tok], own(u, 0)[:, UT:], ACT.Copy), "kT", u, i)
                        done(activate(qT[:, tok], own(u, 0)[:, 0:UT], ACT.Copy, scale=1.0 / SQ8), "qT", u, i)
                    else:
                        done(activate(kT[:, tok], own(u, 0)[:, UT:], ACT.Identity, bias=col(bk)), "kT", u, i)
                        done(activate(qT[:, tok], own(u, 0)[:, 0:UT], ACT.Identity, scale=1.0 / SQ8, bias=col(bq)),
                             "qT", u, i)
                if s == "buckets":
                    for t in range(TU):
                        v.wait("hb_diff", u, 0, t + 1)
                        e = hb[u][:, t, :]
                        activate(e[:, 0:512], e[:, 0:512], ACT.Exp, scale=SQ8)
                        done(activate(e[:, 512:1024], e[:, 512:1024], ACT.Exp), "hb_exp", u)
                if s == "hashT":
                    v.wait("hbT_ps", u, i)
                    done(activate(hash_T[0][u][:, :, P * i:P * (i + 1)], own(u, 0).rearrange("p (i q) -> p i q", i=QUAD),
                                  ACT.Copy, scale=0.1), "qbT", u, i)
                if s == "softmax":
                    for t in range(TU):
                        v.wait("sdiff", u, i, t + 1)
                        p = probs[:, u, :, t, :]
                        done(activate(p, p, ACT.Exp), "probs", u, i)
                if s in ("probsT0", "probsT1"):
                    t = int(s[-1])
                    v.wait(f"pT{t}_ps", u, i)
                    done(activate(pT[:, TU * u + t, 0:4, :].rearrange("p c q -> p (c q)"), own(u, 0), ACT.Copy),
                         f"pT{t}_a", u, i)
                if s == "headsT":
                    v.wait("aT_ps", u, i)
                    src = own(u, 0)[:, 0:UT]
                    if i == 0:
                        a = activate(aT[:, tok], src, ACT.Copy)
                    else:
                        a = activate(aT[:, tok], src, ACT.Identity, bias=col({1: "xbv", 2: "cbv"}[i]))
                    done(a, "aT", u, i)
                if s == "m_hidden":
                    for c in range(FC):
                        if c % 2 == 0:
                            v.wait("m_ps", u, 0, c // 2 + 1)
                        done(activate(hT[u][:, c, :], own(u, c // 2)[:, UT * (c % 2):UT * (c % 2 + 1)], ACT.Relu,
                                      bias=col(f"mb{c}")), "m_h", u)
                if s == "choose":
                    v.wait("r_diff", u, i)
                    e = (E0, E1)[i]
                    done(activate(le[:, tiles(u), 0:e], lg[:, tiles(u), 0:e], ACT.Exp), "r_exp", u, i)
                if s == "e_hidden":
                    v.wait("e_ps", u, i)
                    done(activate(hT[u][:, i, :], own(u, i % 2)[:, UT * (i // 2):UT * (i // 2 + 1)], ACT.Relu),
                         "e_h", u, i)
                if s == "w_qk":
                    for c in range(2):
                        v.wait("wq_ps", u, i, c + 1)
                        k = 4 * i + 2 * c
                        done(activate(wqT[u][:, k:k + 2, :].rearrange("p c t -> p (c t)"), own(u, 0), ACT.Copy,
                                      scale=DK ** -0.5), "wq", u, i)
                if s == "w_v":
                    for t in range(TU):
                        v.wait("wv_a_ps", u, 0, t + 1)
                        done(activate(wvt[u][:, t, 0:512], own(u, 0), ACT.Copy), "wv_a", u)
                if s == "w_softmax":
                    for t in range(TU):
                        v.wait("w_diff", u, 0, t + 1)
                        done(activate(prod[u][:, t, :], prod[u][:, t, :], ACT.Exp), "w_exp", u)
                if s == "w_ctx":
                    v.wait("wc_ps", u, i)
                    done(activate(pT[:, TU * u + i, :, 0:S], own(u, 0).rearrange("p (c q) -> p c q", c=NCH), ACT.Copy),
                         "wc_a", u, i)
                if s == "g_hidden":
                    for n in range(4 * i, 4 * i + 4):
                        if n % 2 == 0:
                            v.wait("g_ps", u, i, n % 4 // 2 + 1)
                        b = own(u, n // 2 % 2)[:, UT * (n % 2):UT * (n % 2 + 1)]
                        done(activate(gh[u][:, n, :], b, ACT.Gelu, bias=col(f"fb{n}")), "g_h", u, i)
                    if i == 3:
                        act.preload_act_table_set(TABLES)

            act.wait_ge(sem["weights0"], W0)
            act.wait_ge(sem["setup"], N_SETUP)
            act.wait_ge(sem["setup_v"], N_SETUP_V)
            TABLES = "natural_log_exp_and_others"
            act.preload_act_table_set(TABLES)
            for s, i, u, _ in FIRST:
                step(Values(act, sem, 0), s, i, u)
            if groups > 1:
                with act.Fori(0, groups - 1) as it:
                    now, following = Values(act, sem, it), Values(act, sem, it, 1)
                    for s, i, u, ahead in BODY:
                        step(following if ahead else now, s, i, u)
            for s, i, u, _ in LAST:
                step(Values(act, sem, groups - 1), s, i, u)

        @block.vector
        def _(dve):
            dve.wait_ge(sem["setup"], N_SETUP)
            dve.tensor_reduce(qmask[:], hmask[:].rearrange("p (j i) -> p i j", i=QUAD), AX.X, ALU.add)\
               .then_inc(sem["setup_v"], 1)
            dve.wait_ge(sem["weights0"], W0)
            for n in range(2):
                for i in range(QUAD):
                    m = dve.tensor_tensor(
                        whash[:, n, i * P:(i + 1) * P].rearrange("p (j n) -> p j n", n=NBK),
                        whash_raw[:, n, :].unsqueeze(1).broadcast_to((P, QUAD, NBK)),
                        hmask[:].rearrange("p (j i) -> p i j", i=QUAD)[:, i, :].unsqueeze(2).broadcast_to((P, QUAD, NBK)),
                        ALU.mult)
                m.then_inc(sem["setup_v"], 1)
            dve.memset(rstd[:], 0.0).then_inc(sem["setup_v"], 1)
            for name in ("xbq", "cbq"):
                dve.tensor_scalar(col(name), col(name), 1.0 / SQ8, None, ALU.mult).then_inc(sem["setup_v"], 1)
            dve.wait_ge(sem["setup_pe"], 3)
            dve.tensor_copy(bias[0:S], bank(2, 2)[0:S, 0:S * H].rearrange("p (s h) -> p h s", h=H))\
               .then_inc(sem["setup_v"], 1)

            n_step = [0] * NU

            def follow(v, u, instruction):
                done_own(instruction, "step", u)
                n_step[u] += 1
                v.wait_own("step", u, n_step[u])

            def norm(v, n, u, src, dst):
                ts, eps = tiles(u), LN_EPS[n]
                for t in range(TU * u, TU * (u + 1)):
                    m = dve.bn_stats(stats[:, t, :], src[:, t, :])
                follow(v, u, m)
                v.apart()
                for t in range(TU * u, TU * (u + 1)):
                    m = dve.bn_aggr(mv[:, t, :], stats[:, t, :])
                done_own(m, "ln_mv", u)
                v.wait_own("ln_guess", u, n + 1)
                y, a, b, r = (rstd[:, ts, k] for k in range(4))
                follow(v, u, dve.scalar_tensor_tensor(a, mv[:, ts, 1], eps, y, ALU.add, ALU.mult))
                follow(v, u, dve.scalar_tensor_tensor(b, a, -0.5, y, ALU.mult, ALU.mult))
                follow(v, u, dve.scalar_tensor_tensor(r, b, 1.5, y, ALU.add, ALU.mult))
                for t in range(TU * u, TU * (u + 1)):
                    m = dve.tensor_scalar(dst[:, t, :], src[:, t, :], mv[:, t, 0:1], rstd[:, t, 3:4],
                                          ALU.subtract, ALU.mult)
                done_own(m, "ln_out", u)

            NORMS = {L_A1: (xin, xn), L_A2: (xa, xn), L_O1: (xb, xa), L_O2: (xb, xa), L_F: (xa, xn),
                     L_O3: (xb, xa), L_O4: (xb, xa), L_X: (xb, xn), L_O5: (xb, xa), L_O6: (xb, yout)}

            def step(v, s, i, u):
                ts = tiles(u)
                if (s, i) == STEPS[0]:
                    n_step[u] = 0
                if s == "norm":
                    if i == L_A1 and u == 0:
                        dve.wait_ge(sem["x_in"], v.group(16) + 16)
                    if i == L_O6 and u == 0:
                        dve.wait_ge(sem["out_free"], v.group(1) + 1)
                    if i == L_F:
                        v.wait_own("ln_out", u, L_O2 + 1)
                    norm(v, i, u, *NORMS[i])
                    if i in (L_O1, L_O3):
                        v.wait_own("ln_out", u, i + 1)
                        follow(v, u, dve.tensor_tensor(xsum[:, ts, :], xa[:, ts, :],
                                                       over_tiles(row("xbo" if i == L_O1 else "cbo"), D), ALU.add))
                    if i == L_X:
                        v.wait_own("ln_out", u, i + 1)
                        dve.tensor_tensor(xn[:, ts, :], xn[:, ts, :], over_tiles(row("lnx_g"), D), ALU.mult)
                        follow(v, u, dve.tensor_tensor(xsum[:, ts, :], xa[:, ts, :], over_tiles(row("lnx_b"), D), ALU.add))
                        follow(v, u, dve.tensor_tensor(xb[:, ts, :], xn[:, ts, :], xsum[:, ts, :], ALU.add))
                    if i == L_O6:
                        v.wait_own("ln_out", u, i + 1)
                        if u == NU - 1:
                            dve.sem_inc(sem["out_ready"], 1)
                if s == "proj":
                    v.wait("v_ps", u, i)
                    for r in range(2):
                        half = slice(S * r, S * (r + 1))
                        m = dve.tensor_copy(vbd[half, BU * u:BU * (u + 1), :, (DH + 1) * r:(DH + 1) * r + DH],
                                            own(u, 1)[half, 0:UT].rearrange("p (b c d) -> p b c d", b=BU, d=DH))
                    done(m, "vbd", u, i)
                if s == "buckets":
                    view = lambda t: hb[u][:, t, :].rearrange("p (h n) -> p h n", n=NBK)
                    for t in range(TU):
                        v.wait("hb_ps", u, 0, t + 1)
                        src = bank(2 * t, 2).rearrange("p (h n) -> p h n", n=NBK)
                        m = hbm[:, TU * u + t, :]
                        follow(v, u, dve.tensor_reduce(m, src, AX.X, ALU.max))
                        done(dve.tensor_tensor(view(t), src, m.unsqueeze(2).broadcast_to((P, 2 * H, NBK)),
                                               ALU.subtract), "hb_diff", u)
                    for t in range(TU):
                        v.wait("hb_exp", u, 0, t + 1)
                        k = TU * u + t
                        follow(v, u, dve.tensor_reduce(hbs[:, k, :], view(t), AX.X, ALU.add))
                        done(dve.reciprocal(hbr[:, k, :], hbs[:, k, :]), "hb_rec", u)
                if s == "hashT":
                    v.wait("hbT_ps", u, i)
                    done(dve.tensor_copy(hash_T[1][u][:, :, P * i:P * (i + 1)],
                                         own(u, 1).rearrange("p (i q) -> p i q", i=QUAD)), "kbT", u, i)
                if s == "softmax":
                    v.wait("scores", u, i)
                    for t in range(TU):
                        sc = quad[:, :, 256 * t:256 * (t + 1)].rearrange("p j (i k) -> p j i k", k=S)
                        pr = probs[:, u, :, t, :].rearrange("p j (i k) -> p j i k", k=S)
                        m = smax[:, TU * u + t, :].rearrange("p (j i) -> p j i", i=QUAD)
                        if i == 2:
                            done(dve.tensor_tensor(pr, sc, bias[:].rearrange("p (j i) k -> p j i k", i=QUAD), ALU.add),
                                 "biased", u, 2)
                            v.wait("biased", u, 2, t + 1)
                            sc = pr
                        follow(v, u, dve.tensor_reduce(m, sc, AX.X, ALU.max))
                        done(dve.tensor_tensor(pr, sc, m.unsqueeze(3).broadcast_to((P, QUAD, QUAD, S)), ALU.subtract),
                             "sdiff", u, i)
                if s in ("probsT0", "probsT1"):
                    t = int(s[-1])
                    v.wait(f"pT{t}_ps", u, i)
                    done(dve.tensor_copy(pT[:, TU * u + t, 4:8, :].rearrange("p c q -> p (c q)"), own(u, 1)),
                         f"pT{t}_v", u, i)
                if s == "pv":
                    for t in range(TU):
                        v.wait("pv_ps", u, i, t + 1)
                        k = TU * u + t
                        pv = own(u, t)[:, 0:288].rearrange("p (c b h e) -> p c b h e", c=8, b=2, h=2)
                        for bb in range(2):
                            q = slice(S * bb, S * (bb + 1))
                            m = dve.reciprocal(rden[q, k, :, :], pv[q, :, bb, :, DH])
                        follow(v, u, m)
                        for bb in range(2):
                            q = slice(S * bb, S * (bb + 1))
                            m = dve.tensor_tensor(attn[q, k, :].rearrange("p (c h d) -> p c h d", c=8, h=2),
                                                  pv[q, :, bb, :, 0:DH],
                                                  rden[q, k, :, :].unsqueeze(3).broadcast_to((S, 8, 2, DH)), ALU.mult)
                        done(m, "attn", u, i)
                if s == "out":
                    v.wait("o_ps", u, i)
                    o = own(u, 1)[:, 0:UT].rearrange("p (t d) -> p t d", t=TU)
                    dst, src = (xa, xin) if i == 0 else (xb, xsum)
                    done(dve.tensor_tensor(dst[:, ts, :], o, src[:, ts, :], ALU.add), "res", u, i)
                    v.wait("res", u, i)
                if s == "m_out":
                    v.wait("m2_ps", u)
                    v.wait("xs", u)
                    follow(v, u, dve.tensor_tensor(xb[:, ts, :], own(u, 0)[:, 0:UT].rearrange("p (t d) -> p t d", t=TU),
                                                   xsum[:, ts, :], ALU.add))
                    if u == NU - 1:
                        dve.sem_inc(sem["x_free"], 1)
                if s == "choose":
                    e = (E0, E1)[i]
                    v.wait("r_ps", u, i)
                    g, o1, o2, ex = (a[:, ts, 0:e] for a in (lg, oh, oh2, le))
                    m = [lgm[:, ts, k] for k in range(6)]
                    fall = over_tiles(falling[i][:], e)
                    logits = own(u, 1)[:, 0:TU * e].rearrange("p (t e) -> p t e", e=e)
                    follow(v, u, dve.tensor_tensor(o1, logits, over_tiles(row(f"r{i}"), e), ALU.add))
                    follow(v, u, dve.tensor_reduce(m[0], o1, AX.X, ALU.max))
                    done(dve.tensor_tensor(g, o1, last(m[0], e), ALU.subtract), "r_diff", u, i)
                    v.wait("r_diff", u, i)
                    follow(v, u, dve.tensor_scalar(o1, g, 0.0, None, ALU.is_equal))
                    follow(v, u, dve.tensor_tensor(o1, o1, fall, ALU.mult))
                    follow(v, u, dve.tensor_reduce(m[1], o1, AX.X, ALU.max))
                    if i == 0:
                        done(dve.tensor_tensor(o2, o1, last(m[1], e), ALU.is_equal), "gates", u, i)
                        v.wait("gates", u, i)
                        v.wait("r_exp", u, i)
                        follow(v, u, dve.tensor_reduce(m[2], ex, AX.X, ALU.add))
                        follow(v, u, dve.reciprocal(m[3], m[2]))
                        follow(v, u, dve.tensor_tensor(o1, o2, last(m[3], e), ALU.mult))
                    else:
                        follow(v, u, dve.tensor_tensor(o2, o1, last(m[1], e), ALU.is_equal))
                        follow(v, u, dve.scalar_tensor_tensor(o1, o2, NEG, g, ALU.mult, ALU.add))
                        follow(v, u, dve.tensor_reduce(m[2], o1, AX.X, ALU.max))
                        follow(v, u, dve.tensor_tensor(o1, o1, last(m[2], e), ALU.is_equal))
                        follow(v, u, dve.tensor_tensor(o1, o1, fall, ALU.mult))
                        follow(v, u, dve.tensor_reduce(m[3], o1, AX.X, ALU.max))
                        follow(v, u, dve.tensor_tensor(o1, o1, last(m[3], e), ALU.is_equal))
                        follow(v, u, dve.tensor_tensor(o2, o2, o1, ALU.add))
                        v.wait("r_exp", u, i)
                        follow(v, u, dve.tensor_tensor(o2, o2, ex, ALU.mult))
                        follow(v, u, dve.tensor_reduce(m[4], o2, AX.X, ALU.add))
                        follow(v, u, dve.reciprocal(m[5], m[4]))
                        done(dve.tensor_tensor(o1, o2, last(m[5], e), ALU.mult), "gates", u, i)
                if s == "gateT":
                    e = (E0, E1)[i]
                    v.wait("gateT_ps", u, i)
                    if i == 0:
                        dve.tensor_copy(gateTb[:, tokens(u)], own(u, 1)[0:e, 0:UT])
                    done(dve.tensor_copy(gateT[0:e, tokens(u)], own(u, 1)[0:e, 0:UT]), "gateT", u, i)
                if s == "masks":
                    v.wait_own("xT", u, XT_OF[L_F])
                    for n in range(4):
                        v.wait("mask_ps", u, 0, n + 1)
                        done(dve.tensor_tensor(xe[u][:, 2 * n:2 * n + 2, :], bank(n).rearrange("p (e t) -> p e t", e=2),
                                               xT[:, tokens(u)].unsqueeze(1).broadcast_to((P, 2, UT)), ALU.mult), "xe", u)
                if s == "e_mix":
                    v.wait("e2_ps", u, i)
                    k = TU * u + i
                    w = oh[:, k, :].unsqueeze(2).broadcast_to((P, E0, D))
                    done(dve.tensor_tensor(prod[u][:, i, :].rearrange("p (e d) -> p e d", e=E0),
                                           bank(2 * i, 2).rearrange("p (e d) -> p e d", e=E0), w, ALU.mult), "e_prod", u, i)
                    v.wait("e_prod", u, i)
                    dve.tensor_reduce(xsum[:, k, :], prod[u][:, i, :].rearrange("p (e d) -> p d e", e=E0), AX.X, ALU.add)
                    follow(v, u, dve.scalar_tensor_tensor(attn[:, k, :], own(u, i)[:, 0:D], lgm[:, k, 3:4],
                                                          xa[:, k, :], ALU.mult, ALU.add))
                    follow(v, u, dve.tensor_tensor(xb[:, k, :], xsum[:, k, :], attn[:, k, :], ALU.add))
                if s == "w_qk":
                    for c in range(2):
                        v.wait("wk_ps", u, i, c + 1)
                        k = 4 * i + 2 * c
                        done(dve.tensor_copy(wkT[u][:, k:k + 2, :].rearrange("p c t -> p (c t)"), own(u, 1)), "wk", u, i)
                if s == "w_v":
                    for t in range(TU):
                        v.wait("wv_v_ps", u, 0, t + 1)
                        done(dve.tensor_copy(wvt[u][:, t, 512:1024], own(u, 1)), "wv_v", u)
                if s == "w_softmax":
                    over = lambda a: a.unsqueeze(1).broadcast_to((P, H, S))
                    for t in range(TU):
                        v.wait("ws_ps", u, 0, t + 1)
                        src = bank(2 * t, 2).rearrange("p (h q) -> p h q", q=S)
                        e = prod[u][:, t, :].rearrange("p (h q) -> p h q", q=S)
                        m = wmax[:, TU * u + t, :]
                        follow(v, u, dve.tensor_reduce(m, src.rearrange("p h q -> p q h"), AX.X, ALU.max))
                        done(dve.tensor_tensor(e, src, over(m), ALU.subtract), "w_diff", u)
                    for t in range(TU):
                        v.wait("w_exp", u, 0, t + 1)
                        e = prod[u][:, t, :].rearrange("p (h q) -> p h q", q=S)
                        m, r = wmax[:, TU * u + t, :], wrec[:, TU * u + t, :]
                        follow(v, u, dve.tensor_reduce(m, e.rearrange("p h q -> p q h"), AX.X, ALU.add))
                        follow(v, u, dve.reciprocal(r, m))
                        done(dve.tensor_tensor(e, e, over(r), ALU.mult), "w_attn", u)
                if s == "w_ctx":
                    v.wait("wc_ps", u, i)
                    done(dve.tensor_copy(pT[:, TU * u + i, :, S:P], own(u, 1).rearrange("p (c q) -> p c q", c=NCH)),
                         "wc_v", u, i)
                if s == "w_out":
                    v.wait("wo_ps", u)
                    follow(v, u, dve.tensor_tensor(xb[:, ts, :], own(u, 0)[:, 0:UT].rearrange("p (t d) -> p t d", t=TU),
                                                   xa[:, ts, :], ALU.add))
                if s == "g_mix":
                    v.wait("g2_ps", u)
                    dve.tensor_tensor(attn[:, ts, :], bank(2)[:, 0:UT].rearrange("p (t d) -> p t d", t=TU),
                                      xa[:, ts, :], ALU.add)
                    for t in range(TU):
                        k = TU * u + t
                        w = oh[:, k, 0:E1].unsqueeze(2).broadcast_to((P, E1, D))
                        done(dve.tensor_tensor(prod[u][:, t, 0:512].rearrange("p (e d) -> p e d", e=E1),
                                               bank(t).rearrange("p (e d) -> p e d", e=E1), w, ALU.mult), "g_prod", u)
                    v.wait("g_prod", u)
                    for t in range(TU):
                        k = TU * u + t
                        m = dve.tensor_reduce(xsum[:, k, :], prod[u][:, t, 0:512].rearrange("p (e d) -> p d e", e=E1),
                                              AX.X, ALU.add)
                    follow(v, u, m)
                    follow(v, u, dve.tensor_tensor(xb[:, ts, :], xsum[:, ts, :], attn[:, ts, :], ALU.add))

            dve.wait_ge(sem["bias_dup"], 16)
            for s, i, u, _ in FIRST:
                step(Values(dve, sem, 0), s, i, u)
            if groups > 1:
                with dve.Fori(0, groups - 1) as it:
                    now, following = Values(dve, sem, it), Values(dve, sem, it, 1)
                    for s, i, u, ahead in BODY:
                        step(following if ahead else now, s, i, u)
            for s, i, u, _ in LAST:
                step(Values(dve, sem, groups - 1), s, i, u)

        @block.tensor
        def _(pe):
            mm, flip = nc.tensor.matmul, nc.tensor.transpose
            pe.wait_ge(sem["weights0"], W0)
            pe.wait_ge(sem["setup"], N_SETUP)
            flip(bank(0)[:, 0:127], emb[0:127, :], ident[0:127, 0:127]).then_inc(sem["setup_pe"], 1)
            pe.wait_ge(sem["setup_act"], 1)
            mm(bank(1)[0:H, 0:127], hmask[:], embT[:, 0:127], start=True, stop=True).then_inc(sem["setup_pe"], 1)
            pe.wait_ge(sem["setup_act"], 2)
            for s in range(S):
                m = flip(bank(2, 2)[0:S, H * s:H * (s + 1)], tabT[:, S - 1 - s:2 * S - 1 - s], ident[0:H, 0:H])
            m.then_inc(sem["setup_pe"], 1)

            reader = []

            def take_quad(v, name, u, c=0):
                if reader:
                    v.wait(*reader.pop())
                reader.append((name, u, c))

            def step(v, s, i, u):
                tok = tokens(u)
                if s == "xT":
                    src = xn if i in (L_A1, L_A2, L_F) else xa
                    v.wait_own("ln_out", u, i + 1)
                    for t in range(TU):
                        m = flip(own(u, 0)[:, P * t:P * (t + 1)], src[:, TU * u + t, :], ident[:])
                    done_own(m, "xT_ps", u)
                if s == "proj":
                    v.wait_own("xT", u, {0: 1, 1: 3, 2: 6}[i])
                    if i == 1 and u == 0:
                        pe.wait_ge(sem["weights"], W1)
                        pe.wait_ge(sem["ctx_in"], v.group(16) + 16)
                    kv = (ctxT if i == 1 else xT)[:, tok]
                    mm(own(u, 0)[:, UT:], wk[i][:], kv, start=True, stop=True)
                    done(mm(own(u, 0)[:, 0:UT], wq[i][:], xT[:, tok], start=True, stop=True), "qk_ps", u, i)
                    for b in range(BU):
                        for r in range(2):
                            m = mm(own(u, 1)[S * r:S * (r + 1), S * b:S * (b + 1)], kv[:, S * b:S * (b + 1)],
                                   wv[i][:].rearrange("p (c r d) -> p r c d", r=2, d=DH)[:, r, :, :], start=True, stop=True)
                    done(m, "v_ps", u, i)
                if s == "hash":
                    v.wait("qT", u, 0)
                    take_quad(v, "hb_diff", u)
                    for t in range(TU):
                        k = tile_tokens(u, t)
                        mm(bank(2 * t), qT[:, k], whash[:, 0, :], start=True, stop=True)
                        done(mm(bank(2 * t + 1), kT[:, k], whash[:, 1, :], start=True, stop=True), "hb_ps", u)
                if s == "hashT":
                    v.wait("hb_norm", u, 0, i + 1)
                    if i == 0:
                        v.wait("vbd", u, 0)
                    else:
                        v.wait("qbT", u, 0)
                        v.wait("kbT", u, 0)
                    for k in range(8):
                        m = flip(own(u, k // 4)[:, P * (k % 4):P * (k % 4 + 1)], hb[u][:, i, P * k:P * (k + 1)], ident[:])
                    done(m, "hbT_ps", u, i)
                if s == "scores":
                    v.wait("qT", u, i)
                    v.wait("kexp", u, i)
                    v.wait("vbd", u, i)
                    if i == 0:
                        v.wait("qbT", u, 1)
                        v.wait("kbT", u, 1)
                    if i < 2:
                        take_quad(v, "sdiff", u, i)
                    else:
                        take_quad(v, "biased", u, 2)
                    for t in range(TU):
                        for bb in range(2):
                            b, q = TU * t + bb, slice(S * bb, S * (bb + 1))
                            k = slice(S * b, S * (b + 1))
                            for j in range(4):
                                r = slice(32 * j, 32 * (j + 1))
                                m = mm(quad[q, j, 256 * t:256 * (t + 1)], qT[r, UT * u + S * b:UT * u + S * (b + 1)],
                                       kexp[u][r, :, k], start=True, stop=(i > 0))
                            if i == 0:
                                for n in range(QUAD):
                                    for j in range(4):
                                        r = slice(32 * j, 32 * (j + 1))
                                        at = 256 * t + S * n
                                        m = mm(quad[q, j, at:at + S], hash_T[0][u][r, n, k], hash_T[1][u][r, n, k],
                                               start=False, stop=(n == 3))
                    done(m, "scores", u, i)
                if s in ("probsT0", "probsT1"):
                    t = int(s[-1])
                    v.wait("probs", u, i, t + 1)
                    if t:
                        v.wait("pT0_a", u, i)
                        v.wait("pT0_v", u, i)
                    for k in range(8):
                        j, i0 = k // 2, 2 * (k % 2)
                        m = flip(own(u, k // 4)[:, P * (k % 4):P * (k % 4 + 1)],
                                 probs[:, u, j, t, S * i0:S * (i0 + 2)], ident[:])
                    done(m, f"pT{t}_ps", u, i)
                if s == "pv":
                    v.wait("pT1_a", u, i)
                    for t in range(TU):
                        if t:
                            v.wait("pT1_v", u, i)
                        else:
                            v.wait("pT0_v", u, i)
                        b = BU * u + 2 * t
                        for k in range(8):
                            m = mm(own(u, t)[:, 36 * k:36 * (k + 1)], pT[:, TU * u + t, k, :], vbd[:, b:b + 2, k, :],
                                   start=True, stop=True)
                        done(m, "pv_ps", u, i)
                if s == "headsT":
                    v.wait("attn", u, i)
                    for t in range(TU):
                        m = flip(own(u, 0)[:, P * t:P * (t + 1)], attn[:, TU * u + t, :], ident[:])
                    done(m, "aT_ps", u, i)
                if s == "out":
                    v.wait("aT", u, i)
                    for t in range(TU):
                        m = mm(own(u, 1)[:, P * t:P * (t + 1)], aT[:, tile_tokens(u, t)], wo[i][:], start=True, stop=True)
                    done(m, "o_ps", u, i)
                if s == "m_hidden":
                    v.wait_own("xT", u, 2)
                    for c in range(FC):
                        m = mm(own(u, c // 2)[:, UT * (c % 2):UT * (c % 2 + 1)], m_w1[:, P * c:P * (c + 1)], xT[:, tok],
                               start=True, stop=True)
                        if c % 2:
                            done(m, "m_ps", u)
                if s == "m_out":
                    v.wait("m_h", u)
                    for t in range(TU):
                        for c in range(FC):
                            m = mm(own(u, 0)[:, P * t:P * (t + 1)], hT[u][:, c, P * t:P * (t + 1)], m_w2[:, c, :],
                                   start=(c == 0), stop=(c == FC - 1))
                    done(m, "m2_ps", u)
                if s == "route":
                    v.wait_own("xT", u, {0: 4, 1: 8}[i])
                    e, w = ((E0, e_r), (E1, g_r))[i]
                    for t in range(TU):
                        m = mm(own(u, 1)[:, e * t:e * (t + 1)], xT[:, tile_tokens(u, t)], w[:], start=True, stop=True)
                    done(m, "r_ps", u, i)
                if s == "gateT":
                    e, src = ((E0, oh2), (E1, oh))[i]
                    v.wait("gates", u, i)
                    if i:
                        v.wait("g_h", u, 3)
                    for t in range(TU):
                        m = flip(own(u, 1)[0:e, P * t:P * (t + 1)], src[:, TU * u + t, 0:e], ident[:])
                    done(m, "gateT_ps", u, i)
                if s == "masks":
                    v.wait("gateT", u, 0)
                    take_quad(v, "xe", u)
                    for n in range(4):
                        for e in (2 * n, 2 * n + 1):
                            m = mm(bank(n)[:, UT * (e % 2):UT * (e % 2 + 1)], pick[:, e, :], gateTb[:, tok],
                                   start=True, stop=True)
                        done(m, "mask_ps", u)
                if s == "e_hidden":
                    f = slice(P * i, P * (i + 1))
                    dst = own(u, i % 2)[:, UT * (i // 2):UT * (i // 2 + 1)]
                    v.wait("xe", u)
                    if i >= 2:
                        v.wait("e_h", u, i - 2)
                    mm(dst, e_b1[:, f], gateT[:, tok], start=True, stop=False)
                    for e in range(E0):
                        m = mm(dst, e_w1[:, e, f], xe[u][:, e, :], start=False, stop=(e == E0 - 1))
                    done(m, "e_ps", u, i)
                if s == "e_out":
                    v.wait("e_h", u, 3)
                    take_quad(v, "e_prod", u, i)
                    for c in range(FC):
                        for n in range(2):
                            mm(bank(2 * i + n), hT[u][:, c, P * i:P * (i + 1)],
                               e_w2[:, c, 4 * n:4 * n + 4, :].rearrange("p e d -> p (e d)"),
                               start=(c == 0), stop=(c == FC - 1))
                    done(mm(own(u, i)[:, 0:D], gateT[:, tile_tokens(u, i)], e_b2[:], start=True, stop=True), "e2_ps", u, i)
                if s == "w_qk":
                    if i == 0:
                        v.wait_own("xT", u, XT_OF[L_O4])
                    for c in range(2):
                        k = 4 * i + 2 * c
                        if k:
                            v.wait("wq", u, *((i, c) if c else (i - 1, 2)))
                        for n in range(2):
                            m = mm(own(u, 0)[:, UT * n:UT * (n + 1)], ww[0][:, P * (k + n):P * (k + n + 1)], xT[:, tok],
                                   start=True, stop=True)
                        done(m, "wq_ps", u, i)
                        if k:
                            v.wait("wk", u, *((i, c) if c else (i - 1, 2)))
                        for n in range(2):
                            m = mm(own(u, 1)[:, UT * n:UT * (n + 1)], ww[1][:, P * (k + n):P * (k + n + 1)], ctxT[:, tok],
                                   start=True, stop=True)
                        done(m, "wk_ps", u, i)
                if s == "w_v":
                    for t in range(TU):
                        for n, (copied, copy) in enumerate((("wq", "wv_a"), ("wk", "wv_v"))):
                            if t == 0:
                                v.wait(copied, u, 1)
                            else:
                                v.wait(copy, u, 0, t)
                            done(mm(own(u, n), ctxT[:, tile_tokens(u, t)], ww[2][:, 512 * n:512 * (n + 1)],
                                    start=True, stop=True), f"{copy}_ps", u)
                if s == "w_scores":
                    v.wait("wq", u, 1)
                    v.wait("wk", u, 1)
                    take_quad(v, "w_diff", u)
                    v.apart()
                    for t in range(TU):
                        for bb in range(2):
                            k = slice(P * t + S * bb, P * t + S * (bb + 1))
                            for c in range(NCH):
                                for r in range(2):
                                    d = slice(S * r, S * (r + 1))
                                    m = mm(bank(2 * t + r)[S * bb:S * (bb + 1), S * c:S * (c + 1)],
                                           wkT[u][d, c, k], wqT[u][d, c, k], start=True, stop=True)
                        done(m, "ws_ps", u)
                if s == "w_ctx":
                    v.wait("w_attn", u, 0, i + 1)
                    if i == 0:
                        v.wait("wv_a", u)
                        v.wait("wv_v", u)
                        if u == NU - 1:
                            pe.sem_inc(sem["ctx_free"], 1)
                        else:
                            v.apart()
                    else:
                        v.wait("wc_a", u, 0)
                        v.wait("wc_v", u, 0)
                        v.apart()
                    for c in range(NCH):
                        for r in range(2):
                            for bb in range(2):
                                k = slice(S * bb, S * (bb + 1))
                                e = prod[u][k, i, 512 * r + S * c:512 * r + S * (c + 1)]
                                m = mm(own(u, bb)[S * r:S * (r + 1), S * c:S * (c + 1)],
                                       wvt[u][k, i, P * c + S * r:P * c + S * (r + 1)], e, start=True, stop=True)
                    done(m, "wc_ps", u, i)
                if s == "w_out":
                    v.wait("wc_a", u, 1)
                    v.wait("wc_v", u, 1)
                    for t in range(TU):
                        for c in range(NCH):
                            m = mm(own(u, 0)[:, P * t:P * (t + 1)], pT[:, TU * u + t, c, :], wwo[:, c, :],
                                   start=(c == 0), stop=(c == NCH - 1))
                    done(m, "wo_ps", u)
                if s == "g_hidden":
                    for p in range(2):
                        if i == 0 and p:
                            v.wait("r_diff", u, 1)
                        if i:
                            v.wait("g_h", u, i - 1, 2 * p + 2)
                        for n in range(4 * i + 2 * p, 4 * i + 2 * p + 2):
                            e, c = n // FC, n % FC
                            m = mm(own(u, p)[:, UT * (n % 2):UT * (n % 2 + 1)], g_w1[:, e, P * c:P * (c + 1)], xT[:, tok],
                                   start=True, stop=True)
                        done(m, "g_ps", u, i)
                if s == "g_out":
                    v.wait("gateT", u, 1)
                    take_quad(v, "g_prod", u)
                    for t in range(TU):
                        for c in range(FC):
                            for e in range(E1):
                                mm(bank(t)[:, D * e:D * (e + 1)], gh[u][:, e * FC + c, P * t:P * (t + 1)], g_w2[:, c, e, :],
                                   start=(c == 0 and e == 0), stop=(c == FC - 1), skip_group_check=True)
                    for t in range(TU):
                        m = mm(bank(2)[:, P * t:P * (t + 1)], gateT[0:E1, tile_tokens(u, t)], g_b2[:], start=True, stop=True)
                    done(m, "g2_ps", u)

            pe.wait_ge(sem["setup_v"], N_SETUP_V)
            for s, i, u, _ in FIRST:
                step(Values(pe, sem, 0), s, i, u)
            if groups > 1:
                with pe.Fori(0, groups - 1) as it:
                    now, following = Values(pe, sem, it), Values(pe, sem, it, 1)
                    for s, i, u, ahead in BODY:
                        step(following if ahead else now, s, i, u)
                    now.wait(*reader.pop())
            for s, i, u, _ in LAST:
                step(Values(pe, sem, groups - 1), s, i, u)

        rounds = 1 if groups == 1 else 2
        for n in SIGNALS:
            giving, count = giving_steps(n)
            assert sorted(given[n]) == sorted(giving * count * rounds), f"signal {n}: given {given[n]}"
        for n, count in UNIT_SIGNALS.items():
            for u in range(NU):
                assert len(given[n, u]) == count * rounds, f"signal {n}: given {len(given[n, u])} times"


def host_layout(x):
    import numpy as np

    a = {k: np.ascontiguousarray(v) for k, v in x.items()}
    r = {}
    r["x"] = a["x"].reshape(B * S, D)
    r["ctxT"] = a["ctx_1024"].reshape(B * S, D).T
    r["wq0"], r["wk0"], r["wv0"] = (a[f"L0_attn_W{n}"].reshape(D, D) for n in "qkv")
    r["wo0"] = a["L0_attn_Wo"].reshape(D, D)
    r["whq"], r["whk"] = (a[f"L0_attn_Wh{n}"].reshape(D, NBK) for n in "qk")
    r["m_w1"], r["m_w2"] = a["L0_attn_W1"], a["L0_attn_W2"]
    for n in "qkvo":
        r[f"w{n}1"] = a[f"L0_xattn_W{n}"].T
    r["e_r"], r["e_w1"], r["e_w2"] = a["L0_ffn_Wr"], a["L0_ffn_W1"], a["L0_ffn_W2"]
    r["e_b1"], r["e_b2"] = a["L0_ffn_b1"], a["L0_ffn_b2"]
    for i, n in enumerate("qkv"):
        r[f"w{n}2"] = a["L1_attn_qkv_w"][i * D:(i + 1) * D].T
    r["wo2"] = a["L1_attn_proj_w"].T
    r["emb"] = a["L1_attn_rel_pos_emb"][S:S + 127]
    for n in "qkvo":
        r[f"ww{n}"] = a[f"L1_xattn_W_{n.upper()}"]
    r["g_r"], r["g_w1"], r["g_w2"], r["g_b2"] = (a[f"L1_ffn_{n}"] for n in ("Wr", "W1", "W2", "b2"))
    qkv_b = a["L1_attn_qkv_b"].reshape(3, D)
    r["cols"] = np.stack([a["L0_attn_ln1_g"], a["L0_attn_ln1_b"], a["L0_attn_ln2_g"], a["L0_attn_ln2_b"],
                          *a["L0_attn_b1"].reshape(FC, P), a["L0_xattn_bq"], a["L0_xattn_bk"], a["L0_xattn_bv"],
                          a["L0_ffn_ln_g"], a["L0_ffn_ln_b"], *qkv_b, *a["L1_ffn_b1"].reshape(E1 * FC, P)], axis=1)
    r["rows"] = np.concatenate([a["L0_attn_b2"], a["L0_xattn_bo"], a["L1_attn_proj_b"], a["L1_xattn_ln_gamma"],
                                a["L1_xattn_ln_beta"], a["L0_ffn_br"], a["L1_ffn_br"]])[None, :]
    return {k: np.ascontiguousarray(v) for k, v in r.items()}


def kernel(**inputs):
    import concourse.bacc as _bacc
    from concourse import mybir as _mybir
    from concourse.bass_utils import run_bass_kernel_spmd as _run

    nc = _bacc.Bacc("TRN2", target_bir_lowering=False, num_devices=1)
    arrays, args = {}, {}
    for name, a in host_layout(inputs).items():
        arrays[f"in_{name}"] = a
        args[name] = nc.dram_tensor(f"in_{name}", a.shape, _mybir.dt.from_np(a.dtype), kind="ExternalInput").ap()
    out = nc.dram_tensor("out_0_dram", (B, S, D), _mybir.dt.float32, kind="ExternalOutput").ap()
    decoder_kernel(nc, args, out)
    r = _run(nc, [arrays], core_ids=[0])
    return r.results[0]["out_0_dram"]
```

```python
from contextlib import ExitStack

import concourse.bass as bass
from concourse import mybir

F32 = mybir.dt.float32
BF16 = mybir.dt.bfloat16
ALU = mybir.AluOpType
ACT = mybir.ActivationFunctionType
AX = mybir.AxisListType

P = 128
B, S, D = 128, 64, 128
GT = 512
NG = B * S // GT
NT = GT // P
NU = 2
UT = GT // NU
TU = NT // NU
NB = GT // S
BU = NB // NU
H, DH, QUAD = 16, 8, 4
NBK = 32
F = 512
FC = F // P
E0, E1 = 8, 4
DK = 64
NCH = H * DK // P
SQ8 = float(DH) ** 0.5
NEG = -1e30
N_SETUP = 14
N_SETUP_V = 8

COLS = ["ln1_g", "ln1_b", "ln2_g", "ln2_b", "mb0", "mb1", "mb2", "mb3", "xbq", "xbk", "xbv",
        "lnf_g", "lnf_b", "cbq", "cbk", "cbv"] + [f"fb{i}" for i in range(E1 * FC)]
COL = {n: i for i, n in enumerate(COLS)}
ROWS = {"mlp_b2": (0, P), "xbo": (P, P), "cbo": (2 * P, P), "lnx_g": (3 * P, P), "lnx_b": (4 * P, P),
        "r0": (5 * P, E0), "r1": (5 * P + E0, E1)}
NROW = 5 * P + E0 + E1

LN_EPS = [1e-6, 1e-6, 1e-5, 1e-5, 1e-5, 1e-5, 1e-5, 1e-5, 1e-5, 1e-5]
L_A1, L_A2, L_O1, L_O2, L_F, L_O3, L_O4, L_X, L_O5, L_O6 = range(10)


def attention_steps(c):
    return [("scores", c), ("softmax0", c), ("softmax1", c), ("probsT0", c), ("probsT1", c), ("pv", c),
            ("headsT", c), ("out", c)]


def norm_steps(n):
    return [("stats", n), ("norm", n)]


STAGES = [
    [*norm_steps(L_A1), ("xT", L_A1), ("proj", 0), ("hash", 0), ("b_shift", 0), ("b_shift", 1), ("b_scale", 0),
     ("b_scale", 1), ("hashT", 0), ("hashT", 1), *attention_steps(0), *norm_steps(L_A2), ("xT", L_A2),
     ("m_hidden", 0), ("m_out", 0), *norm_steps(L_O1), ("xT", L_O1)],
    [("proj", 1), *attention_steps(1), *norm_steps(L_O2), ("xT", L_O2)],
    [("route", 0), *norm_steps(L_F), ("choose", 0), ("xT", L_F), ("gateT", 0), ("masks", 0), ("e_hidden", 0),
     ("e_hidden", 1), ("e_hidden", 2), ("e_hidden", 3), ("e_out", 0), ("e_mix", 0), ("e_out", 1), ("e_mix", 1),
     *norm_steps(L_O3), ("xT", L_O3)],
    [("proj", 2), *attention_steps(2), *norm_steps(L_O4), ("xT", L_O4)],
    [("w_qk", 0), ("w_qk", 1), ("w_v", 0), ("w_scores", 0), ("w_shift", 0), ("w_shift", 1), ("w_scale", 0),
     ("w_scale", 1), ("w_ctx", 0), ("w_ctx", 1), ("w_out", 0), *norm_steps(L_X), *norm_steps(L_O5), ("xT", L_O5)],
    [("route", 1), ("choose", 1), ("g_hidden", 0), ("g_hidden", 1), ("g_hidden", 2), ("g_hidden", 3), ("gateT", 1),
     ("g_out", 0), ("g_mix", 0), *norm_steps(L_O6)],
]
STEPS = [s for stage in STAGES for s in stage]
ENGINES = ("pe", "act", "dve", "pool")
HEAD = dict(pe=21, act=24, dve=23, pool=7)
MERGE = dict(
    pe=("000111100010011111000101011101010000110000001111000010111100100001011100100010100111100001111101"
        "010111000001011011111010000110100010101010111110000001010111110100001001111110001101010101100111"),
    act=("101110000111111000101111001000000110001111100000011111000000001111110000010011100111001101001110"
        "010110000111110011100100110001010011111100001001001011111100010010011111000011101100100001111001"),
    dve=("100101111100011001010111010100000010011100101111100000011000001110110001000111000111101100110100"
        "000001111110111001001110110001110000101110001001011001111100010001110111100011000000111110111100"),
    pool=("000000000000111100000000011111111111111111111110110000000000000000000000000000000000000000000000"
        "010111111111111111111111111111110000000000000000001000001111111111111111110001111111111111111111"),
)


SIGNALS = {
    "qk_ps": ("proj", 1, "pe"), "v_ps": ("proj", 1, "pe"), "qT": ("proj", 1, "act"), "kT": ("proj", 1, "act"), "kexp": ("proj", 1, "pool"), "vbd": ("proj", 1, "dve"),
    "scores": ("scores", 1, "pe"), "biased0": ("softmax0", 1, "dve"), "biased1": ("softmax1", 1, "dve"), "sdiff0": ("softmax0", 1, "dve"), "sdiff1": ("softmax1", 1, "dve"), "probs0": ("softmax0", 1, "act"), "probs1": ("softmax1", 1, "act"),
    "pT0_ps": ("probsT0", 1, "pe"), "pT0_a": ("probsT0", 1, "act"), "pT0_v": ("probsT0", 1, "dve"), "pT1_ps": ("probsT1", 1, "pe"), "pT1_a": ("probsT1", 1, "act"), "pT1_v": ("probsT1", 1, "dve"),
    "pv_ps": ("pv", 2, "pe"), "attn": ("pv", 2, "dve"), "aT_ps": ("headsT", 1, "pe"), "aT": ("headsT", 1, "act"), "o_ps": ("out", 1, "pe"), "res": ("out", 1, "dve"),
    "hb_ps": ("hash", 2, "pe"), "hb_diff": ("b_shift", 1, "dve"), "hb_exp": ("b_shift", 1, "act"), "hb_rec": ("b_scale", 1, "dve"), "hb_norm": ("b_scale", 1, "pool"), "hb_knorm": ("b_scale", 1, "dve"),
    "hbT_ps": ("hashT", 1, "pe"), "qbT": ("hashT", 1, "act"), "kbT": ("hashT", 1, "dve"),
    "m_ps": ("m_hidden", 2, "pe"), "m_h": ("m_hidden", 4, "act"), "m2_ps": ("m_out", 1, "pe"), "xs_part": ("out", 1, "pool"), "xs": ("out", 1, "pool"),
    "r_ps": ("route", 1, "pe"), "r_diff": ("choose", 1, "dve"), "r_exp": ("choose", 1, "act"), "gates": ("choose", 1, "dve"), "gateT_ps": ("gateT", 1, "pe"), "gateT": ("gateT", 1, "dve"),
    "mask_ps": ("masks", 4, "pe"), "xe": ("masks", 4, "dve"), "e_ps": ("e_hidden", 1, "pe"), "e_h": ("e_hidden", 1, "act"), "e2_ps": ("e_out", 1, "pe"), "e_prod": ("e_mix", 1, "dve"),
    "wq_ps": ("w_qk", 2, "pe"), "wk_ps": ("w_qk", 2, "pe"), "wq": ("w_qk", 2, "act"), "wk": ("w_qk", 2, "dve"),
    "wv_a_ps": ("w_v", 2, "pe"), "wv_v_ps": ("w_v", 2, "pe"), "wv_a": ("w_v", 2, "act"), "wv_v": ("w_v", 2, "dve"),
    "ws_ps": ("w_scores", 2, "pe"), "w_diff": ("w_shift", 1, "dve"), "w_exp": ("w_shift", 1, "act"), "w_rec": ("w_scale", 1, "dve"), "w_even": ("w_scale", 1, "dve"), "w_odd": ("w_scale", 1, "pool"),
    "wc_ps": ("w_ctx", 1, "pe"), "wc_a": ("w_ctx", 1, "act"), "wc_v": ("w_ctx", 1, "dve"), "wo_ps": ("w_out", 1, "pe"),
    "g_ps": ("g_hidden", 2, "pe"), "g_h": ("g_hidden", 4, "act"), "g2_ps": ("g_out", 1, "pe"), "g_prod": ("g_mix", 2, "dve"),
}
UNIT_SIGNALS = {
    "step": 96, "ln_mv": 10, "ln_log": 10, "ln_guess": 10, "ln_out": 10, "xT_ps": 8, "xT": 8,
}
XT_OF = {L_A1: 1, L_A2: 2, L_O1: 3, L_O2: 4, L_F: 5, L_O3: 6, L_O4: 7, L_O5: 8}
DMA_SIGNALS = ("x_in", "ctx_in", "out_done", "weights0", "weights", "bias_dup")
OTHER = ("setup", "setup_pe", "setup_v", "setup_act", "x_free", "ctx_free", "out_ready", "out_free", "apart")


def order(engine):
    at = [HEAD[engine], 0]
    for u in map(int, MERGE[engine]):
        yield (*STEPS[at[u] % len(STEPS)], u, at[u] // len(STEPS))
        at[u] += 1


BODY = {}
FIRST = {}


def giving_steps(name):
    kind, count, engine = SIGNALS[name]
    of_kind = [x for x in BODY[engine] if x[0] == kind]
    assert of_kind == [x for x in of_kind if not x[3]] + [x for x in of_kind if x[3]], name
    of_kind = [x for x in of_kind if x[3]] + [x for x in of_kind if not x[3]]
    return [(i, u) for _, i, u, _ in of_kind if (name not in ("biased0", "biased1") or i == 2)
            and (kind != "out" or name in ("o_ps", "res") or i == 0)], count


class Values:

    def __init__(self, eng, sems, it, ahead=0, base=None):
        self.eng, self.sems, self.it, self.ahead = eng, sems, it, ahead
        self.base = {} if base is None else base

    def following(self):
        return Values(self.eng, self.sems, self.it, 1, self.base)

    def value(self, per, k):
        k += self.ahead * per
        if isinstance(self.it, int):
            return self.it * per + k
        if per not in self.base:
            self.base[per] = self.eng.snap(self.it * per)
        value = self.eng.alloc_register()
        self.eng.reg_add(value, self.base[per], k)
        return value

    def wait(self, name, u, c=0, k=None):
        steps, count = giving_steps(name)
        k = count if k is None else k
        assert 1 <= k <= count, (name, c, k)
        self.eng.wait_ge(self.sems[name], self.value(len(steps) * count, steps.index((c, u)) * count + k))

    def wait_own(self, name, u, k):
        assert 1 <= k <= UNIT_SIGNALS[name], (name, k)
        self.eng.wait_ge(self.sems[name, u], self.value(UNIT_SIGNALS[name], k))

    def apart(self):
        self.eng.sem_inc(self.sems["apart"], 1)


def decoder_kernel(nc, A, out, groups=NG):
    for e in ENGINES:
        FIRST[e] = list((*s, 0) for s in STEPS[:HEAD[e]])
        BODY[e] = list(order(e))
    LAST = {e: list(x for x in BODY[e] if not x[3]) for e in ENGINES}
    ctx = ExitStack()
    with ctx:
        def sb(name, shape, dt=F32):
            return ctx.enter_context(nc.sbuf_tensor(name, shape, dt))

        sem = {n: ctx.enter_context(nc.semaphore(n)) for n in (*SIGNALS, *DMA_SIGNALS, *OTHER)}
        for n in UNIT_SIGNALS:
            for u in range(NU):
                sem[n, u] = ctx.enter_context(nc.semaphore(f"{n}_{u}"))
        given = {n: [] for n in sem}

        wq = [sb(f"wq{c}", [P, P]) for c in range(3)]
        wk = [sb(f"wk{c}", [P, P]) for c in range(3)]
        wv = [sb(f"wv{c}", [P, P]) for c in range(3)]
        wo = [sb(f"wo{c}", [P, P]) for c in range(3)]
        whash_raw = sb("whash_raw", [P, 2, NBK])
        whash = sb("whash", [P, 2, H * NBK])
        m_w1, m_w2 = sb("m_w1", [P, F]), sb("m_w2", [P, FC, P])
        e_w1, e_w2 = sb("e_w1", [P, E0, F]), sb("e_w2", [P, FC, E0, P])
        e_b1, e_b2, e_r = sb("e_b1", [E0, F]), sb("e_b2", [E0, P]), sb("e_r", [P, E0])
        ww = [sb(f"ww{n}", [P, H * DK]) for n in "qkv"]
        wwo = sb("wwo", [P, NCH, P])
        g_w1, g_w2 = sb("g_w1", [P, E1, F]), sb("g_w2", [P, FC, E1, P])
        g_b2, g_r = sb("g_b2", [E1, P]), sb("g_r", [P, E1])
        cols = sb("cols", [P, len(COLS)])
        rows = sb("rows", [P, NROW])

        ident = sb("ident", [P, P])
        hmask = sb("hmask", [P, H])
        qmask = sb("qmask", [P, QUAD])
        pick = sb("pick", [E0, E0, P], BF16)
        falling = [sb("falling0", [P, E0]), sb("falling1", [P, E1])]
        epsc = sb("epsc", [P, 2])
        bias = sb("bias", [P, H, S])

        xin = sb("xin", [P, NT, D])
        xa, xb = sb("xa", [P, NT, D]), sb("xb", [P, NT, D])
        xsum = sb("xsum", [P, NT, D])
        xn = sb("xn", [P, NT, D])
        yout = sb("yout", [P, NT, D])
        xT, ctxT = sb("xT", [P, GT]), sb("ctxT", [P, GT])
        qT, kT = sb("qT", [P, GT]), sb("kT", [P, GT])
        vbd = sb("vbd", [P, NB, H // 2, 2 * (DH + 1)])
        attn, aT = sb("attn", [P, NT, D]), sb("aT", [P, GT])
        probs = sb("probs", [P, NU, QUAD, TU, QUAD * S])
        pT = sb("pT", [P, NT, H // 2, P])
        smax = sb("smax", [P, NT, H])
        rden = sb("rden", [P, NT, H // 2, 2])
        stats, mv = sb("stats", [P, NT, 6]), sb("mv", [P, NT, 2])
        lnlog, rstd = sb("lnlog", [P, NT]), sb("rstd", [P, NT, 4])
        hbm, hbs, hbr = sb("hbm", [P, NT, 2 * H]), sb("hbs", [P, NT, 2 * H]), sb("hbr", [P, NT, 2 * H])
        wmax, wrec = sb("wmax", [P, NT, S]), sb("wrec", [P, NT, S])
        lg, lgm = sb("lg", [P, NT, E0]), sb("lgm", [P, NT, 8])
        le, oh, oh2 = sb("le", [P, NT, E0]), sb("oh", [P, NT, E0]), sb("oh2", [P, NT, E0])
        gateT, gateTb = sb("gateT", [E0, GT]), sb("gateTb", [E0, GT], BF16)

        big = [sb(f"big{u}", [P, 4096]) for u in range(NU)]
        small = [sb(f"small{u}", [P, 2048]) for u in range(NU)]
        part = lambda buf, a, b, pattern, **k: [t[:, a:b].rearrange(pattern, **k) for t in buf]
        hb = part(big, 0, 2048, "p (s f) -> p s f", s=TU)
        hash_T = [part(big, 2048 + 1024 * n, 3072 + 1024 * n, "p (i t) -> p i t", i=QUAD) for n in range(2)]
        xe = part(big, 0, 2048, "p (e t) -> p e t", e=E0)
        wqT = part(big, 0, 2048, "p (c t) -> p c t", c=NCH)
        wkT = part(big, 2048, 4096, "p (c t) -> p c t", c=NCH)
        gh = part(big, 0, 4096, "p (c t) -> p c t", c=E1 * FC)
        kexp = part(small, 0, 1024, "p (i t) -> p i t", i=QUAD)
        hT = part(small, 1024, 2048, "p (c t) -> p c t", c=FC)
        wvt = part(small, 0, 2048, "p (t f) -> p t f", t=TU)
        prod = [probs[:, u].rearrange("p j t f -> p (j t f)").rearrange("p (s f) -> p s f", s=TU) for u in range(NU)]
        emb, embT, tabT = big[0][:, 0:P], big[0][:, P:2 * P], big[0][0:H, 2 * P:3 * P]

        ps = ctx.enter_context(nc.psum_tensor("ps", [P, 8, 512], F32))
        flat = ps[:, :, :].rearrange("p a b -> p (a b)")

        def bank(b, n=1):
            return flat[:, 512 * b:512 * (b + n)]

        quad = ps[:, 0:4, :]

        def own(u, n):
            return bank(4 + 2 * u + n)

        def col(name):
            return cols[:, COL[name]:COL[name] + 1]

        def row(name):
            return rows[:, ROWS[name][0]:ROWS[name][0] + ROWS[name][1]]

        def tiles(u):
            return slice(TU * u, TU * (u + 1))

        def tokens(u):
            return slice(UT * u, UT * (u + 1))

        def tile_tokens(u, t):
            return slice(UT * u + P * t, UT * u + P * (t + 1))

        def over_tiles(r, width):
            return r.unsqueeze(1).broadcast_to((P, TU, width))

        def last(a, n):
            return a.unsqueeze(2).broadcast_to((P, TU, n))

        def done(instruction, name, u, c=0):
            given[name].append((c, u))
            instruction.then_inc(sem[name], 1)

        def done_own(instruction, name, u):
            given[name, u].append(0)
            instruction.then_inc(sem[name, u], 1)

        block = ctx.enter_context(nc.Block())

        x_v = A["x"].rearrange("(g t p) d -> g p t d", t=NT, p=P)
        c_v = A["ctxT"].rearrange("p (g t) -> g p t", t=GT)
        o_v = out.rearrange("b s d -> (b s) d").rearrange("(g t p) d -> g p t d", t=NT, p=P)
        loads0 = [
            (cols[:], A["cols"]), (emb[0:127, :], A["emb"]), (wq[0][:], A["wq0"]), (wk[0][:], A["wk0"]),
            (wv[0][:], A["wv0"]), (whash_raw[:, 0, :], A["whq"]), (whash_raw[:, 1, :], A["whk"]),
            (wo[0][:], A["wo0"]), (rows[:], A["rows"].to_broadcast((P, NROW))),
            (m_w1[:], A["m_w1"]), (m_w2[:], A["m_w2"].rearrange("(c p) d -> p c d", p=P)),
        ]
        loads = [
            (wq[1][:], A["wq1"]), (wk[1][:], A["wk1"]), (wv[1][:], A["wv1"]), (wo[1][:], A["wo1"]),
            (e_r[:], A["e_r"]), (e_w1[:], A["e_w1"].rearrange("e d f -> d e f")),
            (e_b1[:], A["e_b1"]), (e_b2[:], A["e_b2"]),
        ] + [(e_w2[:, c, :, :], A["e_w2"][:, c * P:(c + 1) * P, :].rearrange("e p d -> p e d"))
             for c in range(FC)] + [
            (wq[2][:], A["wq2"]), (wk[2][:], A["wk2"]), (wv[2][:], A["wv2"]), (wo[2][:], A["wo2"]),
            (ww[0][:], A["wwq"]), (ww[1][:], A["wwk"]), (ww[2][:], A["wwv"]),
            (wwo[:], A["wwo"].rearrange("(c p) d -> p c d", p=P)),
            (g_r[:], A["g_r"]), (g_w1[:], A["g_w1"].rearrange("e d f -> d e f")), (g_b2[:], A["g_b2"]),
        ] + [(g_w2[:, c, :, :], A["g_w2"][:, c * P:(c + 1) * P, :].rearrange("e p d -> p e d"))
             for c in range(FC)]
        W0, W1 = 16 * len(loads0), 16 * len(loads)

        @block.sync
        def _(sp):
            sp.dma_start(xin[:], x_v[0]).then_inc(sem["x_in"], 16)
            for dst, src in loads0:
                sp.dma_start(dst, src).then_inc(sem["weights0"], 16)
            sp.dma_start(ctxT[:], c_v[0]).then_inc(sem["ctx_in"], 16)
            for dst, src in loads:
                sp.dma_start(dst, src).then_inc(sem["weights"], 16)
            sp.wait_ge(sem["setup_v"], N_SETUP_V)
            sp.dma_start(bias[S:P, :, :], bias[0:S, :, :]).then_inc(sem["bias_dup"], 16)
            if groups > 1:
                with sp.Fori(0, groups - 1) as it:
                    sp.wait_ge(sem["x_free"], it + 1)
                    sp.dma_start(xin[:], x_v[it + 1]).then_inc(sem["x_in"], 16)
                    sp.wait_ge(sem["ctx_free"], it + 1)
                    sp.dma_start(ctxT[:], c_v[it + 1]).then_inc(sem["ctx_in"], 16)
                    sp.wait_ge(sem["out_ready"], it + 1)
                    sp.dma_start(o_v[it], yout[:]).then_inc(sem["out_done"], 16)
                    sp.wait_ge(sem["out_done"], (it + 1) * 16)
                    sp.sem_inc(sem["out_free"], 1)
            sp.wait_ge(sem["out_ready"], groups)
            sp.dma_start(o_v[groups - 1], yout[:]).then_inc(sem["out_done"], 16)
            sp.wait_ge(sem["out_done"], groups * 16)

        @block.gpsimd
        def _(pool):
            n = [0]

            def link(instruction):
                n[0] += 1
                instruction.then_inc(sem["setup"], 1)
                pool.wait_ge(sem["setup"], n[0])

            link(pool.memset(ident[:], 0.0))
            link(pool.affine_select(ident[:], ident[:], [[-1, P]], ALU.not_equal, 1.0, base=0, channel_multiplier=1))
            link(pool.memset(hmask[:], 1.0))
            link(pool.affine_select(hmask[:], hmask[:], [[-DH, H]], ALU.is_ge, 0.0, base=0, channel_multiplier=1))
            link(pool.affine_select(hmask[:], hmask[:], [[DH, H]], ALU.is_ge, 0.0, base=DH - 1, channel_multiplier=-1))
            link(pool.memset(pick[:], 0.0))
            link(pool.affine_select(pick[:], pick[:], [[-1, E0], [0, P]], ALU.not_equal, 1.0, base=0, channel_multiplier=1))
            for f, e in zip(falling, (E0, E1)):
                link(pool.iota(f[:], [[-1, e]], base=e, channel_multiplier=0, allow_small_or_imprecise_dtypes=True))
            link(pool.memset(vbd[:], 0.0))
            link(pool.memset(vbd[0:S, :, :, DH:DH + 1], 1.0))
            link(pool.memset(vbd[S:P, :, :, 2 * DH + 1:2 * DH + 2], 1.0))
            link(pool.memset(epsc[:, 0:1], 1e-6))
            link(pool.memset(epsc[:, 1:2], 1e-5))
            assert n[0] == N_SETUP
            pool.wait_ge(sem["setup_v"], N_SETUP_V - 1)
            pool.affine_select(bias[0:S], bias[0:S], [[0, H], [-1, S]], ALU.is_ge, NEG, base=0,
                               channel_multiplier=1).then_inc(sem["setup_v"], 1)
            pool.sem_inc(sem["out_free"], 1)

            def step(v, s, i, u):
                if s == "proj":
                    v.wait("kT", u, i)
                    done(pool.tensor_tensor(kexp[u], kT[:, tokens(u)].unsqueeze(1).broadcast_to((P, QUAD, UT)),
                                            qmask[:].unsqueeze(2).broadcast_to((P, QUAD, UT)), ALU.mult),
                         "kexp", u, i)
                if s == "b_scale":
                    v.wait("hb_rec", u, i)
                    e = hb[u][:, i, 0:512].rearrange("p (h n) -> p h n", n=NBK)
                    done(pool.tensor_tensor(e, e, hbr[:, TU * u + i, 0:H].unsqueeze(2).broadcast_to((P, H, NBK)),
                                            ALU.mult), "hb_norm", u, i)
                if s == "w_scale":
                    v.wait("w_rec", u, i)
                    e = prod[u][:, i, 512:1024].rearrange("p (h q) -> p h q", q=S)
                    done(pool.tensor_tensor(e, e, wrec[:, TU * u + i, :].unsqueeze(1).broadcast_to((P, NCH, S)),
                                            ALU.mult), "w_odd", u, i)
                if s == "out" and i == 0:
                    v.wait("res", u, 0)
                    x = xsum[:, tiles(u), :]
                    done(pool.tensor_tensor(x, xin[:, tiles(u), :], xa[:, tiles(u), :], ALU.add), "xs_part", u)
                    v.wait("xs_part", u)
                    done(pool.tensor_tensor(x, x, over_tiles(row("mlp_b2"), D), ALU.add), "xs", u)

            for s, i, u in FIRST["pool"]:
                step(Values(pool, sem, 0), s, i, u)
            if groups > 1:
                with pool.Fori(0, groups - 1) as it:
                    now = Values(pool, sem, it)
                    following = now.following()
                    for s, i, u, ahead in BODY["pool"]:
                        step(following if ahead else now, s, i, u)
            for s, i, u, _ in LAST["pool"]:
                step(Values(pool, sem, groups - 1), s, i, u)

        @block.scalar
        def _(act):
            activate = nc.scalar.activation
            act.wait_ge(sem["setup_pe"], 1)
            activate(embT[:, 0:127], bank(0)[:, 0:127], ACT.Copy).then_inc(sem["setup_act"], 1)
            act.wait_ge(sem["setup_pe"], 2)
            activate(tabT[:, 0:127], bank(1)[0:H, 0:127], ACT.Copy).then_inc(sem["setup_act"], 1)

            def step(v, s, i, u):
                tok = tokens(u)
                if s == "stats":
                    t = tiles(u)
                    v.wait_own("ln_mv", u, i + 1)
                    eps = epsc[:, 0:1] if LN_EPS[i] == 1e-6 else epsc[:, 1:2]
                    done_own(activate(lnlog[:, t], mv[:, t, 1], ACT.Ln, bias=eps), "ln_log", u)
                    v.wait_own("ln_log", u, i + 1)
                    done_own(activate(rstd[:, t, 0], lnlog[:, t], ACT.Exp, scale=-0.5), "ln_guess", u)
                if s == "xT":
                    v.wait_own("xT_ps", u, XT_OF[i])
                    gain = {L_A1: "ln1", L_A2: "ln2", L_F: "lnf"}.get(i)
                    src = own(u, 0)[:, 0:UT]
                    if gain:
                        x = activate(xT[:, tok], src, ACT.Identity, scale=col(gain + "_g"), bias=col(gain + "_b"))
                    else:
                        x = activate(xT[:, tok], src, ACT.Copy)
                    done_own(x, "xT", u)
                if s == "proj":
                    v.wait("qk_ps", u, i)
                    bq, bk = {0: (None, None), 1: ("xbq", "xbk"), 2: ("cbq", "cbk")}[i]
                    if i == 0:
                        done(activate(kT[:, tok], own(u, 0)[:, UT:], ACT.Copy), "kT", u, i)
                        done(activate(qT[:, tok], own(u, 0)[:, 0:UT], ACT.Copy, scale=1.0 / SQ8), "qT", u, i)
                    else:
                        done(activate(kT[:, tok], own(u, 0)[:, UT:], ACT.Identity, bias=col(bk)), "kT", u, i)
                        done(activate(qT[:, tok], own(u, 0)[:, 0:UT], ACT.Identity, scale=1.0 / SQ8, bias=col(bq)),
                             "qT", u, i)
                if s == "b_shift":
                    v.wait("hb_diff", u, i)
                    e = hb[u][:, i, :]
                    activate(e[:, 0:512], e[:, 0:512], ACT.Exp, scale=SQ8)
                    done(activate(e[:, 512:1024], e[:, 512:1024], ACT.Exp), "hb_exp", u, i)
                if s == "hashT":
                    v.wait("hbT_ps", u, i)
                    done(activate(hash_T[0][u][:, :, P * i:P * (i + 1)], own(u, 0).rearrange("p (i q) -> p i q", i=QUAD),
                                  ACT.Copy, scale=0.1), "qbT", u, i)
                if s in ("softmax0", "softmax1"):
                    t = int(s[-1])
                    v.wait(f"sdiff{t}", u, i)
                    p = probs[:, u, :, t, :]
                    done(activate(p, p, ACT.Exp), f"probs{t}", u, i)
                if s in ("probsT0", "probsT1"):
                    t = int(s[-1])
                    v.wait(f"pT{t}_ps", u, i)
                    done(activate(pT[:, TU * u + t, 0:4, :].rearrange("p c q -> p (c q)"), own(u, 0), ACT.Copy),
                         f"pT{t}_a", u, i)
                if s == "headsT":
                    v.wait("aT_ps", u, i)
                    src = own(u, 0)[:, 0:UT]
                    if i == 0:
                        a = activate(aT[:, tok], src, ACT.Copy)
                    else:
                        a = activate(aT[:, tok], src, ACT.Identity, bias=col({1: "xbv", 2: "cbv"}[i]))
                    done(a, "aT", u, i)
                if s == "m_hidden":
                    for c in range(FC):
                        if c % 2 == 0:
                            v.wait("m_ps", u, 0, c // 2 + 1)
                        done(activate(hT[u][:, c, :], own(u, c // 2)[:, UT * (c % 2):UT * (c % 2 + 1)], ACT.Relu,
                                      bias=col(f"mb{c}")), "m_h", u)
                if s == "choose":
                    v.wait("r_diff", u, i)
                    e = (E0, E1)[i]
                    done(activate(le[:, tiles(u), 0:e], lg[:, tiles(u), 0:e], ACT.Exp), "r_exp", u, i)
                if s == "e_hidden":
                    v.wait("e_ps", u, i)
                    done(activate(hT[u][:, i, :], own(u, i % 2)[:, UT * (i // 2):UT * (i // 2 + 1)], ACT.Relu),
                         "e_h", u, i)
                if s == "w_qk":
                    for c in range(2):
                        v.wait("wq_ps", u, i, c + 1)
                        k = 4 * i + 2 * c
                        done(activate(wqT[u][:, k:k + 2, :].rearrange("p c t -> p (c t)"), own(u, 0), ACT.Copy,
                                      scale=DK ** -0.5), "wq", u, i)
                if s == "w_v":
                    for t in range(TU):
                        v.wait("wv_a_ps", u, 0, t + 1)
                        done(activate(wvt[u][:, t, 0:512], own(u, 0), ACT.Copy), "wv_a", u)
                if s == "w_shift":
                    v.wait("w_diff", u, i)
                    done(activate(prod[u][:, i, :], prod[u][:, i, :], ACT.Exp), "w_exp", u, i)
                if s == "w_ctx":
                    v.wait("wc_ps", u, i)
                    done(activate(pT[:, TU * u + i, :, 0:S], own(u, 0).rearrange("p (c q) -> p c q", c=NCH), ACT.Copy),
                         "wc_a", u, i)
                if s == "g_hidden":
                    for n in range(4 * i, 4 * i + 4):
                        if n % 2 == 0:
                            v.wait("g_ps", u, i, n % 4 // 2 + 1)
                        b = own(u, n // 2 % 2)[:, UT * (n % 2):UT * (n % 2 + 1)]
                        done(activate(gh[u][:, n, :], b, ACT.Gelu, bias=col(f"fb{n}")), "g_h", u, i)
                    if i == 3:
                        act.preload_act_table_set(TABLES)

            act.wait_ge(sem["weights0"], W0)
            act.wait_ge(sem["setup"], N_SETUP)
            act.wait_ge(sem["setup_v"], N_SETUP_V)
            TABLES = "natural_log_exp_and_others"
            act.preload_act_table_set(TABLES)
            for s, i, u in FIRST["act"]:
                step(Values(act, sem, 0), s, i, u)
            if groups > 1:
                with act.Fori(0, groups - 1) as it:
                    now = Values(act, sem, it)
                    following = now.following()
                    for s, i, u, ahead in BODY["act"]:
                        step(following if ahead else now, s, i, u)
            for s, i, u, _ in LAST["act"]:
                step(Values(act, sem, groups - 1), s, i, u)

        @block.vector
        def _(dve):
            dve.wait_ge(sem["setup"], N_SETUP)
            dve.tensor_reduce(qmask[:], hmask[:].rearrange("p (j i) -> p i j", i=QUAD), AX.X, ALU.add)\
               .then_inc(sem["setup_v"], 1)
            dve.wait_ge(sem["weights0"], W0)
            for n in range(2):
                for i in range(QUAD):
                    m = dve.tensor_tensor(
                        whash[:, n, i * P:(i + 1) * P].rearrange("p (j n) -> p j n", n=NBK),
                        whash_raw[:, n, :].unsqueeze(1).broadcast_to((P, QUAD, NBK)),
                        hmask[:].rearrange("p (j i) -> p i j", i=QUAD)[:, i, :].unsqueeze(2).broadcast_to((P, QUAD, NBK)),
                        ALU.mult)
                m.then_inc(sem["setup_v"], 1)
            dve.memset(rstd[:], 0.0).then_inc(sem["setup_v"], 1)
            for name in ("xbq", "cbq"):
                dve.tensor_scalar(col(name), col(name), 1.0 / SQ8, None, ALU.mult).then_inc(sem["setup_v"], 1)
            dve.wait_ge(sem["setup_pe"], 3)
            dve.tensor_copy(bias[0:S], bank(2, 2)[0:S, 0:S * H].rearrange("p (s h) -> p h s", h=H))\
               .then_inc(sem["setup_v"], 1)

            n_step = [0] * NU

            def follow(v, u, instruction):
                done_own(instruction, "step", u)
                n_step[u] += 1
                v.wait_own("step", u, n_step[u])

            def statistics(v, n, u, src):
                for t in range(TU * u, TU * (u + 1)):
                    m = dve.bn_stats(stats[:, t, :], src[:, t, :])
                follow(v, u, m)
                v.apart()
                for t in range(TU * u, TU * (u + 1)):
                    m = dve.bn_aggr(mv[:, t, :], stats[:, t, :])
                done_own(m, "ln_mv", u)

            def norm(v, n, u, src, dst):
                ts, eps = tiles(u), LN_EPS[n]
                v.wait_own("ln_guess", u, n + 1)
                y, a, b, r = (rstd[:, ts, k] for k in range(4))
                follow(v, u, dve.scalar_tensor_tensor(a, mv[:, ts, 1], eps, y, ALU.add, ALU.mult))
                follow(v, u, dve.scalar_tensor_tensor(b, a, -0.5, y, ALU.mult, ALU.mult))
                follow(v, u, dve.scalar_tensor_tensor(r, b, 1.5, y, ALU.add, ALU.mult))
                for t in range(TU * u, TU * (u + 1)):
                    m = dve.tensor_scalar(dst[:, t, :], src[:, t, :], mv[:, t, 0:1], rstd[:, t, 3:4],
                                          ALU.subtract, ALU.mult)
                done_own(m, "ln_out", u)

            NORMS = {L_A1: (xin, xn), L_A2: (xa, xn), L_O1: (xb, xa), L_O2: (xb, xa), L_F: (xa, xn),
                     L_O3: (xb, xa), L_O4: (xb, xa), L_X: (xb, xn), L_O5: (xb, xa), L_O6: (xb, yout)}

            def step(v, s, i, u):
                ts = tiles(u)
                if (s, i) == STEPS[0]:
                    n_step[u] = 0
                if s == "stats":
                    if i == L_A1 and u == 0:
                        dve.wait_ge(sem["x_in"], v.value(16, 16))
                    if i == L_F:
                        v.wait_own("ln_out", u, L_O2 + 1)
                    statistics(v, i, u, NORMS[i][0])
                if s == "norm":
                    if i == L_O6 and u == 0:
                        dve.wait_ge(sem["out_free"], v.value(1, 1))
                    norm(v, i, u, *NORMS[i])
                    if i in (L_O1, L_O3):
                        v.wait_own("ln_out", u, i + 1)
                        follow(v, u, dve.tensor_tensor(xsum[:, ts, :], xa[:, ts, :],
                                                       over_tiles(row("xbo" if i == L_O1 else "cbo"), D), ALU.add))
                    if i == L_X:
                        v.wait_own("ln_out", u, i + 1)
                        dve.tensor_tensor(xn[:, ts, :], xn[:, ts, :], over_tiles(row("lnx_g"), D), ALU.mult)
                        follow(v, u, dve.tensor_tensor(xsum[:, ts, :], xa[:, ts, :], over_tiles(row("lnx_b"), D), ALU.add))
                        follow(v, u, dve.tensor_tensor(xb[:, ts, :], xn[:, ts, :], xsum[:, ts, :], ALU.add))
                    if i == L_O6:
                        v.wait_own("ln_out", u, i + 1)
                        if u == NU - 1:
                            dve.sem_inc(sem["out_ready"], 1)
                if s == "proj":
                    v.wait("v_ps", u, i)
                    for r in range(2):
                        half = slice(S * r, S * (r + 1))
                        m = dve.tensor_copy(vbd[half, BU * u:BU * (u + 1), :, (DH + 1) * r:(DH + 1) * r + DH],
                                            own(u, 1)[half, 0:UT].rearrange("p (b c d) -> p b c d", b=BU, d=DH))
                    done(m, "vbd", u, i)
                if s in ("b_shift", "b_scale"):
                    k = TU * u + i
                    e = hb[u][:, i, :].rearrange("p (h n) -> p h n", n=NBK)
                if s == "b_shift":
                    v.wait("hb_ps", u, 0, i + 1)
                    src = bank(2 * i, 2).rearrange("p (h n) -> p h n", n=NBK)
                    follow(v, u, dve.tensor_reduce(hbm[:, k, :], src, AX.X, ALU.max))
                    done(dve.tensor_tensor(e, src, hbm[:, k, :].unsqueeze(2).broadcast_to((P, 2 * H, NBK)),
                                           ALU.subtract), "hb_diff", u, i)
                if s == "b_scale":
                    v.wait("hb_exp", u, i)
                    follow(v, u, dve.tensor_reduce(hbs[:, k, :], e, AX.X, ALU.add))
                    done(dve.reciprocal(hbr[:, k, :], hbs[:, k, :]), "hb_rec", u, i)
                    v.wait("hb_rec", u, i)
                    done(dve.tensor_tensor(e[:, H:2 * H, :], e[:, H:2 * H, :],
                                           hbr[:, k, H:2 * H].unsqueeze(2).broadcast_to((P, H, NBK)), ALU.mult),
                         "hb_knorm", u, i)
                if s == "hashT":
                    v.wait("hbT_ps", u, i)
                    done(dve.tensor_copy(hash_T[1][u][:, :, P * i:P * (i + 1)],
                                         own(u, 1).rearrange("p (i q) -> p i q", i=QUAD)), "kbT", u, i)
                if s in ("softmax0", "softmax1"):
                    t = int(s[-1])
                    v.wait("scores", u, i)
                    sc = quad[:, :, 256 * t:256 * (t + 1)].rearrange("p j (i k) -> p j i k", k=S)
                    pr = probs[:, u, :, t, :].rearrange("p j (i k) -> p j i k", k=S)
                    m = smax[:, TU * u + t, :].rearrange("p (j i) -> p j i", i=QUAD)
                    if i == 2:
                        done(dve.tensor_tensor(pr, sc, bias[:].rearrange("p (j i) k -> p j i k", i=QUAD), ALU.add),
                             f"biased{t}", u, 2)
                        v.wait(f"biased{t}", u, 2)
                        sc = pr
                    follow(v, u, dve.tensor_reduce(m, sc, AX.X, ALU.max))
                    done(dve.tensor_tensor(pr, sc, m.unsqueeze(3).broadcast_to((P, QUAD, QUAD, S)), ALU.subtract),
                         f"sdiff{t}", u, i)
                if s in ("probsT0", "probsT1"):
                    t = int(s[-1])
                    v.wait(f"pT{t}_ps", u, i)
                    done(dve.tensor_copy(pT[:, TU * u + t, 4:8, :].rearrange("p c q -> p (c q)"), own(u, 1)),
                         f"pT{t}_v", u, i)
                if s == "pv":
                    for t in range(TU):
                        v.wait("pv_ps", u, i, t + 1)
                        k = TU * u + t
                        pv = own(u, t)[:, 0:288].rearrange("p (c b h e) -> p c b h e", c=8, b=2, h=2)
                        for bb in range(2):
                            q = slice(S * bb, S * (bb + 1))
                            m = dve.reciprocal(rden[q, k, :, :], pv[q, :, bb, :, DH])
                        follow(v, u, m)
                        for bb in range(2):
                            q = slice(S * bb, S * (bb + 1))
                            m = dve.tensor_tensor(attn[q, k, :].rearrange("p (c h d) -> p c h d", c=8, h=2),
                                                  pv[q, :, bb, :, 0:DH],
                                                  rden[q, k, :, :].unsqueeze(3).broadcast_to((S, 8, 2, DH)), ALU.mult)
                        done(m, "attn", u, i)
                if s == "out":
                    v.wait("o_ps", u, i)
                    o = own(u, 1)[:, 0:UT].rearrange("p (t d) -> p t d", t=TU)
                    dst, src = (xa, xin) if i == 0 else (xb, xsum)
                    done(dve.tensor_tensor(dst[:, ts, :], o, src[:, ts, :], ALU.add), "res", u, i)
                    v.wait("res", u, i)
                if s == "m_out":
                    v.wait("m2_ps", u)
                    v.wait("xs", u)
                    follow(v, u, dve.tensor_tensor(xb[:, ts, :], own(u, 0)[:, 0:UT].rearrange("p (t d) -> p t d", t=TU),
                                                   xsum[:, ts, :], ALU.add))
                    if u == NU - 1:
                        dve.sem_inc(sem["x_free"], 1)
                if s == "choose":
                    e = (E0, E1)[i]
                    v.wait("r_ps", u, i)
                    g, o1, o2, ex = (a[:, ts, 0:e] for a in (lg, oh, oh2, le))
                    m = [lgm[:, ts, k] for k in range(6)]
                    fall = over_tiles(falling[i][:], e)
                    logits = own(u, 1)[:, 0:TU * e].rearrange("p (t e) -> p t e", e=e)
                    follow(v, u, dve.tensor_tensor(o1, logits, over_tiles(row(f"r{i}"), e), ALU.add))
                    follow(v, u, dve.tensor_reduce(m[0], o1, AX.X, ALU.max))
                    done(dve.tensor_tensor(g, o1, last(m[0], e), ALU.subtract), "r_diff", u, i)
                    v.wait("r_diff", u, i)
                    follow(v, u, dve.tensor_scalar(o1, g, 0.0, None, ALU.is_equal))
                    follow(v, u, dve.tensor_tensor(o1, o1, fall, ALU.mult))
                    follow(v, u, dve.tensor_reduce(m[1], o1, AX.X, ALU.max))
                    if i == 0:
                        done(dve.tensor_tensor(o2, o1, last(m[1], e), ALU.is_equal), "gates", u, i)
                        v.wait("gates", u, i)
                        v.wait("r_exp", u, i)
                        follow(v, u, dve.tensor_reduce(m[2], ex, AX.X, ALU.add))
                        follow(v, u, dve.reciprocal(m[3], m[2]))
                        follow(v, u, dve.tensor_tensor(o1, o2, last(m[3], e), ALU.mult))
                    else:
                        follow(v, u, dve.tensor_tensor(o2, o1, last(m[1], e), ALU.is_equal))
                        follow(v, u, dve.scalar_tensor_tensor(o1, o2, NEG, g, ALU.mult, ALU.add))
                        follow(v, u, dve.tensor_reduce(m[2], o1, AX.X, ALU.max))
                        follow(v, u, dve.tensor_tensor(o1, o1, last(m[2], e), ALU.is_equal))
                        follow(v, u, dve.tensor_tensor(o1, o1, fall, ALU.mult))
                        follow(v, u, dve.tensor_reduce(m[3], o1, AX.X, ALU.max))
                        follow(v, u, dve.tensor_tensor(o1, o1, last(m[3], e), ALU.is_equal))
                        follow(v, u, dve.tensor_tensor(o2, o2, o1, ALU.add))
                        v.wait("r_exp", u, i)
                        follow(v, u, dve.tensor_tensor(o2, o2, ex, ALU.mult))
                        follow(v, u, dve.tensor_reduce(m[4], o2, AX.X, ALU.add))
                        follow(v, u, dve.reciprocal(m[5], m[4]))
                        done(dve.tensor_tensor(o1, o2, last(m[5], e), ALU.mult), "gates", u, i)
                if s == "gateT":
                    e = (E0, E1)[i]
                    v.wait("gateT_ps", u, i)
                    if i == 0:
                        dve.tensor_copy(gateTb[:, tokens(u)], own(u, 1)[0:e, 0:UT])
                    done(dve.tensor_copy(gateT[0:e, tokens(u)], own(u, 1)[0:e, 0:UT]), "gateT", u, i)
                if s == "masks":
                    v.wait_own("xT", u, XT_OF[L_F])
                    for n in range(4):
                        v.wait("mask_ps", u, 0, n + 1)
                        done(dve.tensor_tensor(xe[u][:, 2 * n:2 * n + 2, :], bank(n).rearrange("p (e t) -> p e t", e=2),
                                               xT[:, tokens(u)].unsqueeze(1).broadcast_to((P, 2, UT)), ALU.mult), "xe", u)
                if s == "e_mix":
                    v.wait("e2_ps", u, i)
                    k = TU * u + i
                    w = oh[:, k, :].unsqueeze(2).broadcast_to((P, E0, D))
                    done(dve.tensor_tensor(prod[u][:, i, :].rearrange("p (e d) -> p e d", e=E0),
                                           bank(2 * i, 2).rearrange("p (e d) -> p e d", e=E0), w, ALU.mult), "e_prod", u, i)
                    v.wait("e_prod", u, i)
                    dve.tensor_reduce(xsum[:, k, :], prod[u][:, i, :].rearrange("p (e d) -> p d e", e=E0), AX.X, ALU.add)
                    follow(v, u, dve.scalar_tensor_tensor(attn[:, k, :], own(u, i)[:, 0:D], lgm[:, k, 3:4],
                                                          xa[:, k, :], ALU.mult, ALU.add))
                    follow(v, u, dve.tensor_tensor(xb[:, k, :], xsum[:, k, :], attn[:, k, :], ALU.add))
                if s == "w_qk":
                    for c in range(2):
                        v.wait("wk_ps", u, i, c + 1)
                        k = 4 * i + 2 * c
                        done(dve.tensor_copy(wkT[u][:, k:k + 2, :].rearrange("p c t -> p (c t)"), own(u, 1)), "wk", u, i)
                if s == "w_v":
                    for t in range(TU):
                        v.wait("wv_v_ps", u, 0, t + 1)
                        done(dve.tensor_copy(wvt[u][:, t, 512:1024], own(u, 1)), "wv_v", u)
                if s in ("w_shift", "w_scale"):
                    k = TU * u + i
                    e = prod[u][:, i, :].rearrange("p (h q) -> p h q", q=S)
                if s == "w_shift":
                    v.wait("ws_ps", u, 0, i + 1)
                    src = bank(2 * i, 2).rearrange("p (h q) -> p h q", q=S)
                    follow(v, u, dve.tensor_reduce(wmax[:, k, :], src.rearrange("p h q -> p q h"), AX.X, ALU.max))
                    done(dve.tensor_tensor(e, src, wmax[:, k, :].unsqueeze(1).broadcast_to((P, H, S)), ALU.subtract),
                         "w_diff", u, i)
                if s == "w_scale":
                    v.wait("w_exp", u, i)
                    follow(v, u, dve.tensor_reduce(wmax[:, k, :], e.rearrange("p h q -> p q h"), AX.X, ALU.add))
                    done(dve.reciprocal(wrec[:, k, :], wmax[:, k, :]), "w_rec", u, i)
                    v.wait("w_rec", u, i)
                    done(dve.tensor_tensor(e[:, 0:NCH, :], e[:, 0:NCH, :],
                                           wrec[:, k, :].unsqueeze(1).broadcast_to((P, NCH, S)), ALU.mult), "w_even", u, i)
                if s == "w_ctx":
                    v.wait("wc_ps", u, i)
                    done(dve.tensor_copy(pT[:, TU * u + i, :, S:P], own(u, 1).rearrange("p (c q) -> p c q", c=NCH)),
                         "wc_v", u, i)
                if s == "w_out":
                    v.wait("wo_ps", u)
                    follow(v, u, dve.tensor_tensor(xb[:, ts, :], own(u, 0)[:, 0:UT].rearrange("p (t d) -> p t d", t=TU),
                                                   xa[:, ts, :], ALU.add))
                if s == "g_mix":
                    v.wait("g2_ps", u)
                    dve.tensor_tensor(attn[:, ts, :], bank(2)[:, 0:UT].rearrange("p (t d) -> p t d", t=TU),
                                      xa[:, ts, :], ALU.add)
                    for t in range(TU):
                        k = TU * u + t
                        w = oh[:, k, 0:E1].unsqueeze(2).broadcast_to((P, E1, D))
                        done(dve.tensor_tensor(prod[u][:, t, 0:512].rearrange("p (e d) -> p e d", e=E1),
                                               bank(t).rearrange("p (e d) -> p e d", e=E1), w, ALU.mult), "g_prod", u)
                    v.wait("g_prod", u)
                    for t in range(TU):
                        k = TU * u + t
                        m = dve.tensor_reduce(xsum[:, k, :], prod[u][:, t, 0:512].rearrange("p (e d) -> p d e", e=E1),
                                              AX.X, ALU.add)
                    follow(v, u, m)
                    follow(v, u, dve.tensor_tensor(xb[:, ts, :], xsum[:, ts, :], attn[:, ts, :], ALU.add))

            dve.wait_ge(sem["bias_dup"], 16)
            for s, i, u in FIRST["dve"]:
                step(Values(dve, sem, 0), s, i, u)
            if groups > 1:
                with dve.Fori(0, groups - 1) as it:
                    now = Values(dve, sem, it)
                    following = now.following()
                    for s, i, u, ahead in BODY["dve"]:
                        step(following if ahead else now, s, i, u)
            for s, i, u, _ in LAST["dve"]:
                step(Values(dve, sem, groups - 1), s, i, u)

        @block.tensor
        def _(pe):
            mm, flip = nc.tensor.matmul, nc.tensor.transpose
            pe.wait_ge(sem["weights0"], W0)
            pe.wait_ge(sem["setup"], N_SETUP)
            flip(bank(0)[:, 0:127], emb[0:127, :], ident[0:127, 0:127]).then_inc(sem["setup_pe"], 1)
            pe.wait_ge(sem["setup_act"], 1)
            mm(bank(1)[0:H, 0:127], hmask[:], embT[:, 0:127], start=True, stop=True).then_inc(sem["setup_pe"], 1)
            pe.wait_ge(sem["setup_act"], 2)
            for s in range(S):
                m = flip(bank(2, 2)[0:S, H * s:H * (s + 1)], tabT[:, S - 1 - s:2 * S - 1 - s], ident[0:H, 0:H])
            m.then_inc(sem["setup_pe"], 1)

            reader = []

            def take_quad(v, name, u, c=0):
                if reader:
                    by, of = reader.pop()
                    by.wait(*of)
                reader.append((v, (name, u, c)))

            def step(v, s, i, u):
                tok = tokens(u)
                if s == "xT":
                    src = xn if i in (L_A1, L_A2, L_F) else xa
                    v.wait_own("ln_out", u, i + 1)
                    for t in range(TU):
                        m = flip(own(u, 0)[:, P * t:P * (t + 1)], src[:, TU * u + t, :], ident[:])
                    done_own(m, "xT_ps", u)
                if s == "proj":
                    v.wait_own("xT", u, {0: 1, 1: 3, 2: 6}[i])
                    if i == 1 and u == 0:
                        pe.wait_ge(sem["weights"], W1)
                        pe.wait_ge(sem["ctx_in"], v.value(16, 16))
                    kv = (ctxT if i == 1 else xT)[:, tok]
                    mm(own(u, 0)[:, UT:], wk[i][:], kv, start=True, stop=True)
                    done(mm(own(u, 0)[:, 0:UT], wq[i][:], xT[:, tok], start=True, stop=True), "qk_ps", u, i)
                    for b in range(BU):
                        for r in range(2):
                            m = mm(own(u, 1)[S * r:S * (r + 1), S * b:S * (b + 1)], kv[:, S * b:S * (b + 1)],
                                   wv[i][:].rearrange("p (c r d) -> p r c d", r=2, d=DH)[:, r, :, :], start=True, stop=True)
                    done(m, "v_ps", u, i)
                if s == "hash":
                    v.wait("qT", u, 0)
                    take_quad(v, "hb_diff", u, 1)
                    for t in range(TU):
                        k = tile_tokens(u, t)
                        mm(bank(2 * t), qT[:, k], whash[:, 0, :], start=True, stop=True)
                        done(mm(bank(2 * t + 1), kT[:, k], whash[:, 1, :], start=True, stop=True), "hb_ps", u)
                if s == "hashT":
                    v.wait("hb_norm", u, i)
                    v.wait("hb_knorm", u, i)
                    if i == 0:
                        v.wait("vbd", u, 0)
                    else:
                        v.wait("qbT", u, 0)
                        v.wait("kbT", u, 0)
                    for k in range(8):
                        m = flip(own(u, k // 4)[:, P * (k % 4):P * (k % 4 + 1)], hb[u][:, i, P * k:P * (k + 1)], ident[:])
                    done(m, "hbT_ps", u, i)
                if s == "scores":
                    v.wait("qT", u, i)
                    v.wait("kexp", u, i)
                    v.wait("vbd", u, i)
                    if i == 0:
                        v.wait("qbT", u, 1)
                        v.wait("kbT", u, 1)
                    if i < 2:
                        take_quad(v, "sdiff1", u, i)
                    else:
                        take_quad(v, "biased1", u, 2)
                    for t in range(TU):
                        for bb in range(2):
                            b, q = TU * t + bb, slice(S * bb, S * (bb + 1))
                            k = slice(S * b, S * (b + 1))
                            for j in range(4):
                                r = slice(32 * j, 32 * (j + 1))
                                m = mm(quad[q, j, 256 * t:256 * (t + 1)], qT[r, UT * u + S * b:UT * u + S * (b + 1)],
                                       kexp[u][r, :, k], start=True, stop=(i > 0))
                            if i == 0:
                                for n in range(QUAD):
                                    for j in range(4):
                                        r = slice(32 * j, 32 * (j + 1))
                                        at = 256 * t + S * n
                                        m = mm(quad[q, j, at:at + S], hash_T[0][u][r, n, k], hash_T[1][u][r, n, k],
                                               start=False, stop=(n == 3))
                    done(m, "scores", u, i)
                if s in ("probsT0", "probsT1"):
                    t = int(s[-1])
                    v.wait(f"probs{t}", u, i)
                    if t:
                        v.wait("pT0_a", u, i)
                        v.wait("pT0_v", u, i)
                    for k in range(8):
                        j, i0 = k // 2, 2 * (k % 2)
                        m = flip(own(u, k // 4)[:, P * (k % 4):P * (k % 4 + 1)],
                                 probs[:, u, j, t, S * i0:S * (i0 + 2)], ident[:])
                    done(m, f"pT{t}_ps", u, i)
                if s == "pv":
                    v.wait("pT1_a", u, i)
                    for t in range(TU):
                        if t:
                            v.wait("pT1_v", u, i)
                        else:
                            v.wait("pT0_v", u, i)
                        b = BU * u + 2 * t
                        for k in range(8):
                            m = mm(own(u, t)[:, 36 * k:36 * (k + 1)], pT[:, TU * u + t, k, :], vbd[:, b:b + 2, k, :],
                                   start=True, stop=True)
                        done(m, "pv_ps", u, i)
                if s == "headsT":
                    v.wait("attn", u, i)
                    for t in range(TU):
                        m = flip(own(u, 0)[:, P * t:P * (t + 1)], attn[:, TU * u + t, :], ident[:])
                    done(m, "aT_ps", u, i)
                if s == "out":
                    v.wait("aT", u, i)
                    for t in range(TU):
                        m = mm(own(u, 1)[:, P * t:P * (t + 1)], aT[:, tile_tokens(u, t)], wo[i][:], start=True, stop=True)
                    done(m, "o_ps", u, i)
                if s == "m_hidden":
                    v.wait_own("xT", u, 2)
                    for c in range(FC):
                        m = mm(own(u, c // 2)[:, UT * (c % 2):UT * (c % 2 + 1)], m_w1[:, P * c:P * (c + 1)], xT[:, tok],
                               start=True, stop=True)
                        if c % 2:
                            done(m, "m_ps", u)
                if s == "m_out":
                    v.wait("m_h", u)
                    for t in range(TU):
                        for c in range(FC):
                            m = mm(own(u, 0)[:, P * t:P * (t + 1)], hT[u][:, c, P * t:P * (t + 1)], m_w2[:, c, :],
                                   start=(c == 0), stop=(c == FC - 1))
                    done(m, "m2_ps", u)
                if s == "route":
                    v.wait_own("xT", u, {0: 4, 1: 8}[i])
                    e, w = ((E0, e_r), (E1, g_r))[i]
                    for t in range(TU):
                        m = mm(own(u, 1)[:, e * t:e * (t + 1)], xT[:, tile_tokens(u, t)], w[:], start=True, stop=True)
                    done(m, "r_ps", u, i)
                if s == "gateT":
                    e, src = ((E0, oh2), (E1, oh))[i]
                    v.wait("gates", u, i)
                    if i:
                        v.wait("g_h", u, 3)
                    for t in range(TU):
                        m = flip(own(u, 1)[0:e, P * t:P * (t + 1)], src[:, TU * u + t, 0:e], ident[:])
                    done(m, "gateT_ps", u, i)
                if s == "masks":
                    v.wait("gateT", u, 0)
                    take_quad(v, "xe", u)
                    for n in range(4):
                        for e in (2 * n, 2 * n + 1):
                            m = mm(bank(n)[:, UT * (e % 2):UT * (e % 2 + 1)], pick[:, e, :], gateTb[:, tok],
                                   start=True, stop=True)
                        done(m, "mask_ps", u)
                if s == "e_hidden":
                    f = slice(P * i, P * (i + 1))
                    dst = own(u, i % 2)[:, UT * (i // 2):UT * (i // 2 + 1)]
                    v.wait("xe", u)
                    if i >= 2:
                        v.wait("e_h", u, i - 2)
                    mm(dst, e_b1[:, f], gateT[:, tok], start=True, stop=False)
                    for e in range(E0):
                        m = mm(dst, e_w1[:, e, f], xe[u][:, e, :], start=False, stop=(e == E0 - 1))
                    done(m, "e_ps", u, i)
                if s == "e_out":
                    v.wait("e_h", u, 3)
                    take_quad(v, "e_prod", u, i)
                    for c in range(FC):
                        for n in range(2):
                            mm(bank(2 * i + n), hT[u][:, c, P * i:P * (i + 1)],
                               e_w2[:, c, 4 * n:4 * n + 4, :].rearrange("p e d -> p (e d)"),
                               start=(c == 0), stop=(c == FC - 1))
                    done(mm(own(u, i)[:, 0:D], gateT[:, tile_tokens(u, i)], e_b2[:], start=True, stop=True), "e2_ps", u, i)
                if s == "w_qk":
                    if i == 0:
                        v.wait_own("xT", u, XT_OF[L_O4])
                    for c in range(2):
                        k = 4 * i + 2 * c
                        if k:
                            v.wait("wq", u, *((i, c) if c else (i - 1, 2)))
                        for n in range(2):
                            m = mm(own(u, 0)[:, UT * n:UT * (n + 1)], ww[0][:, P * (k + n):P * (k + n + 1)], xT[:, tok],
                                   start=True, stop=True)
                        done(m, "wq_ps", u, i)
                        if k:
                            v.wait("wk", u, *((i, c) if c else (i - 1, 2)))
                        for n in range(2):
                            m = mm(own(u, 1)[:, UT * n:UT * (n + 1)], ww[1][:, P * (k + n):P * (k + n + 1)], ctxT[:, tok],
                                   start=True, stop=True)
                        done(m, "wk_ps", u, i)
                if s == "w_v":
                    for t in range(TU):
                        for n, (copied, copy) in enumerate((("wq", "wv_a"), ("wk", "wv_v"))):
                            if t == 0:
                                v.wait(copied, u, 1)
                            else:
                                v.wait(copy, u, 0, t)
                            done(mm(own(u, n), ctxT[:, tile_tokens(u, t)], ww[2][:, 512 * n:512 * (n + 1)],
                                    start=True, stop=True), f"{copy}_ps", u)
                if s == "w_scores":
                    v.wait("wq", u, 1)
                    v.wait("wk", u, 1)
                    take_quad(v, "w_diff", u, 1)
                    v.apart()
                    for t in range(TU):
                        for bb in range(2):
                            k = slice(P * t + S * bb, P * t + S * (bb + 1))
                            for c in range(NCH):
                                for r in range(2):
                                    d = slice(S * r, S * (r + 1))
                                    m = mm(bank(2 * t + r)[S * bb:S * (bb + 1), S * c:S * (c + 1)],
                                           wkT[u][d, c, k], wqT[u][d, c, k], start=True, stop=True)
                        done(m, "ws_ps", u)
                if s == "w_ctx":
                    v.wait("w_even", u, i)
                    v.wait("w_odd", u, i)
                    if i == 0:
                        v.wait("wv_a", u)
                        v.wait("wv_v", u)
                        if u == NU - 1:
                            pe.sem_inc(sem["ctx_free"], 1)
                        else:
                            v.apart()
                    else:
                        v.wait("wc_a", u, 0)
                        v.wait("wc_v", u, 0)
                        v.apart()
                    for c in range(NCH):
                        for r in range(2):
                            for bb in range(2):
                                k = slice(S * bb, S * (bb + 1))
                                e = prod[u][k, i, 512 * r + S * c:512 * r + S * (c + 1)]
                                m = mm(own(u, bb)[S * r:S * (r + 1), S * c:S * (c + 1)],
                                       wvt[u][k, i, P * c + S * r:P * c + S * (r + 1)], e, start=True, stop=True)
                    done(m, "wc_ps", u, i)
                if s == "w_out":
                    v.wait("wc_a", u, 1)
                    v.wait("wc_v", u, 1)
                    for t in range(TU):
                        for c in range(NCH):
                            m = mm(own(u, 0)[:, P * t:P * (t + 1)], pT[:, TU * u + t, c, :], wwo[:, c, :],
                                   start=(c == 0), stop=(c == NCH - 1))
                    done(m, "wo_ps", u)
                if s == "g_hidden":
                    for p in range(2):
                        if i == 0 and p:
                            v.wait("r_diff", u, 1)
                        if i:
                            v.wait("g_h", u, i - 1, 2 * p + 2)
                        for n in range(4 * i + 2 * p, 4 * i + 2 * p + 2):
                            e, c = n // FC, n % FC
                            m = mm(own(u, p)[:, UT * (n % 2):UT * (n % 2 + 1)], g_w1[:, e, P * c:P * (c + 1)], xT[:, tok],
                                   start=True, stop=True)
                        done(m, "g_ps", u, i)
                if s == "g_out":
                    v.wait("gateT", u, 1)
                    take_quad(v, "g_prod", u)
                    for t in range(TU):
                        for c in range(FC):
                            for e in range(E1):
                                mm(bank(t)[:, D * e:D * (e + 1)], gh[u][:, e * FC + c, P * t:P * (t + 1)], g_w2[:, c, e, :],
                                   start=(c == 0 and e == 0), stop=(c == FC - 1), skip_group_check=True)
                    for t in range(TU):
                        m = mm(bank(2)[:, P * t:P * (t + 1)], gateT[0:E1, tile_tokens(u, t)], g_b2[:], start=True, stop=True)
                    done(m, "g2_ps", u)

            pe.wait_ge(sem["setup_v"], N_SETUP_V)
            for s, i, u in FIRST["pe"]:
                step(Values(pe, sem, 0), s, i, u)
            if groups > 1:
                with pe.Fori(0, groups - 1) as it:
                    now = Values(pe, sem, it)
                    following = now.following()
                    if reader:
                        reader[0] = (now, reader[0][1])
                    for s, i, u, ahead in BODY["pe"]:
                        step(following if ahead else now, s, i, u)
                    held, of = reader.pop()
                    if held is following:
                        reader.append((Values(pe, sem, groups - 1), of))
                    else:
                        held.wait(*of)
            for s, i, u, _ in LAST["pe"]:
                step(Values(pe, sem, groups - 1), s, i, u)

        rounds = 1 if groups == 1 else 2
        for n in SIGNALS:
            giving, count = giving_steps(n)
            assert sorted(given[n]) == sorted(giving * count * rounds), f"signal {n}: given {given[n]}"
        for n, count in UNIT_SIGNALS.items():
            for u in range(NU):
                assert len(given[n, u]) == count * rounds, f"signal {n}: given {len(given[n, u])} times"


def host_layout(x):
    import numpy as np

    a = {k: np.ascontiguousarray(v) for k, v in x.items()}
    r = {}
    r["x"] = a["x"].reshape(B * S, D)
    r["ctxT"] = a["ctx_1024"].reshape(B * S, D).T
    r["wq0"], r["wk0"], r["wv0"] = (a[f"L0_attn_W{n}"].reshape(D, D) for n in "qkv")
    r["wo0"] = a["L0_attn_Wo"].reshape(D, D)
    r["whq"], r["whk"] = (a[f"L0_attn_Wh{n}"].reshape(D, NBK) for n in "qk")
    r["m_w1"], r["m_w2"] = a["L0_attn_W1"], a["L0_attn_W2"]
    for n in "qkvo":
        r[f"w{n}1"] = a[f"L0_xattn_W{n}"].T
    r["e_r"], r["e_w1"], r["e_w2"] = a["L0_ffn_Wr"], a["L0_ffn_W1"], a["L0_ffn_W2"]
    r["e_b1"], r["e_b2"] = a["L0_ffn_b1"], a["L0_ffn_b2"]
    for i, n in enumerate("qkv"):
        r[f"w{n}2"] = a["L1_attn_qkv_w"][i * D:(i + 1) * D].T
    r["wo2"] = a["L1_attn_proj_w"].T
    r["emb"] = a["L1_attn_rel_pos_emb"][S:S + 127]
    for n in "qkvo":
        r[f"ww{n}"] = a[f"L1_xattn_W_{n.upper()}"]
    r["g_r"], r["g_w1"], r["g_w2"], r["g_b2"] = (a[f"L1_ffn_{n}"] for n in ("Wr", "W1", "W2", "b2"))
    qkv_b = a["L1_attn_qkv_b"].reshape(3, D)
    r["cols"] = np.stack([a["L0_attn_ln1_g"], a["L0_attn_ln1_b"], a["L0_attn_ln2_g"], a["L0_attn_ln2_b"],
                          *a["L0_attn_b1"].reshape(FC, P), a["L0_xattn_bq"], a["L0_xattn_bk"], a["L0_xattn_bv"],
                          a["L0_ffn_ln_g"], a["L0_ffn_ln_b"], *qkv_b, *a["L1_ffn_b1"].reshape(E1 * FC, P)], axis=1)
    r["rows"] = np.concatenate([a["L0_attn_b2"], a["L0_xattn_bo"], a["L1_attn_proj_b"], a["L1_xattn_ln_gamma"],
                                a["L1_xattn_ln_beta"], a["L0_ffn_br"], a["L1_ffn_br"]])[None, :]
    return {k: np.ascontiguousarray(v) for k, v in r.items()}


def kernel(**inputs):
    import concourse.bacc as _bacc
    from concourse import mybir as _mybir
    from concourse.bass_utils import run_bass_kernel_spmd as _run

    nc = _bacc.Bacc("TRN2", target_bir_lowering=False, num_devices=1)
    arrays, args = {}, {}
    for name, a in host_layout(inputs).items():
        arrays[f"in_{name}"] = a
        args[name] = nc.dram_tensor(f"in_{name}", a.shape, _mybir.dt.from_np(a.dtype), kind="ExternalInput").ap()
    out = nc.dram_tensor("out_0_dram", (B, S, D), _mybir.dt.float32, kind="ExternalOutput").ap()
    decoder_kernel(nc, args, out)
    r = _run(nc, [arrays], core_ids=[0])
    return r.results[0]["out_0_dram"]
```
